# Optimizing a Trainium2 kernel written in Bass

```python
import numpy as np
import jax
import jax.numpy as jnp

def _softmax(x, axis=-1):
    return jax.nn.softmax(x, axis=axis)

def _gelu(x):
    return jax.nn.gelu(x, approximate=True)

def _silu(x):
    return jax.nn.silu(x)

def _sigmoid(x):
    return jax.nn.sigmoid(x)

def _layernorm(x, axis=-1, eps=1e-05):
    m = jnp.mean(x, axis=axis, keepdims=True)
    v = jnp.var(x, axis=axis, keepdims=True)
    return (x - m) / jnp.sqrt(v + eps)

def _scatter_add(tgt, idx, src, axis=0):
    return tgt.at[idx].add(src)

def _segment_sum(src, seg, n):
    return jax.ops.segment_sum(src, seg, n)
kernel_name = 'mk_vit_tower_cls_d1_tok_img768_r4_1afd8d'

def setup_inputs(seed: int=0):
    np.random.seed(seed)
    _w = jnp.asarray

    def _rec_inputs():
        import jax
        import jax.numpy as jnp
        _rk = jax.random.key(seed)
        x = -0.00040386 + 0.999972 * jax.random.normal(jax.random.fold_in(_rk, 1), (32, 3, 128, 128), jnp.float32)
        cls_tok = 0.02 * jax.random.normal(jax.random.fold_in(_rk, 5), (1, 1, 192), jnp.float32)
        return (x, cls_tok)
    x, cls_tok = _rec_inputs()

    def _L0_tok_setup():
        import jax, jax.numpy as jnp
        import numpy as np
        P = 16
        WIN = 64
        NH = 12

        def _layernorm(x, g, b, eps=1e-05):
            m = x.mean(-1, keepdims=True)
            v = ((x - m) ** 2).mean(-1, keepdims=True)
            return (x - m) * jax.lax.rsqrt(v + eps) * g + b

        def _sinusoidal_pe(n, d):
            pos = jnp.arange(n, dtype=jnp.float32)[:, None]
            i = jnp.arange(d // 2, dtype=jnp.float32)[None, :]
            ang = pos / jnp.power(10000.0, 2.0 * i / d)
            pe = jnp.zeros((n, d), jnp.float32)
            pe = pe.at[:, 0::2].set(jnp.sin(ang)).at[:, 1::2].set(jnp.cos(ang))
            return pe
        key = jax.random.key(seed)
        ks = jax.random.split(key, 8)
        B, C, H, W, D, F = (16, 3, 128, 128, 192, 768)
        s = lambda k, shape: jax.random.normal(k, shape, jnp.float32) * 0.02
        return {'input': jax.random.normal(ks[0], (B, C, H, W), jnp.float32), 'patch_w': s(ks[1], (D, C, P, P)), 'patch_b': jnp.zeros((D,), jnp.float32), 'ln_g': jnp.ones((D,), jnp.float32), 'ln_b': jnp.zeros((D,), jnp.float32), 'qkv_w': s(ks[2], (D, 3 * D)), 'qkv_b': jnp.zeros((3 * D,), jnp.float32), 'proj_w': s(ks[3], (D, D)), 'proj_b': jnp.zeros((D,), jnp.float32), 'ff1_w': s(ks[4], (D, F)), 'ff1_b': jnp.zeros((F,), jnp.float32), 'ff2_w': s(ks[5], (F, D)), 'ff2_b': jnp.zeros((D,), jnp.float32)}
    _L0_tok_all = _L0_tok_setup()
    _L0_tok_in = {k: v for k, v in _L0_tok_all.items() if k in ('patch_w', 'patch_b', 'ln_g', 'ln_b', 'qkv_w', 'qkv_b', 'proj_w', 'proj_b', 'ff1_w', 'ff1_b', 'ff2_w', 'ff2_b')}
    del _L0_tok_all

    def _L0_attn_setup():
        import jax, jax.numpy as jnp
        import numpy as np
        B, S, E, H = (8, 256, 192, 12)
        SPARSITY = 0.4
        key = jax.random.key(seed)
        ks = jax.random.split(key, 5)
        return {'hidden_states': jax.random.normal(ks[0], (B, S, E), dtype=jnp.float32), 'W_qkv': jax.random.normal(ks[1], (E, 3 * E), dtype=jnp.float32) * E ** (-0.5), 'b_qkv': jax.random.normal(ks[2], (3 * E,), dtype=jnp.float32) * 0.02, 'W_proj': jax.random.normal(ks[3], (E, E), dtype=jnp.float32) * E ** (-0.5), 'b_proj': jax.random.normal(ks[4], (E,), dtype=jnp.float32) * 0.02}
    _L0_attn_all = _L0_attn_setup()
    _L0_attn_in = {k: v for k, v in _L0_attn_all.items() if k in ('W_qkv', 'b_qkv', 'W_proj', 'b_proj')}
    del _L0_attn_all

    def _L0_ffn_setup():
        import jax, jax.numpy as jnp
        import numpy as np
        E = 128
        I = 464
        IS = 928
        K = 6
        G = 1
        TG = 1
        SCALE = 2.5
        CAP = 192

        def moe_forward(hidden_states, Wg, e_bias, W_gate_up, W_down, Wsg, Wsu, Wsd):
            B, S, H = hidden_states.shape
            x = hidden_states.reshape(-1, H)
            T = x.shape[0]
            logits = x.astype(jnp.float32) @ Wg.T
            sig = jax.nn.sigmoid(logits)
            choice = sig + e_bias[None, :]
            grp = choice.reshape(T, G, E // G)
            group_scores = jax.lax.top_k(grp, 2)[0].sum(-1)
            gidx = jax.lax.top_k(group_scores, TG)[1]
            gmask = jnp.zeros((T, G), jnp.float32).at[jnp.arange(T)[:, None], gidx].set(1.0)
            smask = jnp.repeat(gmask, E // G, axis=1)
            scores_for_choice = jnp.where(smask > 0, choice, 0.0)
            topk_idx = jax.lax.top_k(scores_for_choice, K)[1]
            topk_w = jnp.take_along_axis(sig, topk_idx, axis=1)
            topk_w = topk_w / (topk_w.sum(-1, keepdims=True) + 1e-20)
            topk_w = topk_w * SCALE
            P = T * K
            flat_e = topk_idx.reshape(-1)
            order = jnp.argsort(flat_e)
            se = flat_e[order]
            counts = jax.ops.segment_sum(jnp.ones(P, jnp.int32), flat_e, num_segments=E)
            starts = jnp.cumsum(counts) - counts
            pos = jnp.arange(P) - starts[se]
            buf_idx = jnp.where(pos < CAP, se * CAP + pos, E * CAP)
            tok_of_pair = (order // K).astype(jnp.int32)
            w_of_pair = topk_w.reshape(-1)[order]
            token_buf = jnp.zeros((E * CAP,), jnp.int32).at[buf_idx].set(tok_of_pair, mode='drop')
            w_buf = jnp.zeros((E * CAP,), x.dtype).at[buf_idx].set(w_of_pair.astype(x.dtype), mode='drop')
            xb = x[token_buf].reshape(E, CAP, H)
            gu = jnp.einsum('ech,ehf->ecf', xb, W_gate_up)
            g, u = jnp.split(gu, 2, axis=-1)
            inter = jax.nn.silu(g) * u
            yb = jnp.einsum('eci,eih->ech', inter, W_down)
            yb = yb * w_buf.reshape(E, CAP, 1)
            routed = jnp.zeros((T, H), x.dtype).at[token_buf].add(yb.reshape(E * CAP, H))
            shared = jax.nn.silu(x @ Wsg) * (x @ Wsu) @ Wsd
            return (routed + shared).reshape(B, S, H)
        key = jax.random.key(seed)
        ks = jax.random.split(key, 8)
        B, S, H = (1, 512, 192)
        sc = 0.02
        return {'hidden_states': jax.random.normal(ks[0], (B, S, H), jnp.float32), 'Wg': jax.random.normal(ks[1], (E, H), jnp.float32) * sc, 'e_bias': jnp.zeros((E,), jnp.float32), 'W_gate_up': jax.random.normal(ks[2], (E, H, 2 * I), jnp.float32) * sc, 'W_down': jax.random.normal(ks[3], (E, I, H), jnp.float32) * sc, 'Wsg': jax.random.normal(ks[4], (H, IS), jnp.float32) * sc, 'Wsu': jax.random.normal(ks[5], (H, IS), jnp.float32) * sc, 'Wsd': jax.random.normal(ks[6], (IS, H), jnp.float32) * sc}
    _L0_ffn_all = _L0_ffn_setup()
    _L0_ffn_in = {k: v for k, v in _L0_ffn_all.items() if k in ('Wg', 'e_bias', 'W_gate_up', 'W_down', 'Wsg', 'Wsu', 'Wsd')}
    del _L0_ffn_all
    return {'x': x, 'cls_tok': cls_tok, 'L0_tok_patch_w': _L0_tok_in['patch_w'], 'L0_tok_patch_b': _L0_tok_in['patch_b'], 'L0_tok_ln_g': _L0_tok_in['ln_g'], 'L0_tok_ln_b': _L0_tok_in['ln_b'], 'L0_tok_qkv_w': _L0_tok_in['qkv_w'], 'L0_tok_qkv_b': _L0_tok_in['qkv_b'], 'L0_tok_proj_w': _L0_tok_in['proj_w'], 'L0_tok_proj_b': _L0_tok_in['proj_b'], 'L0_tok_ff1_w': _L0_tok_in['ff1_w'], 'L0_tok_ff1_b': _L0_tok_in['ff1_b'], 'L0_tok_ff2_w': _L0_tok_in['ff2_w'], 'L0_tok_ff2_b': _L0_tok_in['ff2_b'], 'L0_attn_W_qkv': _L0_attn_in['W_qkv'], 'L0_attn_b_qkv': _L0_attn_in['b_qkv'], 'L0_attn_W_proj': _L0_attn_in['W_proj'], 'L0_attn_b_proj': _L0_attn_in['b_proj'], 'L0_ffn_Wg': _L0_ffn_in['Wg'], 'L0_ffn_e_bias': _L0_ffn_in['e_bias'], 'L0_ffn_W_gate_up': _L0_ffn_in['W_gate_up'], 'L0_ffn_W_down': _L0_ffn_in['W_down'], 'L0_ffn_Wsg': _L0_ffn_in['Wsg'], 'L0_ffn_Wsu': _L0_ffn_in['Wsu'], 'L0_ffn_Wsd': _L0_ffn_in['Wsd']}

def reference(x, cls_tok, L0_tok_patch_w, L0_tok_patch_b, L0_tok_ln_g, L0_tok_ln_b, L0_tok_qkv_w, L0_tok_qkv_b, L0_tok_proj_w, L0_tok_proj_b, L0_tok_ff1_w, L0_tok_ff1_b, L0_tok_ff2_w, L0_tok_ff2_b, L0_attn_W_qkv, L0_attn_b_qkv, L0_attn_W_proj, L0_attn_b_proj, L0_ffn_Wg, L0_ffn_e_bias, L0_ffn_W_gate_up, L0_ffn_W_down, L0_ffn_Wsg, L0_ffn_Wsu, L0_ffn_Wsd):
    import jax
    import jax.numpy as jnp

    def _L0_tok_ref(input, patch_w, patch_b, ln_g, ln_b, qkv_w, qkv_b, proj_w, proj_b, ff1_w, ff1_b, ff2_w, ff2_b):
        import jax, jax.numpy as jnp
        import numpy as np
        P = 16
        WIN = 64
        NH = 12

        def _layernorm(x, g, b, eps=1e-05):
            m = x.mean(-1, keepdims=True)
            v = ((x - m) ** 2).mean(-1, keepdims=True)
            return (x - m) * jax.lax.rsqrt(v + eps) * g + b

        def _sinusoidal_pe(n, d):
            pos = jnp.arange(n, dtype=jnp.float32)[:, None]
            i = jnp.arange(d // 2, dtype=jnp.float32)[None, :]
            ang = pos / jnp.power(10000.0, 2.0 * i / d)
            pe = jnp.zeros((n, d), jnp.float32)
            pe = pe.at[:, 0::2].set(jnp.sin(ang)).at[:, 1::2].set(jnp.cos(ang))
            return pe
        B, C, H, W = input.shape
        D = patch_w.shape[0]
        dh = D // NH
        xp = input.reshape(B, C, H // P, P, W // P, P)
        x = jnp.einsum('bchpwq,dcpq->bhwd', xp, patch_w) + patch_b
        x = x.reshape(B, -1, D)
        x = _layernorm(x, ln_g, ln_b)
        N = x.shape[1]
        x = x + _sinusoidal_pe(N, D)

        def ff(y):
            return jax.nn.gelu(y @ ff1_w + ff1_b) @ ff2_w + ff2_b

        def sparse_attn(y):
            nW = N // WIN
            qkv = (y @ qkv_w + qkv_b).reshape(B, nW, WIN, 3, NH, dh)
            q, k, v = (qkv[:, :, :, 0], qkv[:, :, :, 1], qkv[:, :, :, 2])
            scores = jnp.einsum('bwqhd,bwkhd->bwhqk', q, k) * dh ** (-0.5)
            a = jax.nn.softmax(scores, axis=-1)
            o = jnp.einsum('bwhqk,bwkhd->bwqhd', a, v).reshape(B, N, D)
            return o @ proj_w + proj_b
        identity = x
        x = ff(x)
        x = sparse_attn(x)
        x = x + identity
        identity = x
        x = ff(x)
        x = x + identity
        return x

    def _L0_attn_ref(hidden_states, W_qkv, b_qkv, W_proj, b_proj):
        import jax, jax.numpy as jnp
        import numpy as np
        B, S, E, H = (8, 256, 192, 12)
        SPARSITY = 0.4
        bsz, tgt_len, embed_dim = hidden_states.shape
        head_dim = embed_dim // H
        scale = head_dim ** (-0.5)
        qkv = (hidden_states @ W_qkv + b_qkv).reshape(bsz, tgt_len, 3, H, head_dim)
        qkv = qkv.transpose(2, 0, 3, 1, 4)
        q, k, v = (qkv[0], qkv[1], qkv[2])
        attn_weights = jnp.einsum('bhqd,bhkd->bhqk', q, k) * scale
        top_k = max(1, int(SPARSITY * tgt_len))
        top_k = min(top_k, tgt_len)
        kth = jax.lax.top_k(attn_weights, top_k)[0][..., -1:]
        min_val = jnp.finfo(attn_weights.dtype).min
        sparse_weights = jnp.where(attn_weights >= kth, attn_weights, min_val)
        attn = jax.nn.softmax(sparse_weights.astype(jnp.float32), axis=-1)
        attn = attn.astype(v.dtype)
        out = jnp.einsum('bhqk,bhkd->bqhd', attn, v).reshape(bsz, tgt_len, embed_dim)
        return out @ W_proj + b_proj

    def _L0_ffn_ref(hidden_states, Wg, e_bias, W_gate_up, W_down, Wsg, Wsu, Wsd):
        import jax, jax.numpy as jnp
        import numpy as np
        E = 128
        I = 464
        IS = 928
        K = 6
        G = 1
        TG = 1
        SCALE = 2.5
        CAP = 192

        def moe_forward(hidden_states, Wg, e_bias, W_gate_up, W_down, Wsg, Wsu, Wsd):
            B, S, H = hidden_states.shape
            x = hidden_states.reshape(-1, H)
            T = x.shape[0]
            logits = x.astype(jnp.float32) @ Wg.T
            sig = jax.nn.sigmoid(logits)
            choice = sig + e_bias[None, :]
            grp = choice.reshape(T, G, E // G)
            group_scores = jax.lax.top_k(grp, 2)[0].sum(-1)
            gidx = jax.lax.top_k(group_scores, TG)[1]
            gmask = jnp.zeros((T, G), jnp.float32).at[jnp.arange(T)[:, None], gidx].set(1.0)
            smask = jnp.repeat(gmask, E // G, axis=1)
            scores_for_choice = jnp.where(smask > 0, choice, 0.0)
            topk_idx = jax.lax.top_k(scores_for_choice, K)[1]
            topk_w = jnp.take_along_axis(sig, topk_idx, axis=1)
            topk_w = topk_w / (topk_w.sum(-1, keepdims=True) + 1e-20)
            topk_w = topk_w * SCALE
            P = T * K
            flat_e = topk_idx.reshape(-1)
            order = jnp.argsort(flat_e)
            se = flat_e[order]
            counts = jax.ops.segment_sum(jnp.ones(P, jnp.int32), flat_e, num_segments=E)
            starts = jnp.cumsum(counts) - counts
            pos = jnp.arange(P) - starts[se]
            buf_idx = jnp.where(pos < CAP, se * CAP + pos, E * CAP)
            tok_of_pair = (order // K).astype(jnp.int32)
            w_of_pair = topk_w.reshape(-1)[order]
            token_buf = jnp.zeros((E * CAP,), jnp.int32).at[buf_idx].set(tok_of_pair, mode='drop')
            w_buf = jnp.zeros((E * CAP,), x.dtype).at[buf_idx].set(w_of_pair.astype(x.dtype), mode='drop')
            xb = x[token_buf].reshape(E, CAP, H)
            gu = jnp.einsum('ech,ehf->ecf', xb, W_gate_up)
            g, u = jnp.split(gu, 2, axis=-1)
            inter = jax.nn.silu(g) * u
            yb = jnp.einsum('eci,eih->ech', inter, W_down)
            yb = yb * w_buf.reshape(E, CAP, 1)
            routed = jnp.zeros((T, H), x.dtype).at[token_buf].add(yb.reshape(E * CAP, H))
            shared = jax.nn.silu(x @ Wsg) * (x @ Wsu) @ Wsd
            return (routed + shared).reshape(B, S, H)
        return moe_forward(hidden_states, Wg, e_bias, W_gate_up, W_down, Wsg, Wsu, Wsd)
    h = _L0_tok_ref(x, L0_tok_patch_w, L0_tok_patch_b, L0_tok_ln_g, L0_tok_ln_b, L0_tok_qkv_w, L0_tok_qkv_b, L0_tok_proj_w, L0_tok_proj_b, L0_tok_ff1_w, L0_tok_ff1_b, L0_tok_ff2_w, L0_tok_ff2_b)
    h = jnp.concatenate([jnp.broadcast_to(cls_tok, (h.shape[0], 1, h.shape[2])), h], axis=1)
    h = h + _L0_attn_ref(_layernorm(h, axis=-1), L0_attn_W_qkv, L0_attn_b_qkv, L0_attn_W_proj, L0_attn_b_proj)
    h = h + _L0_ffn_ref(_layernorm(h, axis=-1), L0_ffn_Wg, L0_ffn_e_bias, L0_ffn_W_gate_up, L0_ffn_W_down, L0_ffn_Wsg, L0_ffn_Wsu, L0_ffn_Wsd)
    return h

_drawn_inputs = setup_inputs


def setup_inputs(seed=0):
    import zlib

    import numpy as np

    out = dict(_drawn_inputs(seed))
    spreads = {'L0_tok_patch_b': (0.0, 0.1),
     'L0_tok_ln_g': (1.0, 0.2),
     'L0_tok_ln_b': (0.0, 0.1),
     'L0_tok_qkv_b': (0.0, 0.303),
     'L0_tok_proj_b': (0.0, 0.1),
     'L0_tok_ff1_b': (0.0, 0.1),
     'L0_tok_ff2_b': (0.0, 0.1),
     'L0_ffn_e_bias': (0.0, 0.641)}
    factors = {'L0_tok_qkv_w': 5.398,
     'L0_attn_b_qkv': 3.067,
     'L0_attn_b_proj': 3.9,
     'L0_ffn_Wg': 8.0,
     'L0_ffn_W_gate_up': 7.785,
     'L0_ffn_W_down': 7.736,
     'L0_ffn_Wsg': 3.166,
     'L0_ffn_Wsu': 3.137,
     'L0_ffn_Wsd': 3.105}
    for name, (base, spread) in spreads.items():
        noise = np.random.default_rng([zlib.crc32(name.encode()), seed]).standard_normal(out[name].shape)
        drawn = base * np.exp(spread * noise) if base else spread * noise
        out[name] = jnp.asarray(drawn.astype(out[name].dtype))
    for name, factor in factors.items():
        out[name] = (out[name] * factor).astype(out[name].dtype)
    return out
```

```python
import concourse.bass as bass
from concourse import mybir
from contextlib import ExitStack

B, C, IMG, PATCH = 32, 3, 128, 16
D = 192
NP = (IMG // PATCH) ** 2
NKEY = NP + 1
T = B * NKEY
NH, DH = 12, 16
F = 768
TOP_KEYS = int(0.4 * NKEY)
E, TOPE, CAP = 128, 6, 192
I = 464
IS = 928
TILES = B * NP // 128
KC = C * PATCH * PATCH // 128
DA, DB = 128, D - 128
FC = F // 128
HB = NH // 4
VD = DH + 1
SC = 116
NSC, NIC = IS // SC, I // SC
EK = D // 2
HS = CAP // 2
NT = TILES + 1
DUMMY = T
ROWS = T + CAP
STEPS = 150
LIST = E + 4

SEMAPHORES = """
    zero_rows rows_free patch_mm xm_ready x_stored0 acc_ready x_stored1 cls_stored rows_ready
    list_ready down_mm w_loaded0 w_loaded1 h0_ready h0_T ff0_xT ff0_up ff0_hid ff0_down y_ready
    y_T at0_xT at0_qk at0_v at0_k_sb at0_qk_sb at0_s at0_p held at0_T0 at0_aT0 at0_T1 at0_aT1
    at0_o at0_osb at0_oT at0_oxT at0_proj h1_ready h1_T ff1_xT ff1_up ff1_hid ff1_down n2_ready
    n2_T at1_xT at1_qk at1_v at1_k_sb at1_qk_sb at1_s at1_p at1_T0 at1_aT0 at1_T1 at1_aT1 at1_o
    at1_osb at1_oT cls_oT at1_oxT at1_proj xm_T xm_xT logits sh_up0 sh_inner0 sh_up1 sh_inner1
    sh_down cls_osb chosen_all slots_mm slots_done count_mm active_ready rank_mm pick_ready
    list_mm hot_ready y_done index_mm gathered0 xe_T xeT_ready einner0 eup0 einner1 eup1
    gathered1 index_ready ff0_sq ff0_poly ff0_th at0_v_sb at0_sub ff1_sq ff1_poly ff1_th
    at1_v_sb at1_s_sb at1_sub at1_exp sig_exp sh_th0 sh_th1 eth0 eth1 step sums memsets top_max
    h3_ready slots_ready active_f rank_ready index_a index_b esilu0 esilu1 add_done added
"""


def tower_kernel(nc, a, out):
    f32, bf16, i32 = mybir.dt.float32, mybir.dt.bfloat16, mybir.dt.int32
    ALU, ACT, AX = mybir.AluOpType, mybir.ActivationFunctionType, mybir.AxisListType

    ctx = ExitStack()
    with ctx:
        def sb(name, shape, dt=f32):
            return ctx.enter_context(nc.sbuf_tensor("b_" + name, shape, dt))

        def two(name, shape, dt=f32):
            return [sb(f"{name}{s}", shape, dt) for s in range(2)]

        arena = [sb(f"arena{s}", [128, 5760]) for s in range(2)]

        def carve(start, rows, *dims, dt=f32):
            n = 1
            for d in dims:
                n *= d
            n = n if dt == f32 else n // 2
            views = [x[0:rows, start:start + n] for x in arena]
            if dt != f32:
                views = [x.bitcast(dt) for x in views]
            if len(dims) == 2:
                views = [x.rearrange("p (a b) -> p a b", b=dims[1]) for x in views]
            return views, start + n

        def pb(name, shape, dt=f32):
            return ctx.enter_context(nc.psum_tensor("p_" + name, shape, dt))

        def sem(name):
            return ctx.enter_context(nc.semaphore("s_" + name))

        ident = sb("ident", [128, 128])
        patch_w = sb("patch_w", [128, KC, D])
        patch_b = sb("patch_b", [128, D])
        ln_g = sb("ln_g", [128, D])
        ln_b = sb("ln_b", [128, D])
        pe_sb = sb("pe", [128, D])
        ff1a, ff1b = sb("ff1a", [DA, F]), sb("ff1b", [DB + 1, F])
        ff2 = sb("ff2", [128, FC, D])
        ff2_b = sb("ff2_b", [128, D])
        wqk = [(sb(f"wqk{n}a", [DA, 2 * HB * 128]), sb(f"wqk{n}b", [DB + 1, 2 * HB * 128])) for n in range(2)]
        wv = [(sb(f"wv{n}a", [DA, D]), sb(f"wv{n}b", [DB + 1, D])) for n in range(2)]
        wo = [(sb(f"wo{n}a", [DA, D]), sb(f"wo{n}b", [DB + 1, D])) for n in range(2)]
        wg_a, wg_b = sb("wg_a", [DA, E]), sb("wg_b", [DB, E])
        e_bias = sb("e_bias", [128, E])
        wsga, wsgb = sb("wsga", [DA, IS]), sb("wsgb", [DB, IS])
        wsua, wsub = sb("wsua", [DA, IS]), sb("wsub", [DB, IS])
        wsd = sb("wsd", [SC, NSC, D])
        cls_row = sb("cls_row", [B, D])
        mask_q = sb("mask_q", [128, HB, 64])
        mask_o = sb("mask_o", [128, D])
        img_sel = sb("img_sel", [128, 2])
        zrows = sb("zrows", [CAP // 2, 2 * D])
        before_f = sb("before_f", [128, 128])
        cls_before_f = arena[0][0:B, 0:TILES * 128]
        pat_before_f = arena[1][:, 0:TILES * B]
        iota_f = sb("iota_f", [128, CAP])
        tok_f = sb("tok_f", [128, NT * 3])
        dummy_f = sb("dummy_f", [HS, 2])
        eval_f = sb("eval_f", [128, 2])
        before = sb("before", [128, 128], bf16)
        cls_before = sb("cls_before", [B, TILES * 128], bf16)
        pat_before = sb("pat_before", [128, TILES * B], bf16)
        ones = sb("ones", [128, 128], bf16)
        eval_b = sb("eval_b", [128, 2], bf16)

        xp = two("xp", [128, KC, 128])
        h0, h1, h2, norm = two("h0", [128, D]), two("h1", [128, D]), two("h2", [128, D]), two("norm", [128, D])
        ln_in, h3 = h1, h1
        stat, mv, rstd = two("stat", [128, 6]), two("mv", [128, 2]), two("rstd", [128, 1])
        var, newton = two("var", [128, 1]), two("newton", [128, 1])
        xTa, xTb = two("xTa", [DA, 128]), two("xTb", [DB + 1, 128])
        sq, hid = two("sq", [128, F]), two("hid", [128, F])
        qT = two("qT", [128, HB, 128])
        kT2 = two("kT2", [128, HB, 2, NKEY])
        vv = two("vv", [NP, 2, NH, VD])
        vv2 = two("vv2", [NKEY, 2, NH, VD])
        att, at = carve(0, 128, (NH + 1) * NKEY)
        sc_sb, at = carve(at, 128, (NH + 1) * NKEY)
        work, at = carve(at, 128, (NH + 1) * NKEY)
        aT, at = carve(at, NKEY, NH + 1, 128)
        mx = two("mx", [128, NH])
        top_a, top_b, top_c, top_d = (two(f"top_{n}", [128, (NH + 1) * 8]) for n in "abcd")
        rr, rc = two("rr", [128, NH]), two("rc", [128, 1])
        o_sb, oc_sb = two("o_sb", [128, D]), two("oc_sb", [128, D])
        xm, acc = two("xm", [128, D]), two("acc", [128, D])
        sig, wtok = two("sig", [128, E]), two("wtok", [128, E])
        choice, picked = two("choice", [128, E + 2]), two("picked", [128, E + 2])
        best = two("best", [128, 8])
        wsum, wres = two("wsum", [128, 1]), two("wres", [128, E])
        k_blk, at = carve(at, 128, HB * 2, 4 * NKEY)
        k_blk = [x.rearrange("p (m g) (j k) -> p m g j k", g=2, k=NKEY) for x in k_blk]
        assert at <= 5760
        th, at = carve(0, SC, 4 * 128)
        inner, at = carve(at, SC, NSC, 128)

        oclsTa, oclsTb = sb("oclsTa", [DA, B]), sb("oclsTb", [DB + 1, B])
        cxTa, cxTb = sb("cxTa", [DA, B]), sb("cxTb", [DB + 1, B])
        qcls = sb("qcls", [128, HB])
        qcls_blk = sb("qcls_blk", [128, HB, 64])
        v_cls = sb("v_cls", [NKEY, D])

        chosen = sb("chosen", [128, NT, E], bf16)
        before_sum = sb("before_sum", [128, NT, E], bf16)
        wsplit = sb("wsplit", [128, NT, E + 1, 3], bf16)
        slot = sb("slot", [128, NT, E + 1], bf16)
        counts, active_f = sb("counts", [128, 1]), sb("active_f", [128, 1])
        active = sb("active", [128, 1], bf16)
        rank, pick = sb("rank", [128, 1]), sb("pick", [128, LIST], bf16)
        lists = sb("lists", [1, 2 * LIST + 2], i32)

        hot, at = carve(0, 128, NT, CAP, dt=bf16)
        rhs = two("rhs", [128, NT, 6], bf16)
        slot_a, slot_b = two("slot_a", [HS, 2]), two("slot_b", [HS, 2])
        slot_w = two("slot_w", [HS, 2])
        index, add_index = two("index", [HS, 2], i32), two("add_index", [HS, 2], i32)
        xeT = two("xeT", [EK, 2, CAP])
        w_gu, at = carve(at, EK, 2, 2 * I)
        w_dn, at = carve(at, SC, NIC, D)
        xg, at = carve(at, HS, 2, D)
        einner, at = carve(at, SC, NIC, CAP)
        assert at <= 5760
        eth = [x[0:SC, 0:2 * CAP] for x in hid]
        y = [x[0:HS, 0:2 * D].rearrange("p (h d) -> p h d", d=D) for x in sq]

        big = [pb(f"big{s}", [128, 2, 512]) for s in range(2)]
        small = [pb(f"small{s}", [128, 512]) for s in range(2)]
        aux = [pb(f"aux{s}", [128, 512]) for s in range(2)]

        x_rows = nc.dram_tensor("x_rows", [ROWS, D], f32).ap()
        x_img = x_rows[0:T, :].rearrange("(b q) d -> b q d", q=NKEY)
        out_img = out[0:T, :].rearrange("(b q) d -> b q d", q=NKEY)

        consts = sem("consts")
        cls_loads = sem("cls_loads")
        xp_loaded = [sem(f"xp_loaded{s}") for s in range(2)]
        presets = sem("presets")
        acts_preset = sem("acts_preset")
        cls_norm = sem("cls_norm")
        cls_T, cls_xT, cls_qk, cls_q, cls_v, cls_ready = (sem("cls_" + n) for n in ("T", "xT", "qk", "q", "v", "ready"))
        named = {name: sem(name) for name in SEMAPHORES.split()}

        def S(name):
            return named[name]

        def hold(eng, semaphore, value):
            eng.wait_ge(semaphore, value)
            eng.sem_inc(S("held"), 1)

        def halves(w, n):
            return [(w[0][:], n[0:DA, :]), (w[1][0:DB, :], n[DA:D, :])]

        def row(w, bias):
            return [(w[1][DB:DB + 1, :], bias.partition_broadcast(1))]

        def everywhere(v, n=128):
            return v.partition_broadcast(n)

        first_loads = [(ident[:], a["ident"]), (cls_row[:], everywhere(a["cls"], B)),
                       (mask_q[:], a["mask_q"]),
                       *halves(wqk[1], a["wqk2"]), *row(wqk[1], a["bqk2"]),
                       *halves(wv[1], a["wv2"]), *row(wv[1], a["bv2"])]
        loads = [(patch_w[:], a["patch_w"]), (patch_b[:], everywhere(a["patch_b"])),
                 (ln_g[:], everywhere(a["ln_g"])), (ln_b[:], everywhere(a["ln_b"])), (pe_sb[:], a["pe"]),
                 *halves((ff1a, ff1b), a["ff1_w"]), *row((ff1a, ff1b), a["ff1_b"]),
                 (ff2[:], a["ff2_w"].rearrange("(c p) d -> p c d", p=128)), (ff2_b[:], everywhere(a["ff2_b"])),
                 *halves(wqk[0], a["wqk1"]), *row(wqk[0], a["bqk1"]),
                 *halves(wv[0], a["wv1"]), *row(wv[0], a["bv1"]),
                 *halves(wo[0], a["proj1_w"]), *row(wo[0], a["proj1_b"]),
                 *halves(wo[1], a["proj2_w"]), *row(wo[1], a["proj2_b"]),
                 (wg_a[:], a["wgT"][0:DA, :]), (wg_b[:], a["wgT"][DA:D, :]), (e_bias[:], everywhere(a["e_bias"])),
                 (wsga[:], a["wsg"][0:DA, :]), (wsgb[:], a["wsg"][DA:D, :]),
                 (wsua[:], a["wsu"][0:DA, :]), (wsub[:], a["wsu"][DA:D, :]),
                 (wsd[:], a["wsd"].rearrange("(c p) d -> p c d", p=SC)),
                 (mask_o[:], a["mask_o"]), (img_sel[:], a["img_sel"]),
                 (before_f[:], a["before"]), (cls_before_f, a["cls_before"]), (pat_before_f, a["pat_before"]),
                 (iota_f[:], a["iota"]), (tok_f[:], a["tok"]), (dummy_f[:], a["dummy"]), (eval_f[:], a["evals"])]
        N_FIRST, N_CONST = 16 * len(first_loads), 16 * len(loads)

        block = ctx.enter_context(nc.Block())

        def s1_scores(s):
            return big[s][:, :, 0:6 * NP].rearrange("p b (h k) -> p b h k", k=NP)

        def k_psum(s):
            return big[s][:, 1, 0:384].rearrange("p (m g t) -> p m g t", g=2, t=NP)

        @block.sync
        def _(sp):
            for dst, src in first_loads:
                sp.dma_start(dst, src).then_inc(cls_loads, 16)
            for s in range(2):
                sp.dma_start(xp[s][:], a["xp"][s]).then_inc(xp_loaded[s], 16)
            for dst, src in loads:
                sp.dma_start(dst, src).then_inc(consts, 16)
            sp.wait_ge(presets, 1)
            sp.dma_start(x_rows[T:ROWS, :].rearrange("(p r) d -> p (r d)", r=2), zrows[:]).then_inc(S("zero_rows"), 16)
            sp.dma_start(out[T:ROWS, :].rearrange("(p r) d -> p (r d)", r=2), zrows[:]).then_inc(S("zero_rows"), 16)
            sp.sem_inc(S("rows_free"), 2)

            def stores(i, s, v):
                sp.wait_ge(S("xm_ready"), v)
                for g in range(2):
                    sp.dma_start(x_img[4 * i + 2 * s + g, 1:NKEY, :], xm[s][64 * g:64 * g + 64, :])\
                      .then_inc(S(f"x_stored{s}"), 16)
                sp.wait_ge(S("acc_ready"), v + 2)
                for g in range(2):
                    sp.dma_start(out_img[4 * i + 2 * s + g, 1:NKEY, :], acc[s][64 * g:64 * g + 64, :])\
                      .then_inc(S(f"x_stored{s}"), 16)

            def stored(i, s):
                sp.wait_ge(S(f"x_stored{s}"), 64 * i + 64)
                sp.sem_inc(S("rows_free"), 1)

            with sp.Fori(0, TILES // 2 - 1) as i:
                for s in range(2):
                    sp.wait_ge(S("patch_mm"), 2 * i + s + 1)
                    sp.dma_start(xp[s][:], a["xp"][2 * i + s + 2]).then_inc(xp_loaded[s], 16)
                for s in range(2):
                    stores(i, s, 2 * i + s + 1)
                for s in range(2):
                    stored(i, s)
            last = TILES // 2 - 1
            for s in range(2):
                stores(last, s, 2 * last + s + 1)
            for s in range(2):
                stored(last, s)
            sp.wait_ge(S("xm_ready"), NT)
            sp.dma_start(x_img[:, 0, :], xm[0][0:B, :]).then_inc(S("cls_stored"), 16)
            sp.wait_ge(S("acc_ready"), NT + 2)
            sp.dma_start(out_img[:, 0, :], acc[0][0:B, :]).then_inc(S("cls_stored"), 16)
            sp.wait_ge(S("cls_stored"), 32)
            sp.wait_ge(S("zero_rows"), 32)
            sp.sem_inc(S("rows_ready"), 1)

            sp.wait_ge(S("list_ready"), 1)
            n2 = sp.value_load(lists[0:1, 2 * LIST:2 * LIST + 1], min_val=1, max_val=E // 2)
            sp.sem_inc(S("down_mm"), 2)
            with sp.Fori(0, n2) as i:
                for s in range(2):
                    e = sp.value_load(lists[0:1, bass.ds(LIST + 2 * i + s, 1)], min_val=0, max_val=E - 1)
                    sp.wait_ge(S("down_mm"), 2 * i + s + 1)
                    dn = a["w_down"][e].rearrange("(c p) d -> p c d", p=SC)
                    sp.dma_start(w_gu[s][:], a["w_gate_up"][e].rearrange("(k p) f -> p k f", p=EK)).then_inc(S(f"w_loaded{s}"), 16)
                    sp.dma_start(w_dn[s][0:112], dn[0:112]).then_inc(S(f"w_loaded{s}"), 16)
                    sp.dma_start(w_dn[s][112:SC], dn[112:SC]).then_inc(S(f"w_loaded{s}"), 16)

        @block.tensor
        def _(pe):
            mm, tr = nc.tensor.matmul, nc.tensor.transpose

            def to_features(src, s, rows, done):
                tr(small[s][0:DA, 0:rows], src[0:rows, 0:DA], ident[0:rows, 0:rows])
                tr(small[s][0:DB, 128:128 + rows], src[0:rows, DA:D], ident[0:rows, 0:rows]).then_inc(done, 1)

            def ff(s, v, n):
                pe.wait_ge(S(f"ff{n}_xT"), v)
                for c in range(FC):
                    o = big[s][:, c // 3, (c % 3) * 128:(c % 3 + 1) * 128]
                    mm(o, ff1a[:, c * 128:(c + 1) * 128], xTa[s][:], start=True, stop=False)
                    last = mm(o, ff1b[:, c * 128:(c + 1) * 128], xTb[s][:], start=False, stop=True)
                last.then_inc(S(f"ff{n}_up"), 1)
                yield
                pe.wait_ge(S(f"ff{n}_hid"), v)
                for c in range(FC):
                    last = mm(small[s][:, 0:D], hid[s][:, c * 128:(c + 1) * 128], ff2[:, c, :],
                              start=(c == 0), stop=(c == FC - 1))
                last.then_inc(S(f"ff{n}_down"), 1)
                yield

            def qkv(s, v, n):
                pe.wait_ge(S(f"at{n}_xT"), v)
                for m in range(2 * HB):
                    o = big[s][:, m // HB, (m % HB) * 128:(m % HB + 1) * 128]
                    mm(o, wqk[n][0][:, m * 128:(m + 1) * 128], xTa[s][:], start=True, stop=False)
                    last = mm(o, wqk[n][1][:, m * 128:(m + 1) * 128], xTb[s][:], start=False, stop=True)
                last.then_inc(S(f"at{n}_qk"), 1)
                for g in range(2):
                    o = aux[s][0:NP, g * D:(g + 1) * D]
                    mm(o, xTa[s][:, 64 * g:64 * g + 64], wv[n][0][:], start=True, stop=False)
                    last = mm(o, xTb[s][:, 64 * g:64 * g + 64], wv[n][1][:], start=False, stop=True)
                last.then_inc(S(f"at{n}_v"), 1)
                yield

            def scores(s, v, n):
                keys, per_bank = ((NP, 6), (NKEY, 7))[n]
                pe.wait_ge(S(f"at{n}_k_sb"), v)
                pe.wait_ge(S(f"at{n}_qk_sb"), v)
                for g in range(2):
                    rows = slice(64 * g, 64 * g + 64)
                    for m in range(HB):
                        cut = min(max(per_bank - 4 * m, 0), 4)
                        for lo, hi in ((0, cut), (cut, 4)):
                            if lo < hi:
                                h = 4 * m + lo
                                at = (h % per_bank) * keys
                                last = mm(big[s][rows, h // per_bank, at:at + (hi - lo) * keys],
                                          qT[s][:, m, rows], k_blk[s][:, m, g, lo:hi, 0:keys], start=True, stop=True)
                if n == 1:
                    at = (NH % per_bank) * keys
                    for g in range(2):
                        for m in range(HB):
                            last = mm(big[s][64 * g:64 * g + 64, 1, at:at + keys],
                                      qcls_blk[:, m, :], kT2[s][:, m, g, :], start=(m == 0), stop=(m == HB - 1))
                last.then_inc(S(f"at{n}_s"), 1)
                yield

            def weigh(s, v, n):
                keys, heads = ((NP, NH), (NKEY, NH + 1))[n]
                for part, (lo, hi) in enumerate(((0, 8), (8, heads))):
                    hold(pe, S(f"at{n}_p") if part == 0 else S(f"at{n}_aT0"), v)
                    for h in range(lo, hi):
                        r = h - lo
                        last = tr(big[s][0:keys, r // 4, (r % 4) * 128:(r % 4 + 1) * 128],
                                  att[s][:, h * keys:(h + 1) * keys], ident[:])
                    last.then_inc(S(f"at{n}_T{part}"), 1)
                    yield
                v_sb = (vv, vv2)[n][s]
                hold(pe, S(f"at{n}_aT1"), v)
                for g in range(2):
                    rows = slice(64 * g, 64 * g + 64)
                    for h in range(NH):
                        last = mm(small[s][rows, h * VD:(h + 1) * VD], aT[s][0:keys, h, rows], v_sb[:, g, h, :],
                                  start=True, stop=True)
                    if n == 1:
                        last = mm(aux[s][rows, 0:NH * VD], aT[s][0:keys, NH, rows],
                                  v_sb[:, g, :, :].rearrange("p h d -> p (h d)"), start=True, stop=True)
                last.then_inc(S(f"at{n}_o"), 1)
                yield
                pe.wait_ge(S(f"at{n}_osb"), v)
                to_features(o_sb[s], s, 128, S(f"at{n}_oT"))
                if n == 1:
                    mm(aux[s][:, 256:258], oc_sb[s][:, 0:DA], img_sel[:], start=True, stop=True)
                    mm(aux[s][0:DB, 258:260], oc_sb[s][:, DA:D], img_sel[:], start=True, stop=True).then_inc(S("cls_oT"), 1)
                yield

            def project(s, v, n, la, lb, rows, ready):
                pe.wait_ge(ready, v)
                mm(small[s][0:rows, 0:D], la, wo[n][0][:], start=True, stop=False)
                mm(small[s][0:rows, 0:D], lb, wo[n][1][:], start=False, stop=True).then_inc(S(f"at{n}_proj"), 1)
                yield

            def experts_in(s, v, rows):
                pe.wait_ge(S("xm_ready"), v)
                to_features(xm[s], s, rows, S("xm_T"))
                yield
                pe.wait_ge(S("xm_xT"), v)
                mm(aux[s][0:rows, 0:E], xTa[s][:, 0:rows], wg_a[:], start=True, stop=False)
                mm(aux[s][0:rows, 0:E], xTb[s][0:DB, 0:rows], wg_b[:], start=False, stop=True).then_inc(S("logits"), 1)
                for half in range(2):
                    if half:
                        pe.wait_ge(S("sh_inner0"), v)
                    for r in range(4):
                        c = 4 * half + r
                        for bank, (wa, wb) in enumerate(((wsga, wsgb), (wsua, wsub))):
                            o = big[s][0:SC, bank, r * 128:r * 128 + rows]
                            mm(o, wa[:, c * SC:(c + 1) * SC], xTa[s][:, 0:rows], start=True, stop=False)
                            last = mm(o, wb[:, c * SC:(c + 1) * SC], xTb[s][0:DB, 0:rows], start=False, stop=True)
                    last.then_inc(S(f"sh_up{half}"), 1)
                    yield
                pe.wait_ge(S("sh_inner1"), v)
                for c in range(NSC):
                    last = mm(small[s][0:rows, 0:D], inner[s][:, c, 0:rows], wsd[:, c, :],
                              start=(c == 0), stop=(c == NSC - 1))
                last.then_inc(S("sh_down"), 1)
                yield

            pe.wait_ge(cls_loads, N_FIRST)
            pe.wait_ge(cls_norm, 1)
            tr(small[0][0:DA, 0:B], norm[0][0:B, 0:DA], ident[0:B, 0:B])
            tr(small[0][0:DB, 128:128 + B], norm[0][0:B, DA:D], ident[0:B, 0:B]).then_inc(cls_T, 1)
            pe.wait_ge(cls_xT, 1)
            for m in range(2 * HB):
                mm(small[1][:, m:m + 1], wqk[1][0][:, m * 128:(m + 1) * 128], cxTa[:, 0:1], start=True, stop=False)
                last = mm(small[1][:, m:m + 1], wqk[1][1][:, m * 128:(m + 1) * 128], cxTb[:, 0:1], start=False, stop=True)
            last.then_inc(cls_qk, 1)
            mm(aux[0][NP:NKEY, 0:D], cxTa[:, 0:1], wv[1][0][:], start=True, stop=False)
            mm(aux[0][NP:NKEY, 0:D], cxTb[:, 0:1], wv[1][1][:], start=False, stop=True).then_inc(cls_v, 1)
            pe.wait_ge(cls_ready, 1)
            pe.wait_ge(acts_preset, 1)
            pe.wait_ge(consts, N_CONST)

            with pe.Fori(0, TILES // 2) as i:
                def tile(s):
                    v = 2 * i + s + 1
                    pe.wait_ge(xp_loaded[s], 16 * i + 16)
                    pe.wait_ge(S("acc_ready"), v)
                    for c in range(KC):
                        last = mm(small[s][:, 0:D], xp[s][:, c, :], patch_w[:, c, :], start=(c == 0), stop=(c == KC - 1))
                    last.then_inc(S("patch_mm"), 1)
                    yield
                    pe.wait_ge(S("h0_ready"), v)
                    to_features(h0[s], s, 128, S("h0_T"))
                    yield
                    yield from ff(s, v, 0)
                    pe.wait_ge(S("y_ready"), v)
                    to_features(norm[s], s, 128, S("y_T"))
                    yield
                    yield from qkv(s, v, 0)
                    yield from scores(s, v, 0)
                    yield from weigh(s, v, 0)
                    yield from project(s, v, 0, xTa[s][:], xTb[s][:], 128, S("at0_oxT"))
                    pe.wait_ge(S("h1_ready"), v)
                    to_features(h1[s], s, 128, S("h1_T"))
                    yield
                    yield from ff(s, v, 1)
                    pe.wait_ge(S("n2_ready"), v)
                    to_features(norm[s], s, 128, S("n2_T"))
                    yield
                    yield from qkv(s, v, 1)
                    yield from scores(s, v, 1)
                    yield from weigh(s, v, 1)
                    yield from project(s, v, 1, xTa[s][:], xTb[s][:], 128, S("at1_oxT"))
                    yield from experts_in(s, v, 128)
                for _ in zip(tile(0), tile(1)):
                    pass

            pe.wait_ge(S("acc_ready"), NT)
            for _ in project(0, TILES, 1, oclsTa[:], oclsTb[:], B, S("cls_osb")):
                pass
            for _ in experts_in(0, NT, B):
                pass

            pe.wait_ge(S("chosen_all"), 1)
            for t in range(TILES):
                p = big[t % 2][:, 0, 0:E]
                if t >= 2:
                    pe.wait_ge(S("slots_done"), t - 1)
                mm(p, before[:], chosen[:, t, :], start=True, stop=False)
                mm(p, ones[:], before_sum[:, t, :], start=False, stop=False)
                mm(p, cls_before[:, t * 128:(t + 1) * 128], chosen[0:B, TILES, :], start=False, stop=True)\
                    .then_inc(S("slots_mm"), 1)
            pe.wait_ge(S("slots_done"), TILES - 1)
            for t in range(TILES):
                mm(big[0][0:B, 0, 0:E], pat_before[:, t * B:(t + 1) * B], chosen[:, t, :], start=(t == 0), stop=False)
            mm(big[0][0:B, 0, 0:E], before[0:B, 0:B], chosen[0:B, TILES, :], start=False, stop=True)\
                .then_inc(S("slots_mm"), 1)
            mm(small[1][:, 0:1], before_sum[:, TILES, :], ones[:, 0:1], start=True, stop=False)
            mm(small[1][:, 0:1], chosen[0:B, TILES, :], ones[0:B, 0:1], start=False, stop=True).then_inc(S("count_mm"), 1)
            pe.wait_ge(S("active_ready"), 1)
            mm(small[0][:, 0:1], before[:], active[:], start=True, stop=True).then_inc(S("rank_mm"), 1)
            pe.wait_ge(S("pick_ready"), 1)
            mm(aux[1][0:1, 0:LIST], eval_b[:, 0:1], pick[:], start=True, stop=True)
            mm(aux[1][0:1, LIST:2 * LIST], eval_b[:, 1:2], pick[:], start=True, stop=True)
            mm(aux[1][0:1, 2 * LIST:2 * LIST + 1], active[:], ones[:, 0:1], start=True, stop=True).then_inc(S("list_mm"), 1)

            def slots_of(s, v):
                pe.wait_ge(S("hot_ready"), v)
                pe.wait_ge(S("y_done"), v)
                for h in range(2):
                    for t in range(NT):
                        last = mm(aux[s][0:HS, 6 * h:6 * h + 6], hot[s][:, t, h * HS:(h + 1) * HS], rhs[s][:, t, :],
                                  start=(t == 0), stop=(t == NT - 1))
                last.then_inc(S("index_mm"), 1)

            def gathered(s, gather_value, v):
                pe.wait_ge(S(f"gathered{s}"), gather_value)
                for h in range(2):
                    for k in range(2):
                        last = tr(small[s][0:EK, k * CAP + h * HS:k * CAP + (h + 1) * HS],
                                  xg[s][:, h, k * EK:(k + 1) * EK], ident[0:HS, 0:HS])
                last.then_inc(S("xe_T"), 1)

            pe.wait_ge(S("list_ready"), 1)
            n2 = pe.value_load(lists[0:1, 2 * LIST:2 * LIST + 1], min_val=1, max_val=E // 2)
            slots_of(0, 1)
            gathered(0, 32, 1)
            with pe.Fori(0, n2) as i:
                for s in range(2):
                    v = 2 * i + s + 1
                    slots_of(1 - s, v + 1)
                    pe.wait_ge(S(f"w_loaded{s}"), 48 * i + 48)
                    pe.wait_ge(S("xeT_ready"), v)
                    for r in range(2):
                        pe.wait_ge(S(f"einner{r}"), v)
                        for bank in range(2):
                            for j in range(2):
                                c = bank * I + (2 * r + j) * SC
                                for k in range(2):
                                    last = mm(big[r][0:SC, bank, j * CAP:(j + 1) * CAP], w_gu[s][:, k, c:c + SC],
                                              xeT[s][:, k, :], start=(k == 0), stop=(k == 1))
                        last.then_inc(S(f"eup{r}"), 1)
                    gathered(1 - s, 32 * i + 32 + 32 * s, v + 1)
                    pe.wait_ge(S("einner0"), v + 1)
                    pe.wait_ge(S("einner1"), v + 1)
                    pe.wait_ge(S("index_ready"), v)
                    for h in range(2):
                        for c in range(NIC):
                            last = mm(aux[s][0:HS, 64 + h * D:64 + (h + 1) * D],
                                      einner[s][:, c, h * HS:(h + 1) * HS], w_dn[s][:, c, :],
                                      start=(c == 0), stop=(c == NIC - 1))
                    last.then_inc(S("down_mm"), 1)

        @block.scalar
        def _(act):
            f, cp = nc.scalar.activation, nc.scalar.copy

            def features(s, v, rows, wait, done):
                act.wait_ge(wait, v)
                cp(xTa[s][:, 0:rows], small[s][0:DA, 0:rows])
                cp(xTb[s][0:DB, 0:rows], small[s][0:DB, 128:128 + rows]).then_inc(done, 1)

            def ff(s, v, n):
                act.wait_ge(S(f"ff{n}_up"), v)
                u = big[s][:, :, 0:384]
                f(sq[s][:].rearrange("p (b c) -> p b c", b=2), u, ACT.Square, scale=0.044715 ** 0.5).then_inc(S(f"ff{n}_sq"), 1)
                yield
                act.wait_ge(S(f"ff{n}_poly"), v)
                f(hid[s][:], sq[s][:], ACT.Tanh, scale=0.7978845608028654).then_inc(S(f"ff{n}_th"), 1)
                yield

            def attention(s, v, n):
                act.wait_ge(S(f"at{n}_qk"), v)
                cp(qT[s][:], big[s][:, 0, 0:384].rearrange("p (m t) -> p m t", t=128))
                k_in = k_psum(s)
                if n == 1:
                    cp(kT2[s][0:64, :, :, 0:NP], k_in[0:64])
                for j in range(2):
                    rows = slice(32 * j, 32 * j + DH)
                    last = cp(k_blk[s][rows, :, :, j, 0:NP], k_in[rows])
                last.then_inc(S(f"at{n}_qk_sb"), 1)
                act.wait_ge(S(f"at{n}_v"), v)
                for g in range(2):
                    last = cp((vv, vv2)[n][s][0:NP, g, :, 0:DH],
                              aux[s][0:NP, g * D:(g + 1) * D].rearrange("p (h d) -> p h d", d=DH))
                last.then_inc(S(f"at{n}_v_sb"), 1)
                yield
                if n == 1:
                    act.wait_ge(S("at1_s"), v)
                    cp(sc_sb[s][:, 0:7 * NKEY], big[s][:, 0, 0:7 * NKEY])
                    cp(sc_sb[s][:, 7 * NKEY:13 * NKEY], big[s][:, 1, 0:6 * NKEY]).then_inc(S("at1_s_sb"), 1)
                    yield
                keys, heads = ((NP, NH), (NKEY, NH + 1))[n]
                act.wait_ge(S(f"at{n}_sub"), v)
                f(att[s][:, 0:heads * keys], att[s][:, 0:heads * keys], ACT.Exp, scale=float(DH) ** -0.5)\
                    .then_inc(S(f"at{n}_exp" if n else "at0_p"), 1)
                yield
                for part, (lo, hi) in enumerate(((0, 8), (8, heads))):
                    act.wait_ge(S(f"at{n}_T{part}"), v)
                    for bank in range((hi - lo + 3) // 4):
                        m = min(hi - lo - 4 * bank, 4)
                        last = cp(aT[s][0:keys, lo + 4 * bank:lo + 4 * bank + m, :],
                                  big[s][0:keys, bank, 0:m * 128].rearrange("p (h t) -> p h t", t=128))
                    last.then_inc(S(f"at{n}_aT{part}"), 1)
                    yield

            def router(s, v, rows):
                act.wait_ge(S("logits"), v)
                f(sig[s][0:rows, :], aux[s][0:rows, 0:E], ACT.Exp, scale=-1.0).then_inc(S("sig_exp"), 1)

            def shared(s, v, rows):
                for half in range(2):
                    act.wait_ge(S(f"sh_up{half}"), v)
                    g = big[s][0:SC, 0, :].rearrange("p (c t) -> p c t", t=128)[:, :, 0:rows]
                    if half:
                        act.wait_ge(S("sh_inner0"), v)
                    f(th[s][:].rearrange("p (c t) -> p c t", t=128)[:, :, 0:rows], g, ACT.Tanh, scale=0.5)\
                        .then_inc(S(f"sh_th{half}"), 1)
                    yield

            act.wait_ge(cls_T, 1)
            act.wait_ge(presets, 2)
            cp(cxTa[:], small[0][0:DA, 0:B])
            cp(cxTb[0:DB, :], small[0][0:DB, 128:128 + B]).then_inc(cls_xT, 1)
            act.wait_ge(cls_qk, 1)
            cp(qcls[:], small[1][:, 0:HB]).then_inc(cls_q, 1)
            for s in range(2):
                for g in range(2):
                    cp(kT2[s][:, :, g, NP:NKEY], small[1][:, HB:2 * HB].unsqueeze(2))
                    for j in range(4):
                        rows = slice(32 * j, 32 * j + DH)
                        cp(k_blk[s][rows, :, g, j, NP:NKEY], small[1][rows, HB:2 * HB].unsqueeze(2))
            act.wait_ge(cls_v, 1)
            for s in range(2):
                for g in range(2):
                    last = cp(vv2[s][NP:NKEY, g, :, 0:DH], aux[0][NP:NKEY, 0:D].rearrange("p (h d) -> p h d", d=DH))
            last.then_inc(acts_preset, 1)

            with act.Fori(0, TILES // 2) as i:
                def tile(s):
                    v = 2 * i + s + 1
                    features(s, v, 128, S("h0_T"), S("ff0_xT"))
                    yield
                    yield from ff(s, v, 0)
                    features(s, v, 128, S("y_T"), S("at0_xT"))
                    yield
                    yield from attention(s, v, 0)
                    features(s, v, 128, S("at0_oT"), S("at0_oxT"))
                    yield
                    features(s, v, 128, S("h1_T"), S("ff1_xT"))
                    yield
                    yield from ff(s, v, 1)
                    features(s, v, 128, S("n2_T"), S("at1_xT"))
                    yield
                    yield from attention(s, v, 1)
                    features(s, v, 128, S("at1_oT"), S("at1_oxT"))
                    yield
                    features(s, v, 128, S("xm_T"), S("xm_xT"))
                    yield
                    router(s, v, 128)
                    yield from shared(s, v, 128)
                for _ in zip(tile(0), tile(1)):
                    pass
            features(0, NT, B, S("xm_T"), S("xm_xT"))
            router(0, NT, B)
            for _ in shared(0, NT, B):
                pass

            def rows_in(s, v):
                act.wait_ge(S("xe_T"), v)
                cp(xeT[s][:].rearrange("p k c -> p (k c)"), small[s][0:EK, 0:2 * CAP]).then_inc(S("xeT_ready"), 1)

            act.wait_ge(S("list_ready"), 1)
            n2 = act.value_load(lists[0:1, 2 * LIST:2 * LIST + 1], min_val=1, max_val=E // 2)
            rows_in(0, 1)
            with act.Fori(0, n2) as i:
                for s in range(2):
                    v = 2 * i + s + 1
                    for r in range(2):
                        act.wait_ge(S(f"eup{r}"), v)
                        act.wait_ge(S(f"einner{r}"), v)
                        f(eth[r][:], big[r][0:SC, 0, 0:2 * CAP], ACT.Tanh, scale=0.5).then_inc(S(f"eth{r}"), 1)
                    rows_in(1 - s, v + 1)

        @block.vector
        def _(dve):
            V = nc.vector
            ts, tt, stt = V.tensor_scalar, V.tensor_tensor, V.scalar_tensor_tensor

            step = S("step")
            seen = {"base": 0, "n": 0}

            def note(name, s):
                seen["n"] += 1
                seen[name, s] = seen["n"]
                return 1

            def noted(name, s):
                return seen["base"] + seen[name, s]

            def inverse_deviation(s, rows):
                x, r, q = var[s][0:rows, :], rstd[s][0:rows, :], newton[s][0:rows, :]
                dve.wait_ge(step, noted("aggr", s))
                ts(x, mv[s][0:rows, 1:2], 1e-5, None, op0=ALU.add).then_inc(step, note("eps", s))
                yield
                dve.wait_ge(step, noted("eps", s))
                ts(q.bitcast(i32), x.bitcast(i32), 1, None, op0=ALU.logical_shift_right).then_inc(step, note("half_bits", s))
                yield
                dve.wait_ge(step, noted("half_bits", s))
                ts(r.bitcast(i32), q.bitcast(i32), -1.0, float(0x5f3759df), op0=ALU.mult, op1=ALU.add)\
                    .then_inc(step, note("newton2", s))
                yield
                for _ in range(3):
                    dve.wait_ge(step, noted("newton2", s))
                    stt(q, r, r, x, ALU.mult, ALU.mult).then_inc(step, note("newton0", s))
                    yield
                    dve.wait_ge(step, noted("newton0", s))
                    ts(q, q, -0.5, 1.5, op0=ALU.mult, op1=ALU.add).then_inc(step, note("newton1", s))
                    yield
                    dve.wait_ge(step, noted("newton1", s))
                    tt(r, r, q, ALU.mult).then_inc(step, note("newton2", s))
                    yield
                dve.wait_ge(step, noted("newton2", s))

            def layernorm(dst, src, s, v, rows, name, waits=()):
                V.bn_stats(stat[s][0:rows, :], src).then_inc(step, note(name + "_stat", s))
                yield
                hold(dve, step, noted(name + "_stat", s))
                V.bn_aggr(mv[s][0:rows, :], stat[s][0:rows, :]).then_inc(step, note("aggr", s))
                yield
                yield from inverse_deviation(s, rows)
                yield ts(dst, src, mv[s][0:rows, 0:1], rstd[s][0:rows, :], op0=ALU.subtract, op1=ALU.mult)

            def ff(s, v, n):
                u = big[s][:, :, 0:384]
                two_banks = "p (b c) -> p b c"
                dve.wait_ge(S(f"ff{n}_sq"), v)
                stt(sq[s][:].rearrange(two_banks, b=2), sq[s][:].rearrange(two_banks, b=2), 1.0, u, ALU.add, ALU.mult)\
                    .then_inc(S(f"ff{n}_poly"), 1)
                yield
                dve.wait_ge(S(f"ff{n}_th"), v)
                stt(hid[s][:].rearrange(two_banks, b=2), hid[s][:].rearrange(two_banks, b=2), 1.0, u, ALU.add, ALU.mult)\
                    .then_inc(S(f"ff{n}_hid"), 1)
                yield

            def keys_of(s, v, n):
                dve.wait_ge(S(f"at{n}_qk"), v)
                if n == 1:
                    V.tensor_copy(kT2[s][64:128, :, :, 0:NP], k_psum(s)[64:128])
                for j in range(2, 4):
                    rows = slice(32 * j, 32 * j + DH)
                    last = V.tensor_copy(k_blk[s][rows, :, :, j, 0:NP], k_psum(s)[rows])
                last.then_inc(S(f"at{n}_k_sb"), 1)
                yield

            def normalise(s, v, n):
                dve.wait_ge(S(f"at{n}_o"), v)
                o = small[s][:, 0:NH * VD].rearrange("p (h d) -> p h d", d=VD)
                V.reciprocal(rr[s][:].unsqueeze(2), o[:, :, DH:VD]).then_inc(step, note(f"at{n}_rr", s))
                if n == 1:
                    V.reciprocal(rc[s][:], aux[s][:, DH:VD]).then_inc(step, note("cls_rr", s))
                yield
                dve.wait_ge(step, noted(f"at{n}_rr", s))
                last = tt(o_sb[s][:].rearrange("p (h d) -> p h d", d=DH), o[:, :, 0:DH],
                          rr[s][:].unsqueeze(2).to_broadcast([128, NH, DH]), ALU.mult)
                if n == 1:
                    dve.wait_ge(step, noted("cls_rr", s))
                    oc = aux[s][:, 0:NH * VD].rearrange("p (h d) -> p h d", d=VD)
                    last = stt(oc_sb[s][:].rearrange("p (h d) -> p h d", d=DH), oc[:, :, 0:DH], rc[s][:],
                               mask_o[:].rearrange("p (h d) -> p h d", d=DH), ALU.mult, ALU.mult)
                last.then_inc(S(f"at{n}_osb"), 1)
                yield

            def experts_in(s, v, rows, t):
                src = h3[s][0:rows, :]
                dve.wait_ge(S("h3_ready"), v)
                dve.wait_ge(S("rows_free"), v)
                for last in layernorm(xm[s][0:rows, :], src, s, v, rows, "n3"):
                    if last is not None:
                        last.then_inc(S("xm_ready"), 1)
                    yield
                dve.wait_ge(S("sig_exp"), v)
                ts(sig[s][0:rows, :], sig[s][0:rows, :], 1.0, None, op0=ALU.add).then_inc(step, note("sig_add", s))
                yield
                dve.wait_ge(step, noted("sig_add", s))
                V.reciprocal(sig[s][0:rows, :], sig[s][0:rows, :]).then_inc(step, note("sig_rec", s))
                yield
                dve.wait_ge(step, noted("sig_rec", s))
                tt(choice[s][0:rows, 0:E], sig[s][0:rows, :], e_bias[0:rows, :], ALU.add).then_inc(step, note("choice", s))
                yield
                hold(dve, step, noted("choice", s))
                V.max(best[s][0:rows, :], choice[s][0:rows, :]).then_inc(step, note("best", s))
                yield
                hold(dve, step, noted("best", s))
                V.match_replace(picked[s][0:rows, :], best[s][0:rows, :], choice[s][0:rows, :], -3e38).then_inc(step, note("picked", s))
                yield
                dve.wait_ge(step, noted("picked", s))
                ts(chosen[0:rows, t, :], picked[s][0:rows, 0:E], -2e38, None, op0=ALU.is_lt).then_inc(step, note("chosen", s))
                stt(wtok[s][0:rows, :], picked[s][0:rows, 0:E], -2e38, sig[s][0:rows, :], ALU.is_lt, ALU.mult).then_inc(step, note("w_masked", s))
                yield
                dve.wait_ge(step, noted("w_masked", s))
                V.reduce_sum(wsum[s][0:rows, :], wtok[s][0:rows, :], axis=AX.X).then_inc(step, note("w_sum", s))
                yield
                dve.wait_ge(step, noted("w_sum", s))
                ts(wsum[s][0:rows, :], wsum[s][0:rows, :], 1e-20, None, op0=ALU.add).then_inc(step, note("w_eps", s))
                yield
                dve.wait_ge(step, noted("w_eps", s))
                V.reciprocal(wsum[s][0:rows, :], wsum[s][0:rows, :]).then_inc(step, note("w_rec", s))
                yield
                dve.wait_ge(step, noted("w_rec", s))
                ts(wtok[s][0:rows, :], wtok[s][0:rows, :], wsum[s][0:rows, :], 2.5, op0=ALU.mult, op1=ALU.mult).then_inc(step, note("w_tok", s))
                yield
                parts = [wsplit[0:rows, t, 0:E, n:n + 1] for n in range(3)]
                wt, wr = wtok[s][0:rows, :].unsqueeze(2), wres[s][0:rows, :].unsqueeze(2)
                dve.wait_ge(step, noted("w_tok", s))
                V.tensor_copy(parts[0], wt).then_inc(step, note("w_p0", s))
                yield
                dve.wait_ge(step, noted("w_p0", s))
                tt(wr, wt, parts[0], ALU.subtract).then_inc(step, note("w_r0", s))
                yield
                dve.wait_ge(step, noted("w_r0", s))
                V.tensor_copy(parts[1], wr).then_inc(step, note("w_p1", s))
                yield
                dve.wait_ge(step, noted("w_p1", s))
                tt(parts[2], wr, parts[1], ALU.subtract).then_inc(step, note("w_p2", s))
                yield
                for half in range(2):
                    view = "p (c t) -> p c t"
                    thv = th[s][:].rearrange(view, t=128)[:, :, 0:rows]
                    g, u = (big[s][0:SC, b, :].rearrange(view, t=128)[:, :, 0:rows] for b in range(2))
                    dve.wait_ge(S(f"sh_th{half}"), v)
                    stt(thv, thv, 1.0, g, ALU.add, ALU.mult).then_inc(step, note(f"sh_silu{half}", s))
                    yield
                    dve.wait_ge(step, noted(f"sh_silu{half}", s))
                    tt(inner[s][:, 4 * half:4 * half + 4, 0:rows], thv, u, ALU.mult).then_inc(S(f"sh_inner{half}"), 1)
                    yield
                dve.wait_ge(S("sh_down"), v)
                stt(acc[s][0:rows, :], small[s][0:rows, 0:D], 0.5, h3[s][0:rows, :], ALU.mult, ALU.add).then_inc(S("acc_ready"), 1)
                yield

            V.memset(zrows[:], 0.0).then_inc(presets, 1)
            V.memset(cxTb[DB:DB + 1, :], 1.0)
            V.memset(oclsTb[DB:DB + 1, :], 1.0)
            for s in range(2):
                V.memset(xTb[s][DB:DB + 1, :], 1.0)
                V.memset(vv[s][:, :, :, DH:VD], 1.0)
                V.memset(vv2[s][:, :, :, DH:VD], 1.0)
                V.memset(choice[s][:, E:E + 2], 3e38)
                V.memset(k_blk[s], 0.0)
            V.memset(ones[:], 1.0).then_inc(presets, 1)
            V.memset(before_sum[:, 0, :], 0.0).then_inc(S("sums"), 1)
            V.memset(chosen[:, TILES, :], 0.0)
            V.memset(slot[:], -1.0)
            V.memset(wsplit[:], 0.0).then_inc(S("memsets"), 1)
            dve.wait_ge(cls_loads, N_FIRST)
            for last in layernorm(norm[0][0:B, :], cls_row[:], 0, 1, B, "cls"):
                if last is not None:
                    last.then_inc(cls_norm, 1)
            dve.wait_ge(cls_q, 1)
            tt(qcls_blk[:], mask_q[:], qcls[:].unsqueeze(2).to_broadcast([128, HB, 64]), ALU.mult)
            dve.wait_ge(consts, N_CONST)
            tt(pe_sb[:], pe_sb[:], ln_b[:], ALU.add)
            V.tensor_copy(before[:], before_f[:])
            V.tensor_copy(cls_before[:], cls_before_f)
            V.tensor_copy(pat_before[:], pat_before_f)
            V.tensor_copy(eval_b[:], eval_f[:])
            for s in range(2):
                V.tensor_copy(rhs[s][:, :, 0:3], tok_f[:].rearrange("p (t c) -> p t c", c=3))
            V.memset(best[0][0:1, 0:1], 0.0).then_inc(cls_ready, 1)
            dve.wait_ge(cls_ready, 1)
            dve.wait_ge(S("memsets"), 1)
            dve.sem_inc(S("acc_ready"), 2)

            start = seen["n"]
            with dve.Fori(0, TILES // 2) as i:
                seen.update(base=STEPS * i + start, n=0)
                def tile(s):
                    v = 2 * i + s + 1
                    t = 2 * i + s
                    dve.wait_ge(S("patch_mm"), v)
                    tt(ln_in[s][:], small[s][:, 0:D], patch_b[:], ALU.add).then_inc(step, note("patch_x", s))
                    yield
                    dve.wait_ge(step, noted("patch_x", s))
                    for last in layernorm(norm[s][:], ln_in[s][:], s, v, 128, "n0"):
                        if last is not None:
                            last.then_inc(step, note("n0_norm", s))
                        yield
                    dve.wait_ge(step, noted("n0_norm", s))
                    tt(norm[s][:], norm[s][:], ln_g[:], ALU.mult).then_inc(step, note("n0_gain", s))
                    yield
                    dve.wait_ge(step, noted("n0_gain", s))
                    tt(h0[s][:], norm[s][:], pe_sb[:], ALU.add).then_inc(S("h0_ready"), 1)
                    yield
                    yield from ff(s, v, 0)
                    dve.wait_ge(S("ff0_down"), v)
                    stt(norm[s][:], small[s][:, 0:D], 0.5, ff2_b[:], ALU.mult, ALU.add).then_inc(S("y_ready"), 1)
                    yield
                    yield from keys_of(s, v, 0)
                    dve.wait_ge(S("at0_s"), v)
                    V.reduce_max(mx[s][:].rearrange("p (b h) -> p b h", b=2), s1_scores(s), axis=AX.X).then_inc(step, note("at0_max", s))
                    yield
                    dve.wait_ge(step, noted("at0_max", s))
                    tt(att[s][:, 0:NH * NP].rearrange("p (b h k) -> p b h k", b=2, k=NP), s1_scores(s),
                       mx[s][:].rearrange("p (b h) -> p b h", b=2).unsqueeze(3).to_broadcast([128, 2, 6, NP]),
                       ALU.subtract).then_inc(S("at0_sub"), 1)
                    yield
                    yield from normalise(s, v, 0)
                    dve.wait_ge(S("at0_proj"), v)
                    tt(h1[s][:], small[s][:, 0:D], h0[s][:], ALU.add).then_inc(S("h1_ready"), 1)
                    yield
                    dve.wait_ge(S("h1_ready"), v)
                    tt(h2[s][:], h1[s][:], ff2_b[:], ALU.add).then_inc(step, note("h1_bias", s))
                    yield from ff(s, v, 1)
                    dve.wait_ge(S("ff1_down"), v)
                    dve.wait_ge(step, noted("h1_bias", s))
                    stt(h2[s][:], small[s][:, 0:D], 0.5, h2[s][:], ALU.mult, ALU.add).then_inc(step, note("h2_ready", s))
                    yield
                    dve.wait_ge(step, noted("h2_ready", s))
                    for last in layernorm(norm[s][:], h2[s][:], s, v, 128, "n2"):
                        if last is not None:
                            last.then_inc(S("n2_ready"), 1)
                        yield
                    yield from keys_of(s, v, 1)
                    hold(dve, S("at1_s_sb"), v)
                    rounds = (top_a[s], top_b[s], top_c[s], top_d[s])
                    for r, top in enumerate(rounds):
                        if r:
                            hold(dve, step, noted(f"top_cut{r - 1}", s))
                        src = sc_sb[s] if r == 0 else work[s]
                        for h in range(NH + 1):
                            last = V.max(top[:, 8 * h:8 * h + 8], src[:, h * NKEY:(h + 1) * NKEY])
                        if r == 0:
                            last.then_inc(S("top_max"), 1)
                            hold(dve, S("top_max"), v)
                        else:
                            last.then_inc(step, note(f"top_max{r}", s))
                            if r == 3:
                                break
                            hold(dve, step, noted(f"top_max{r}", s))
                        for h in range(NH + 1):
                            last = V.match_replace(work[s][:, h * NKEY:(h + 1) * NKEY], top[:, 8 * h:8 * h + 8],
                                                   src[:, h * NKEY:(h + 1) * NKEY], -3e38)
                        last.then_inc(step, note(f"top_cut{r}", s))
                    yield
                    nth = TOP_KEYS - 24 - 1
                    kth = top_d[s][:].rearrange("p (h e) -> p h e", e=8)[:, :, nth:nth + 1].to_broadcast([128, NH + 1, NKEY])
                    by_head = "p (h k) -> p h k"
                    dve.wait_ge(step, noted("top_max3", s))
                    tt(work[s][:].rearrange(by_head, k=NKEY), sc_sb[s][:].rearrange(by_head, k=NKEY), kth, ALU.is_ge)\
                        .then_inc(step, note("at1_mask", s))
                    yield
                    dve.wait_ge(S("at1_exp"), v)
                    dve.wait_ge(step, noted("at1_mask", s))
                    tt(att[s][:], att[s][:], work[s][:], ALU.mult).then_inc(S("at1_p"), 1)
                    yield
                    yield from normalise(s, v, 1)
                    dve.wait_ge(S("cls_oT"), v)
                    V.tensor_copy(oclsTa[:, bass.ds(2 * t, 2)], aux[s][:, 256:258])
                    V.tensor_copy(oclsTb[0:DB, bass.ds(2 * t, 2)], aux[s][0:DB, 258:260]).then_inc(S("cls_osb"), 1)
                    dve.wait_ge(S("at1_proj"), v)
                    tt(h3[s][:], small[s][:, 0:D], h2[s][:], ALU.add).then_inc(S("h3_ready"), 1)
                    yield
                    yield from experts_in(s, v, 128, t)
                for _ in zip(tile(0), tile(1)):
                    pass
                for s in range(2):
                    dve.wait_ge(step, noted("chosen", s))
                    dve.wait_ge(S("sums"), 2 * i + s + 1)
                    tt(before_sum[:, 2 * i + s + 1, :], before_sum[:, 2 * i + s, :], chosen[:, 2 * i + s, :], ALU.add)\
                        .then_inc(S("sums"), 1)

            assert seen["n"] == STEPS, seen["n"]
            seen.update(base=STEPS * (TILES // 2) + start, n=0)
            dve.wait_ge(S("at1_proj"), NT)
            tt(h3[0][0:B, :], small[0][0:B, 0:D], cls_row[:], ALU.add).then_inc(S("h3_ready"), 1)
            for _ in experts_in(0, NT, B, TILES):
                pass
            dve.wait_ge(step, noted("chosen", 0))
            dve.wait_ge(S("sums"), NT)
            V.memset(best[0][0:1, 0:1], 0.0).then_inc(S("chosen_all"), 1)

            for t in range(NT):
                rows = 128 if t < TILES else B
                dve.wait_ge(S("slots_mm"), t + 1)
                stt(slot[0:rows, t, 0:E], big[t % 2][0:rows, 0, 0:E], 1.0, chosen[0:rows, t, :], ALU.add, ALU.mult)\
                    .then_inc(S("slots_done"), 1)
            dve.wait_ge(S("slots_done"), NT)
            ts(slot[:, 0:TILES, 0:E], slot[:, 0:TILES, 0:E], -1.0, None, op0=ALU.add)
            ts(slot[0:B, TILES, 0:E], slot[0:B, TILES, 0:E], -1.0, None, op0=ALU.add).then_inc(S("slots_ready"), 1)
            dve.wait_ge(S("count_mm"), 1)
            ts(active_f[:], small[1][:, 0:1], 0.0, None, op0=ALU.is_gt).then_inc(S("active_f"), 1)
            dve.wait_ge(S("active_f"), 1)
            V.tensor_copy(active[:], active_f[:]).then_inc(S("active_ready"), 1)
            dve.wait_ge(S("rank_mm"), 1)
            V.tensor_copy(rank[:], small[0][:, 0:1]).then_inc(S("rank_ready"), 1)
            dve.wait_ge(S("rank_ready"), 1)
            ts(pick[:], iota_f[:, 0:LIST], rank[:], active_f[:], op0=ALU.is_equal, op1=ALU.mult).then_inc(S("pick_ready"), 1)
            dve.wait_ge(S("list_mm"), 1)
            ts(lists[:, 0:LIST], aux[1][0:1, 0:LIST], float(E), None, op0=ALU.add)
            V.tensor_copy(lists[:, LIST:2 * LIST], aux[1][0:1, LIST:2 * LIST])
            ts(lists[:, 2 * LIST:2 * LIST + 1], aux[1][0:1, 2 * LIST:2 * LIST + 1], 0.5, 0.25, op0=ALU.mult, op1=ALU.add)\
                .then_inc(S("list_ready"), 1)

            def slots_of(j, s):
                e = dve.value_load(lists[0:1, bass.ds(j, 1)] if not isinstance(j, int) else lists[0:1, j:j + 1],
                                   min_val=0, max_val=E)
                tt(hot[s][:], iota_f[:, None, 0:CAP].to_broadcast([128, NT, CAP]),
                   slot[:, :, bass.ds(e, 1)].to_broadcast([128, NT, CAP]), ALU.is_equal)
                V.tensor_copy(rhs[s][:, :, 3:6], wsplit[:, :, bass.ds(e, 1), :].squeeze(2)).then_inc(S("hot_ready"), 1)

            def indices_of(s, v):
                dve.wait_ge(S("index_mm"), v)
                p = aux[s][0:HS, 0:12].rearrange("p (h c) -> p h c", c=6)
                stt(slot_a[s][:].unsqueeze(2), p[:, :, 2:3], 1.0, dummy_f[:].unsqueeze(2), ALU.subtract, ALU.mult)
                V.reduce_sum(slot_w[s][:].unsqueeze(2), p[:, :, 3:6], axis=AX.X)
                V.tensor_copy(slot_b[s][:].unsqueeze(2), p[:, :, 1:2]).then_inc(S("index_a"), 1)
                dve.wait_ge(S("index_a"), v)
                tt(slot_a[s][:], slot_a[s][:], slot_b[s][:], ALU.add).then_inc(S("index_b"), 1)
                dve.wait_ge(S("index_b"), v)
                stt(index[s][:].unsqueeze(2), p[:, :, 0:1], 64.0, slot_a[s][:].unsqueeze(2), ALU.mult, ALU.add)\
                    .then_inc(S("index_ready"), 1)

            dve.wait_ge(S("list_ready"), 1)
            dve.wait_ge(S("slots_ready"), 1)
            n2 = dve.value_load(lists[0:1, 2 * LIST:2 * LIST + 1], min_val=1, max_val=E // 2)
            for r in range(2):
                dve.sem_inc(S(f"einner{r}"), 1)
            dve.sem_inc(S("y_done"), 2)
            slots_of(0, 0)
            slots_of(1, 1)
            indices_of(0, 1)
            with dve.Fori(0, n2) as i:
                for s in range(2):
                    v = 2 * i + s + 1
                    indices_of(1 - s, v + 1)
                    for r in range(2):
                        g, u = (big[r][0:SC, b, 0:2 * CAP] for b in range(2))
                        dve.wait_ge(S(f"eth{r}"), v)
                        stt(eth[r][:], eth[r][:], 1.0, g, ALU.add, ALU.mult).then_inc(S(f"esilu{r}"), 1)
                        dve.wait_ge(S(f"esilu{r}"), v)
                        if r == 0:
                            dve.wait_ge(S("down_mm"), v)
                        tt(einner[s][:, 2 * r:2 * r + 2, :].rearrange("p c n -> p (c n)"), eth[r][:], u, ALU.mult)\
                            .then_inc(S(f"einner{r}"), 1)
                    slots_of(2 * i + s + 2, s)
                    dve.wait_ge(S("add_done"), v)
                    V.tensor_copy(add_index[s][:], index[s][:])
                    dve.wait_ge(S("down_mm"), v + 2)
                    for h in range(2):
                        last = ts(y[s][:, h, :], aux[s][0:HS, 64 + h * D:64 + (h + 1) * D], slot_w[s][:, h:h + 1], 0.5,
                                  op0=ALU.mult, op1=ALU.mult)
                    last.then_inc(S("y_done"), 1)

        @block.gpsimd
        def _(pool):
            G = nc.gpsimd
            with pool.Fori(0, TILES // 2) as i:
                for s in range(2):
                    v = 2 * i + s + 1
                    by_head = "p (h k) -> p h k"
                    pool.wait_ge(S("top_max"), v)
                    G.tensor_tensor(att[s][:].rearrange(by_head, k=NKEY), sc_sb[s][:].rearrange(by_head, k=NKEY),
                                    top_a[s][:].rearrange("p (h e) -> p h e", e=8)[:, :, 0:1].to_broadcast([128, NH + 1, NKEY]),
                                    ALU.subtract).then_inc(S("at1_sub"), 1)

            def gather(s, v):
                hold(pool, S("index_ready"), v)
                for h in range(2):
                    G.indirect_dma_start(xg[s][:, h, :], None, x_rows[:, :],
                                         bass.IndirectOffsetOnAxis(index[s][:, h:h + 1], 0)).then_inc(S(f"gathered{s}"), 16)

            pool.wait_ge(S("rows_ready"), 1)
            pool.wait_ge(S("list_ready"), 1)
            n2 = pool.value_load(lists[0:1, 2 * LIST:2 * LIST + 1], min_val=1, max_val=E // 2)
            gather(0, 1)
            pool.sem_inc(S("add_done"), 2)
            with pool.Fori(0, n2) as i:
                for s in range(2):
                    v = 2 * i + s + 1
                    gather(1 - s, v + 1)
                    hold(pool, S("y_done"), v + 2)
                    for h in range(2):
                        G.indirect_dma_start(out[:, :], bass.IndirectOffsetOnAxis(add_index[s][:, h:h + 1], 0),
                                             y[s][:, h, :], None, compute_op=ALU.add).then_inc(S("added"), 16)
                    pool.wait_ge(S("added"), 64 * i + 32 * s + 32)
                    pool.sem_inc(S("add_done"), 1)


def _host_constants():
    import numpy as np
    f = np.float32
    p = np.arange(128)
    pos = np.arange(NP, dtype=f)[:, None]
    ang = pos / np.power(f(10000.0), f(2.0) * np.arange(D // 2, dtype=f)[None, :] / f(D)).astype(f)
    pe = np.zeros((NP, D), f)
    pe[:, 0::2], pe[:, 1::2] = np.sin(ang), np.cos(ang)
    mask_q = np.zeros((128, HB, 64), f)
    for m in range(HB):
        for j in range(4):
            mask_q[32 * j:32 * j + DH, m, 4 * m + j] = 1
    mask_o = np.zeros((128, NH, DH), f)
    for g in range(2):
        for h in range(NH):
            mask_o[64 * g + h, h] = 1
    tile = np.arange(TILES)
    img = 2 * tile[None, :] + (p // 64)[:, None]
    tok = np.zeros((128, NT), np.int64)
    tok[:, :TILES] = img * NKEY + 1 + (p % 64)[:, None]
    tok[:B, TILES] = np.arange(B) * NKEY
    tok = np.stack([tok // 64, tok % 64, np.ones_like(tok)], -1).astype(f).reshape(128, NT * 3)
    return {
        "ident": np.eye(128, dtype=f), "pe": np.concatenate([pe, pe]), "mask_q": mask_q,
        "mask_o": mask_o.reshape(128, D), "img_sel": (p[:, None] // 64 == np.arange(2)).astype(f),
        "before": (p[:, None] < p[None, :]).astype(f),
        "cls_before": (np.arange(B)[:, None, None] <= img.T[None]).astype(f).reshape(B, TILES * 128),
        "pat_before": (img[:, :, None] < np.arange(B)).astype(f).reshape(128, TILES * B),
        "iota": np.tile(np.arange(CAP, dtype=f), (128, 1)), "tok": tok,
        "dummy": -(DUMMY + np.arange(HS)[:, None] + HS * np.arange(2)[None, :]).astype(f),
        "evals": np.stack([p - E, p], -1).astype(f),
    }


def kernel(**inputs):
    import numpy as np
    import concourse.bacc as bacc
    from concourse.bass_utils import run_bass_kernel_spmd

    x = {k: np.ascontiguousarray(v) for k, v in inputs.items()}
    heads = np.arange(HB * 4).reshape(HB, 4, 1) * DH + np.arange(32)
    cols = np.concatenate([heads.reshape(-1), D + heads.reshape(-1)])
    n = IMG // PATCH
    patches = x["x"].reshape(TILES, 2, C, n, PATCH, n, PATCH).transpose(0, 2, 4, 6, 1, 3, 5)
    t, at, m = "L0_tok_", "L0_attn_", "L0_ffn_"
    arrays = {
        "xp": patches.reshape(TILES, KC, 128, 128).transpose(0, 2, 1, 3), "cls": x["cls_tok"].reshape(D),
        "patch_w": x[t + "patch_w"].reshape(D, KC, 128).transpose(2, 1, 0), "patch_b": x[t + "patch_b"],
        "ln_g": x[t + "ln_g"], "ln_b": x[t + "ln_b"],
        "ff1_w": x[t + "ff1_w"], "ff1_b": x[t + "ff1_b"], "ff2_w": x[t + "ff2_w"], "ff2_b": x[t + "ff2_b"],
        "wqk1": x[t + "qkv_w"][:, cols], "bqk1": x[t + "qkv_b"][cols],
        "wv1": x[t + "qkv_w"][:, 2 * D:], "bv1": x[t + "qkv_b"][2 * D:],
        "proj1_w": x[t + "proj_w"], "proj1_b": x[t + "proj_b"],
        "wqk2": x[at + "W_qkv"][:, cols], "bqk2": x[at + "b_qkv"][cols],
        "wv2": x[at + "W_qkv"][:, 2 * D:], "bv2": x[at + "b_qkv"][2 * D:],
        "proj2_w": x[at + "W_proj"], "proj2_b": x[at + "b_proj"],
        "wgT": x[m + "Wg"].T, "e_bias": x[m + "e_bias"],
        "w_gate_up": x[m + "W_gate_up"], "w_down": x[m + "W_down"],
        "wsg": x[m + "Wsg"], "wsu": x[m + "Wsu"], "wsd": x[m + "Wsd"],
        **_host_constants(),
    }
    nc = bacc.Bacc("TRN2", target_bir_lowering=False, num_devices=1)
    f32 = mybir.dt.float32
    arrays = {"in_" + k: np.ascontiguousarray(v) for k, v in arrays.items()}
    aps = {k[3:]: nc.dram_tensor(k, v.shape, f32, kind="ExternalInput").ap() for k, v in arrays.items()}
    out = nc.dram_tensor("out_rows", (ROWS, D), f32, kind="ExternalOutput").ap()
    tower_kernel(nc, aps, out)
    r = run_bass_kernel_spmd(nc, [arrays], core_ids=[0])
    return r.results[0]["out_rows"][0:T].reshape(B, NKEY, D)
```

```python
import concourse.bass as bass
from concourse import mybir
from contextlib import ExitStack

B, C, IMG, PATCH = 32, 3, 128, 16
D = 192
NP = (IMG // PATCH) ** 2
NKEY = NP + 1
T = B * NKEY
NH, DH = 12, 16
F = 768
TOP_KEYS = int(0.4 * NKEY)
E, TOPE, CAP = 128, 6, 192
I = 464
IS = 928
TILES = B * NP // 128
KC = C * PATCH * PATCH // 128
DA, DB = 128, D - 128
FC = F // 128
HB = NH // 4
VD = DH + 1
SC = 116
NSC, NIC = IS // SC, I // SC
EK = D // 2
HS = CAP // 2
NT = TILES + 1
DUMMY = T
ROWS = T + CAP
STEPS = 74
LIST = E + 4


PATCHES = dict(patch=2.6, ln0=4.2)
FIRST = dict(pe=.4, h0T=.5, h0c=.7, up0=2.8, sq0=1, poly0=1.2, th0=1, hid0=1.2, down0=2.2, y=.5,
             yT=.5, yc=.7, qkv0=4, qc0=1.4, s0=2.8, max0=1.2, sub0=1.5, exp0=1.2, T0a=1.9, c0a=1.2, T0b=1, c0b=.7,
             o0=2.8, norm0=1.2, oT0=.5, oc0=.7, proj0=.8, h1=.5, h1T=.5, h1c=.7,
             up1=2.8, sq1=1, poly1=1.2, th1=1, hid1=1.2, down1=2.2, h2=.5)
SECOND = dict(ln2=4, n2T=.5, n2c=.7, qkv1=4, qc1=2, s1=3.8, sc1=1.4, top0=1.8, sub1=.1, cut0=1.8, exp1=.1, top1=1.8,
              cut1=1.8, top2=1.8, cut2=1.8, top3=1.8, mask=2, T1a=2, c1a=1.4, T1b=1.2, c1b=1, o1=3.8, norm1=1.5,
              oT1=.5, oc1=.7, proj1=.8, h3=.5)
THIRD = dict(ln3=4, xT=.5, xc=.7, logits=.5, router=.1)
for r in range(4):
    THIRD.update({f"sh_up{r}": 1.8, f"sh_th{r}": .4, f"sh_in{r}": 1.2})
THIRD.update(down=2.6, acc=.5)


def _starts(*stages):
    starts = {}
    for stage, at in stages:
        for step, lasts in stage.items():
            starts[step] = at
            at += lasts
    return starts


STARTS = _starts((PATCHES, 32.0), (FIRST, 0.0), (SECOND, 0.0), (THIRD, 0.0))


def interleave(*stages):
    clocks = {stage: STARTS[next(stage)] for stage in stages}
    while clocks:
        stage = min(clocks, key=clocks.get)
        try:
            step = next(stage)
        except StopIteration:
            del clocks[stage]
            continue
        clocks[stage] = STARTS[step] if step else clocks[stage] + 0.2


def run(stage):
    for _ in stage:
        pass

SEMAPHORES = """
    zero_rows x_stored acc_stored patch_mm xm_ready acc_ready cls_stored rows_ready list_ready
    eup1 down_mm w_loaded0 w_loaded1 h0_ready h0_T ff0_xT ff0_up ff0_hid ff0_down y_ready y_T
    at0_xT at0_qk at0_v at0_k_sb at0_qk_sb at0_s at0_p held at0_T0 at0_aT0 at0_T1 at0_aT1 at0_o
    patch_taken at0_osb at0_oT at0_oxT at0_proj h1_ready h1_T ff1_xT ff1_up ff1_hid ff1_down
    n2_ready n2_T at1_xT at1_qk at1_v at1_k_sb at1_qk_sb at1_s at1_p at1_T0 at1_aT0 at1_T1
    at1_aT1 at1_o at1_osb at1_oT cls_oT at1_oxT at1_proj xm_T xm_xT logits sh_up sh_inner
    sig_exp sh_down h3_ready chosen_all slots_mm slots_done count_mm active_ready rank_mm
    pick_ready list_mm hot_ready index_mm gathered0 xe_T xeT_ready einner0 eup0 einner1
    gathered1 y_done ff0_sq ff0_poly ff0_th at0_v_sb at0_sub ff1_sq ff1_poly ff1_th at1_v_sb
    at1_s_sb at1_sub at1_exp sh_th eth0 eth1 step sums memsets patches_ready h2_ready h2_taken
    top_max h3_taken slots_ready active_f rank_ready pairs_counted index_a index_b index_ready
    esilu0 esilu1 add_done kept added
"""


def tower_kernel(nc, a, out):
    f32, bf16, i32 = mybir.dt.float32, mybir.dt.bfloat16, mybir.dt.int32
    ALU, ACT, AX = mybir.AluOpType, mybir.ActivationFunctionType, mybir.AxisListType

    ctx = ExitStack()
    with ctx:
        def sb(name, shape, dt=f32):
            return ctx.enter_context(nc.sbuf_tensor("b_" + name, shape, dt))

        def two(name, shape, dt=f32):
            return [sb(f"{name}{s}", shape, dt) for s in range(2)]

        def each(name, shape):
            return [sb(f"{name}{s}", shape) for s in range(4)]

        def of(stages, name, shape, dt=f32):
            return {s: sb(f"{name}{s}", shape, dt) for s in stages}

        arena = [sb(f"arena{s}", [128, 5760]) for s in range(2)]

        def carve(start, rows, *dims, dt=f32):
            n = 1
            for d in dims:
                n *= d
            n = n if dt == f32 else n // 2
            views = [x[0:rows, start:start + n] for x in arena]
            if dt != f32:
                views = [x.bitcast(dt) for x in views]
            if len(dims) == 2:
                views = [x.rearrange("p (a b) -> p a b", b=dims[1]) for x in views]
            return views, start + n

        def pb(name, shape, dt=f32):
            return ctx.enter_context(nc.psum_tensor("p_" + name, shape, dt))

        def sem(name):
            return ctx.enter_context(nc.semaphore("s_" + name))

        ident = sb("ident", [128, 128])
        patch_w = sb("patch_w", [128, KC, D])
        patch_b = sb("patch_b", [128, D])
        ln_g = sb("ln_g", [128, D])
        ln_b = sb("ln_b", [128, D])
        pe_sb = sb("pe", [128, D])
        ff1a, ff1b = sb("ff1a", [DA, F]), sb("ff1b", [DB + 1, F])
        ff2 = sb("ff2", [128, FC, D])
        ff2_b = sb("ff2_b", [128, D])
        wqk = [(sb(f"wqk{n}a", [DA, 2 * HB * 128]), sb(f"wqk{n}b", [DB + 1, 2 * HB * 128])) for n in range(2)]
        wv = [(sb(f"wv{n}a", [DA, D]), sb(f"wv{n}b", [DB + 1, D])) for n in range(2)]
        wo = [(sb(f"wo{n}a", [DA, D]), sb(f"wo{n}b", [DB + 1, D])) for n in range(2)]
        wg_a, wg_b = sb("wg_a", [DA, E]), sb("wg_b", [DB, E])
        e_bias = sb("e_bias", [128, E])
        wsga, wsgb = sb("wsga", [DA, IS]), sb("wsgb", [DB, IS])
        wsua, wsub = sb("wsua", [DA, IS]), sb("wsub", [DB, IS])
        wsd = sb("wsd", [SC, NSC, D])
        cls_row = sb("cls_row", [B, D])
        mask_q = sb("mask_q", [128, HB, 64])
        mask_o = sb("mask_o", [128, D])
        img_sel = sb("img_sel", [128, 2])
        zrows = sb("zrows", [CAP // 2, 2 * D])
        before_f = sb("before_f", [128, 128])
        cls_before_f = arena[0][0:B, 0:TILES * 128]
        pat_before_f = arena[1][:, 0:TILES * B]
        iota_f = sb("iota_f", [128, CAP])
        tok_f = sb("tok_f", [128, NT * 3])
        dummy_f = sb("dummy_f", [HS, 2])
        eval_f = sb("eval_f", [128, 2])
        before = sb("before", [128, 128], bf16)
        cls_before = sb("cls_before", [B, TILES * 128], bf16)
        pat_before = sb("pat_before", [128, TILES * B], bf16)
        ones = sb("ones", [128, 128], bf16)
        eval_b = sb("eval_b", [128, 2], bf16)

        xp = sb("xp", [128, KC, 128])
        patch_x, patch_n = sb("patch_x", [128, D]), sb("patch_n", [128, D])
        h0, h1, h1_bias, norm = (sb(n, [128, D]) for n in ("h0", "h1", "h1_bias", "norm"))
        h2, h2_kept, norm2 = (sb(n, [128, D]) for n in ("h2", "h2_kept", "norm2"))
        norm0 = sb("norm0", [128, D])
        h3, h3_kept, xm, acc = (sb(n, [128, D]) for n in ("h3", "h3_kept", "xm", "acc"))
        stat, mv, rstd = each("stat", [128, 6]), each("mv", [128, 2]), each("rstd", [128, 1])
        var, newton = each("var", [128, 1]), each("newton", [128, 1])
        xTa, xTb = of(range(3), "xTa", [DA, 128]), of(range(3), "xTb", [DB + 1, 128])
        sq, hid = sb("sq", [128, F]), sb("hid", [128, F])
        qT = of(range(2), "qT", [128, HB, 128])
        kT2 = sb("kT2", [128, HB, 2, NKEY])
        vv = {0: sb("v0", [NP, 2, NH, VD]), 1: sb("v1", [NKEY, 2, NH, VD])}
        o_sb = of(range(2), "o_sb", [128, D])
        oc_sb = sb("oc_sb", [128, D])
        rr, rc = of(range(2), "rr", [128, NH]), sb("rc", [128, 1])
        mx = sb("mx", [128, NH])
        att0, at = carve(0, 128, NH * NP)
        aT0, at = carve(at, NP, NH, 128)
        k_blk0, at = carve(at, 128, HB * 2, 4 * NP)
        att1, at = carve(0, 128, (NH + 1) * NKEY)
        sc_sb, at = carve(at, 128, (NH + 1) * NKEY)
        work, at = carve(at, 128, (NH + 1) * NKEY)
        aT1, at = carve(at, NKEY, NH + 1, 128)
        k_blk1, at = carve(at, 128, HB * 2, 4 * NKEY)
        assert at <= 5760
        att, aT, sc_sb, work = {0: att0[0], 1: att1[1]}, {0: aT0[0], 1: aT1[1]}, sc_sb[1], work[1]
        k_blk = {n: x.rearrange("p (m g) (j k) -> p m g j k", g=2, j=4) for n, x in ((0, k_blk0[0]), (1, k_blk1[1]))}
        top_a, top_b, top_c, top_d = (sb(f"top_{n}", [128, (NH + 1) * 8]) for n in "abcd")
        sig, wtok = sb("sig", [128, E]), sb("wtok", [128, E])
        choice, picked = sb("choice", [128, E + 2]), sb("picked", [128, E + 2])
        best, wsum, wres = sb("best", [128, 8]), sb("wsum", [128, 1]), sb("wres", [128, E])
        th, inner_buf = sb("th", [SC, 2, 128]), sb("inner", [128, NSC * 128])
        inner = inner_buf[0:SC, :].rearrange("p (c t) -> p c t", t=128)

        oclsTa, oclsTb = sb("oclsTa", [DA, B]), sb("oclsTb", [DB + 1, B])
        cxTa, cxTb = sb("cxTa", [DA, B]), sb("cxTb", [DB + 1, B])
        qcls = sb("qcls", [128, HB])
        qcls_blk = sb("qcls_blk", [128, HB, 64])
        v_cls = sb("v_cls", [NKEY, D])

        chosen = sb("chosen", [128, NT, E], bf16)
        before_sum = sb("before_sum", [128, NT, E], bf16)
        wsplit = sb("wsplit", [128, NT, E + 1, 3], bf16)
        slot = sb("slot", [128, NT, E + 1], bf16)
        counts, active_f = sb("counts", [128, 1]), sb("active_f", [128, 1])
        active = sb("active", [128, 1], bf16)
        rank, pick = sb("rank", [128, 1]), sb("pick", [128, LIST], bf16)
        lists = sb("lists", [1, 2 * LIST + 2], i32)
        n_pairs = sb("n_pairs", [1, 1])

        hot, at = carve(0, 128, NT, CAP, dt=bf16)
        rhs = two("rhs", [128, NT, 6], bf16)
        slot_a, slot_b = two("slot_a", [HS, 2]), two("slot_b", [HS, 2])
        slot_w, add_w = two("slot_w", [HS, 2]), two("add_w", [HS, 2])
        index, add_index = two("index", [HS, 2], i32), two("add_index", [HS, 2], i32)
        xeT = two("xeT", [EK, 2, CAP])
        w_gu, at = carve(at, EK, 2, 2 * I)
        w_dn, at = carve(at, SC, NIC, D)
        xg, at = carve(at, HS, 2, D)
        einner, at = carve(at, SC, NIC, CAP)
        assert at <= 5760
        eth = [hid[0:SC, 0:2 * CAP], inner_buf[0:SC, 0:2 * CAP]]
        y = [x[0:HS, 384:384 + 2 * D].rearrange("p (h d) -> p h d", d=D) for x in (hid, inner_buf)]

        big = [pb(f"big{s}", [128, 2, 512]) for s in range(2)]
        small = [pb(f"small{s}", [128, 512]) for s in range(3)]
        sh_bank = pb("shared", [128, 512])
        aux = [small[2], sh_bank]

        x_rows = nc.dram_tensor("x_rows", [ROWS, D], f32).ap()
        x_img = x_rows[0:T, :].rearrange("(b q) d -> b q d", q=NKEY)
        out_img = out[0:T, :].rearrange("(b q) d -> b q d", q=NKEY)

        consts = sem("consts")
        cls_loads = sem("cls_loads")
        xp_loaded = sem("xp_loaded")
        presets = sem("presets")
        acts_preset = sem("acts_preset")
        cls_norm = sem("cls_norm")
        cls_T, cls_xT, cls_qk, cls_q, cls_v, cls_ready = (sem("cls_" + n) for n in ("T", "xT", "qk", "q", "v", "ready"))
        named = {name: sem(name) for name in SEMAPHORES.split()}

        def S(name):
            return named[name]

        def hold(eng, semaphore, value):
            eng.wait_ge(semaphore, value)
            eng.sem_inc(S("held"), 1)

        def halves(w, n):
            return [(w[0][:], n[0:DA, :]), (w[1][0:DB, :], n[DA:D, :])]

        def row(w, bias):
            return [(w[1][DB:DB + 1, :], bias.partition_broadcast(1))]

        def everywhere(v, n=128):
            return v.partition_broadcast(n)

        first_loads = [(ident[:], a["ident"]), (cls_row[:], everywhere(a["cls"], B)),
                       (mask_q[:], a["mask_q"]),
                       *halves(wqk[1], a["wqk2"]), *row(wqk[1], a["bqk2"]),
                       *halves(wv[1], a["wv2"]), *row(wv[1], a["bv2"])]
        loads = [(patch_w[:], a["patch_w"]), (patch_b[:], everywhere(a["patch_b"])),
                 (ln_g[:], everywhere(a["ln_g"])), (ln_b[:], everywhere(a["ln_b"])), (pe_sb[:], a["pe"]),
                 *halves((ff1a, ff1b), a["ff1_w"]), *row((ff1a, ff1b), a["ff1_b"]),
                 (ff2[:], a["ff2_w"].rearrange("(c p) d -> p c d", p=128)), (ff2_b[:], everywhere(a["ff2_b"])),
                 *halves(wqk[0], a["wqk1"]), *row(wqk[0], a["bqk1"]),
                 *halves(wv[0], a["wv1"]), *row(wv[0], a["bv1"]),
                 *halves(wo[0], a["proj1_w"]), *row(wo[0], a["proj1_b"]),
                 *halves(wo[1], a["proj2_w"]), *row(wo[1], a["proj2_b"]),
                 (wg_a[:], a["wgT"][0:DA, :]), (wg_b[:], a["wgT"][DA:D, :]), (e_bias[:], everywhere(a["e_bias"])),
                 (wsga[:], a["wsg"][0:DA, :]), (wsgb[:], a["wsg"][DA:D, :]),
                 (wsua[:], a["wsu"][0:DA, :]), (wsub[:], a["wsu"][DA:D, :]),
                 (wsd[:], a["wsd"].rearrange("(c p) d -> p c d", p=SC)),
                 (mask_o[:], a["mask_o"]), (img_sel[:], a["img_sel"]),
                 (before_f[:], a["before"]), (cls_before_f, a["cls_before"]), (pat_before_f, a["pat_before"]),
                 (iota_f[:], a["iota"]), (tok_f[:], a["tok"]), (dummy_f[:], a["dummy"]), (eval_f[:], a["evals"])]
        N_FIRST, N_CONST = 16 * len(first_loads), 16 * len(loads)

        block = ctx.enter_context(nc.Block())

        def s1_scores():
            return big[0][:, :, 0:6 * NP].rearrange("p b (h k) -> p b h k", k=NP)

        def k_psum(s):
            return big[s][:, 1, 0:384].rearrange("p (m g t) -> p m g t", g=2, t=NP)

        @block.sync
        def _(sp):
            for dst, src in first_loads:
                sp.dma_start(dst, src).then_inc(cls_loads, 16)
            sp.dma_start(xp[:], a["xp"][0]).then_inc(xp_loaded, 16)
            for dst, src in loads:
                sp.dma_start(dst, src).then_inc(consts, 16)
            sp.wait_ge(presets, 1)
            sp.dma_start(x_rows[T:ROWS, :].rearrange("(p r) d -> p (r d)", r=2), zrows[:]).then_inc(S("zero_rows"), 16)
            sp.dma_start(out[T:ROWS, :].rearrange("(p r) d -> p (r d)", r=2), zrows[:]).then_inc(S("zero_rows"), 16)
            for store in ("x_stored", "acc_stored"):
                sp.sem_inc(S(store), 32)

            def load(v):
                sp.wait_ge(S("patch_mm"), v - 1)
                sp.dma_start(xp[:], a["xp"][v - 1]).then_inc(xp_loaded, 16)

            def store_x(v):
                sp.wait_ge(S("xm_ready"), v)
                for g in range(2):
                    sp.dma_start(x_img[2 * v - 2 + g, 1:NKEY, :], xm[64 * g:64 * g + 64, :]).then_inc(S("x_stored"), 16)

            def store_acc(v):
                sp.wait_ge(S("acc_ready"), v)
                for g in range(2):
                    sp.dma_start(out_img[2 * v - 2 + g, 1:NKEY, :], acc[64 * g:64 * g + 64, :]).then_inc(S("acc_stored"), 16)

            for v in range(2, 5):
                load(v)
            with sp.Fori(0, TILES - 4) as k:
                store_x(k + 1)
                store_acc(k + 1)
                load(k + 5)
            for v in range(TILES - 3, TILES + 1):
                store_x(v)
                store_acc(v)
            sp.wait_ge(S("x_stored"), 32 * TILES + 32)
            sp.wait_ge(S("acc_stored"), 32 * TILES + 32)
            sp.wait_ge(S("xm_ready"), NT)
            sp.dma_start(x_img[:, 0, :], xm[0:B, :]).then_inc(S("cls_stored"), 16)
            sp.wait_ge(S("acc_ready"), NT)
            sp.dma_start(out_img[:, 0, :], acc[0:B, :]).then_inc(S("cls_stored"), 16)
            sp.wait_ge(S("cls_stored"), 32)
            sp.wait_ge(S("zero_rows"), 32)
            sp.sem_inc(S("rows_ready"), 1)

            sp.wait_ge(S("list_ready"), 1)
            n2 = sp.value_load(lists[0:1, 2 * LIST:2 * LIST + 1], min_val=1, max_val=E // 2)
            sp.sem_inc(S("eup1"), 2)
            sp.sem_inc(S("down_mm"), 2)
            with sp.Fori(0, n2) as i:
                for s in range(2):
                    e = sp.value_load(lists[0:1, bass.ds(LIST + 2 * i + s, 1)], min_val=0, max_val=E - 1)
                    gu = a["w_gate_up"][e].rearrange("(k p) f -> p k f", p=EK)
                    dn = a["w_down"][e].rearrange("(c p) d -> p c d", p=SC)
                    sp.wait_ge(S("eup1"), 2 * i + s + 1)
                    sp.dma_start(w_gu[s][:], gu).then_inc(S(f"w_loaded{s}"), 16)
                    sp.wait_ge(S("down_mm"), 2 * i + s + 1)
                    sp.dma_start(w_dn[s][0:112], dn[0:112]).then_inc(S(f"w_loaded{s}"), 16)
                    sp.dma_start(w_dn[s][112:SC], dn[112:SC]).then_inc(S(f"w_loaded{s}"), 16)

        @block.tensor
        def _(pe):
            mm, tr = nc.tensor.matmul, nc.tensor.transpose

            def to_features(src, s, rows, done):
                tr(small[s][0:DA, 0:rows], src[0:rows, 0:DA], ident[0:rows, 0:rows])
                tr(small[s][0:DB, 128:128 + rows], src[0:rows, DA:D], ident[0:rows, 0:rows]).then_inc(done, 1)

            def ff(s, v, n):
                yield f"up{n}"
                pe.wait_ge(S(f"ff{n}_xT"), v)
                for c in range(FC):
                    o = big[s][:, c // 3, (c % 3) * 128:(c % 3 + 1) * 128]
                    mm(o, ff1a[:, c * 128:(c + 1) * 128], xTa[s][:], start=True, stop=False)
                    last = mm(o, ff1b[:, c * 128:(c + 1) * 128], xTb[s][:], start=False, stop=True)
                last.then_inc(S(f"ff{n}_up"), 1)
                yield f"down{n}"
                pe.wait_ge(S(f"ff{n}_hid"), v)
                for c in range(FC):
                    last = mm(small[s][:, 0:D], hid[:, c * 128:(c + 1) * 128], ff2[:, c, :],
                              start=(c == 0), stop=(c == FC - 1))
                last.then_inc(S(f"ff{n}_down"), 1)

            def qkv(s, v, n):
                yield f"qkv{n}"
                pe.wait_ge(S(f"at{n}_xT"), v)
                for m in range(2 * HB):
                    o = big[s][:, m // HB, (m % HB) * 128:(m % HB + 1) * 128]
                    mm(o, wqk[n][0][:, m * 128:(m + 1) * 128], xTa[s][:], start=True, stop=False)
                    last = mm(o, wqk[n][1][:, m * 128:(m + 1) * 128], xTb[s][:], start=False, stop=True)
                last.then_inc(S(f"at{n}_qk"), 1)
                for g in range(2):
                    o = small[s][0:NP, g * D:(g + 1) * D]
                    mm(o, xTa[s][:, 64 * g:64 * g + 64], wv[n][0][:], start=True, stop=False)
                    last = mm(o, xTb[s][:, 64 * g:64 * g + 64], wv[n][1][:], start=False, stop=True)
                last.then_inc(S(f"at{n}_v"), 1)

            def scores(s, v, n):
                yield f"s{n}"
                keys, per_bank = ((NP, 6), (NKEY, 7))[n]
                pe.wait_ge(S(f"at{n}_k_sb"), v)
                pe.wait_ge(S(f"at{n}_qk_sb"), v)
                for g in range(2):
                    rows = slice(64 * g, 64 * g + 64)
                    for m in range(HB):
                        cut = min(max(per_bank - 4 * m, 0), 4)
                        for lo, hi in ((0, cut), (cut, 4)):
                            if lo < hi:
                                h = 4 * m + lo
                                at = (h % per_bank) * keys
                                last = mm(big[s][rows, h // per_bank, at:at + (hi - lo) * keys],
                                          qT[s][:, m, rows], k_blk[s][:, m, g, lo:hi, 0:keys], start=True, stop=True)
                if n == 1:
                    at = (NH % per_bank) * keys
                    for g in range(2):
                        for m in range(HB):
                            last = mm(big[s][64 * g:64 * g + 64, 1, at:at + keys],
                                      qcls_blk[:, m, :], kT2[:, m, g, :], start=(m == 0), stop=(m == HB - 1))
                last.then_inc(S(f"at{n}_s"), 1)

            def weigh(s, v, n):
                keys, heads = ((NP, NH), (NKEY, NH + 1))[n]
                for part, (lo, hi) in enumerate(((0, 8), (8, heads))):
                    yield f"T{n}{'ab'[part]}"
                    hold(pe, S(f"at{n}_p") if part == 0 else S(f"at{n}_aT0"), v)
                    for h in range(lo, hi):
                        r = h - lo
                        last = tr(big[s][0:keys, r // 4, (r % 4) * 128:(r % 4 + 1) * 128],
                                  att[s][:, h * keys:(h + 1) * keys], ident[:])
                    last.then_inc(S(f"at{n}_T{part}"), 1)
                yield f"o{n}"
                v_sb = vv[n]
                hold(pe, S(f"at{n}_aT1"), v)
                for g in range(2):
                    rows = slice(64 * g, 64 * g + 64)
                    for h in range(NH):
                        last = mm(small[s][rows, h * VD:(h + 1) * VD], aT[s][0:keys, h, rows], v_sb[:, g, h, :],
                                  start=True, stop=True)
                    if n == 1:
                        last = mm(small[s][rows, NH * VD:2 * NH * VD], aT[s][0:keys, NH, rows],
                                  v_sb[:, g, :, :].rearrange("p h d -> p (h d)"), start=True, stop=True)
                last.then_inc(S(f"at{n}_o"), 1)
                yield f"oT{n}"
                pe.wait_ge(S(f"at{n}_osb"), v)
                to_features(o_sb[s], s, 128, S(f"at{n}_oT"))
                if n == 1:
                    mm(small[s][:, 256:258], oc_sb[:, 0:DA], img_sel[:], start=True, stop=True)
                    mm(small[s][0:DB, 258:260], oc_sb[:, DA:D], img_sel[:], start=True, stop=True).then_inc(S("cls_oT"), 1)

            def project(s, v, n, la, lb, rows, ready):
                yield f"proj{n}"
                pe.wait_ge(ready, v)
                mm(small[s][0:rows, 0:D], la, wo[n][0][:], start=True, stop=False)
                mm(small[s][0:rows, 0:D], lb, wo[n][1][:], start=False, stop=True).then_inc(S(f"at{n}_proj"), 1)

            def experts_in(s, v, rows):
                yield "xT"
                pe.wait_ge(S("xm_ready"), v)
                to_features(xm, s, rows, S("xm_T"))
                yield "logits"
                pe.wait_ge(S("xm_xT"), v)
                mm(small[s][0:rows, 256:256 + E], xTa[s][:, 0:rows], wg_a[:], start=True, stop=False)
                mm(small[s][0:rows, 256:256 + E], xTb[s][0:DB, 0:rows], wg_b[:], start=False, stop=True).then_inc(S("logits"), 1)
                for r in range(4):
                    yield f"sh_up{r}"
                    if not r:
                        pe.wait_ge(S("patch_taken"), min(v + 2, TILES) if isinstance(v, int) else v + 2)
                    if r:
                        pe.wait_ge(S("sh_inner"), 4 * v - 4 + r)
                    for n, (wa, wb) in enumerate(((wsga, wsgb), (wsua, wsub))):
                        for c in (2 * r, 2 * r + 1):
                            at = n * 256 + (c % 2) * 128
                            o = sh_bank[0:SC, at:at + rows]
                            mm(o, wa[:, c * SC:(c + 1) * SC], xTa[s][:, 0:rows], start=True, stop=False)
                            last = mm(o, wb[:, c * SC:(c + 1) * SC], xTb[s][0:DB, 0:rows], start=False, stop=True)
                    last.then_inc(S("sh_up"), 1)
                yield "down"
                pe.wait_ge(S("sh_inner"), 4 * v)
                pe.wait_ge(S("sig_exp"), v)
                for c in range(NSC):
                    last = mm(small[s][0:rows, 0:D], inner[:, c, 0:rows], wsd[:, c, :],
                              start=(c == 0), stop=(c == NSC - 1))
                last.then_inc(S("sh_down"), 1)

            pe.wait_ge(cls_loads, N_FIRST)
            pe.wait_ge(cls_norm, 1)
            tr(small[0][0:DA, 0:B], norm2[0:B, 0:DA], ident[0:B, 0:B])
            tr(small[0][0:DB, 128:128 + B], norm2[0:B, DA:D], ident[0:B, 0:B]).then_inc(cls_T, 1)
            pe.wait_ge(cls_xT, 1)
            for m in range(2 * HB):
                mm(small[1][:, m:m + 1], wqk[1][0][:, m * 128:(m + 1) * 128], cxTa[:, 0:1], start=True, stop=False)
                last = mm(small[1][:, m:m + 1], wqk[1][1][:, m * 128:(m + 1) * 128], cxTb[:, 0:1], start=False, stop=True)
            last.then_inc(cls_qk, 1)
            mm(small[2][NP:NKEY, 0:D], cxTa[:, 0:1], wv[1][0][:], start=True, stop=False)
            mm(small[2][NP:NKEY, 0:D], cxTb[:, 0:1], wv[1][1][:], start=False, stop=True).then_inc(cls_v, 1)
            pe.wait_ge(cls_ready, 1)
            pe.wait_ge(acts_preset, 1)
            pe.wait_ge(consts, N_CONST)

            def patches(v):
                yield "patch"
                pe.wait_ge(xp_loaded, 16 * v)
                if isinstance(v, int):
                    if v > 1:
                        pe.wait_ge(S("patch_taken"), v - 1)
                else:
                    pe.wait_ge(S("sh_inner"), 4 * v - 12)
                for c in range(KC):
                    last = mm(sh_bank[:, 0:D], xp[:, c, :], patch_w[:, c, :], start=(c == 0), stop=(c == KC - 1))
                last.then_inc(S("patch_mm"), 1)

            def first(v):
                yield "h0T"
                pe.wait_ge(S("h0_ready"), v)
                to_features(h0, 0, 128, S("h0_T"))
                yield from ff(0, v, 0)
                yield "yT"
                pe.wait_ge(S("y_ready"), v)
                to_features(norm, 0, 128, S("y_T"))
                yield from qkv(0, v, 0)
                yield from scores(0, v, 0)
                yield from weigh(0, v, 0)
                yield from project(0, v, 0, xTa[0][:], xTb[0][:], 128, S("at0_oxT"))
                yield "h1T"
                pe.wait_ge(S("h1_ready"), v)
                to_features(h1, 0, 128, S("h1_T"))
                yield from ff(0, v, 1)

            def second(v):
                yield "n2T"
                pe.wait_ge(S("n2_ready"), v)
                to_features(norm2, 1, 128, S("n2_T"))
                yield from qkv(1, v, 1)
                yield from scores(1, v, 1)
                yield from weigh(1, v, 1)
                yield from project(1, v, 1, xTa[1][:], xTb[1][:], 128, S("at1_oxT"))

            run(patches(1))
            interleave(first(1), patches(2))
            interleave(second(1), first(2), patches(3))
            with pe.Fori(0, TILES - 3) as k:
                interleave(experts_in(2, k + 1, 128), second(k + 2), first(k + 3), patches(k + 4))
            interleave(experts_in(2, TILES - 2, 128), second(TILES - 1), first(TILES))
            interleave(experts_in(2, TILES - 1, 128), second(TILES))
            interleave(experts_in(2, TILES, 128))

            pe.wait_ge(S("h3_ready"), TILES)
            run(project(1, TILES, 1, oclsTa[:], oclsTb[:], B, S("at1_oxT")))
            run(experts_in(2, NT, B))

            pe.wait_ge(S("chosen_all"), 1)
            for t in range(TILES):
                p = big[t % 2][:, 0, 0:E]
                if t >= 2:
                    pe.wait_ge(S("slots_done"), t - 1)
                mm(p, before[:], chosen[:, t, :], start=True, stop=False)
                mm(p, ones[:], before_sum[:, t, :], start=False, stop=False)
                mm(p, cls_before[:, t * 128:(t + 1) * 128], chosen[0:B, TILES, :], start=False, stop=True)\
                    .then_inc(S("slots_mm"), 1)
            pe.wait_ge(S("slots_done"), TILES - 1)
            for t in range(TILES):
                mm(big[0][0:B, 0, 0:E], pat_before[:, t * B:(t + 1) * B], chosen[:, t, :], start=(t == 0), stop=False)
            mm(big[0][0:B, 0, 0:E], before[0:B, 0:B], chosen[0:B, TILES, :], start=False, stop=True)\
                .then_inc(S("slots_mm"), 1)
            mm(small[1][:, 0:1], before_sum[:, TILES, :], ones[:, 0:1], start=True, stop=False)
            mm(small[1][:, 0:1], chosen[0:B, TILES, :], ones[0:B, 0:1], start=False, stop=True).then_inc(S("count_mm"), 1)
            pe.wait_ge(S("active_ready"), 1)
            mm(small[0][:, 0:1], before[:], active[:], start=True, stop=True).then_inc(S("rank_mm"), 1)
            pe.wait_ge(S("pick_ready"), 1)
            mm(aux[1][0:1, 0:LIST], eval_b[:, 0:1], pick[:], start=True, stop=True)
            mm(aux[1][0:1, LIST:2 * LIST], eval_b[:, 1:2], pick[:], start=True, stop=True)
            mm(aux[1][0:1, 2 * LIST:2 * LIST + LIST // 2], ones[:, 0:1], pick[:, 0:LIST:2], start=True, stop=True)\
                .then_inc(S("list_mm"), 1)

            def slots_of(s, v):
                pe.wait_ge(S("hot_ready"), v)
                for h in range(2):
                    for t in range(NT):
                        last = mm(small[s][0:HS, 400 + 6 * h:406 + 6 * h], hot[s][:, t, h * HS:(h + 1) * HS], rhs[s][:, t, :],
                                  start=(t == 0), stop=(t == NT - 1))
                last.then_inc(S("index_mm"), 1)

            def gathered(s, gather_value, v):
                pe.wait_ge(S(f"gathered{s}"), gather_value)
                for h in range(2):
                    for k in range(2):
                        last = tr(small[s][0:EK, k * CAP + h * HS:k * CAP + (h + 1) * HS],
                                  xg[s][:, h, k * EK:(k + 1) * EK], ident[0:HS, 0:HS])
                last.then_inc(S("xe_T"), 1)

            pe.wait_ge(S("list_ready"), 1)
            n2 = pe.value_load(lists[0:1, 2 * LIST:2 * LIST + 1], min_val=1, max_val=E // 2)
            slots_of(0, 1)
            slots_of(1, 2)
            gathered(0, 32, 1)
            with pe.Fori(0, n2) as i:
                for s in range(2):
                    v = 2 * i + s + 1
                    pe.wait_ge(S(f"w_loaded{s}"), 48 * i + 48)
                    pe.wait_ge(S("xeT_ready"), v)
                    for r in range(2):
                        pe.wait_ge(S(f"einner{r}"), v)
                        for bank in range(2):
                            for j in range(2):
                                c = bank * I + (2 * r + j) * SC
                                for k in range(2):
                                    last = mm(big[r][0:SC, bank, j * CAP:(j + 1) * CAP], w_gu[s][:, k, c:c + SC],
                                              xeT[s][:, k, :], start=(k == 0), stop=(k == 1))
                        last.then_inc(S(f"eup{r}"), 1)
                    gathered(1 - s, 32 * i + 32 + 32 * s, v + 1)
                    slots_of(s, v + 2)
                    pe.wait_ge(S("y_done"), v)
                    pe.wait_ge(S("einner0"), v + 1)
                    pe.wait_ge(S("einner1"), v + 1)
                    for h in range(2):
                        for c in range(NIC):
                            last = mm(aux[s][0:HS, h * D:(h + 1) * D],
                                      einner[s][:, c, h * HS:(h + 1) * HS], w_dn[s][:, c, :],
                                      start=(c == 0), stop=(c == NIC - 1))
                    last.then_inc(S("down_mm"), 1)

        @block.scalar
        def _(act):
            f, cp = nc.scalar.activation, nc.scalar.copy

            def features(s, v, rows, wait, done):
                act.wait_ge(wait, v)
                cp(xTa[s][:, 0:rows], small[s][0:DA, 0:rows])
                cp(xTb[s][0:DB, 0:rows], small[s][0:DB, 128:128 + rows]).then_inc(done, 1)

            def ff(s, v, n):
                yield f"sq{n}"
                act.wait_ge(S(f"ff{n}_up"), v)
                u = big[s][:, :, 0:384]
                f(sq[:].rearrange("p (b c) -> p b c", b=2), u, ACT.Square, scale=0.044715 ** 0.5).then_inc(S(f"ff{n}_sq"), 1)
                yield f"th{n}"
                act.wait_ge(S(f"ff{n}_poly"), v)
                f(hid[:], sq[:], ACT.Tanh, scale=0.7978845608028654).then_inc(S(f"ff{n}_th"), 1)

            def attention(s, v, n):
                yield f"qc{n}"
                act.wait_ge(S(f"at{n}_qk"), v)
                cp(qT[s][:], big[s][:, 0, 0:384].rearrange("p (m t) -> p m t", t=128))
                k_in = k_psum(s)
                if n == 1:
                    cp(kT2[0:64, :, :, 0:NP], k_in[0:64])
                for j in range(2):
                    rows = slice(32 * j, 32 * j + DH)
                    last = cp(k_blk[s][rows, :, :, j, 0:NP], k_in[rows])
                last.then_inc(S(f"at{n}_qk_sb"), 1)
                act.wait_ge(S(f"at{n}_v"), v)
                for g in range(2):
                    last = cp(vv[n][0:NP, g, :, 0:DH],
                              small[s][0:NP, g * D:(g + 1) * D].rearrange("p (h d) -> p h d", d=DH))
                last.then_inc(S(f"at{n}_v_sb"), 1)
                if n == 1:
                    yield "sc1"
                    act.wait_ge(S("at1_s"), v)
                    cp(sc_sb[:, 0:7 * NKEY], big[s][:, 0, 0:7 * NKEY])
                    cp(sc_sb[:, 7 * NKEY:13 * NKEY], big[s][:, 1, 0:6 * NKEY]).then_inc(S("at1_s_sb"), 1)
                yield f"exp{n}"
                keys, heads = ((NP, NH), (NKEY, NH + 1))[n]
                act.wait_ge(S(f"at{n}_sub"), v)
                f(att[s][:, 0:heads * keys], att[s][:, 0:heads * keys], ACT.Exp, scale=float(DH) ** -0.5)\
                    .then_inc(S(f"at{n}_exp" if n else "at0_p"), 1)
                for part, (lo, hi) in enumerate(((0, 8), (8, heads))):
                    yield f"c{n}{'ab'[part]}"
                    act.wait_ge(S(f"at{n}_T{part}"), v)
                    for bank in range((hi - lo + 3) // 4):
                        m = min(hi - lo - 4 * bank, 4)
                        last = cp(aT[s][0:keys, lo + 4 * bank:lo + 4 * bank + m, :],
                                  big[s][0:keys, bank, 0:m * 128].rearrange("p (h t) -> p h t", t=128))
                    last.then_inc(S(f"at{n}_aT{part}"), 1)

            def experts_in(s, v, rows):
                yield "xc"
                features(s, v, rows, S("xm_T"), S("xm_xT"))
                yield "router"
                act.wait_ge(S("logits"), v)
                f(sig[0:rows, :], small[s][0:rows, 256:256 + E], ACT.Exp, scale=-1.0).then_inc(S("sig_exp"), 1)
                for r in range(4):
                    yield f"sh_th{r}"
                    act.wait_ge(S("sh_up"), 4 * v - 3 + r)
                    g = sh_bank[0:SC, 0:256].rearrange("p (c t) -> p c t", t=128)[:, :, 0:rows]
                    f(th[:, :, 0:rows], g, ACT.Tanh, scale=0.5).then_inc(S("sh_th"), 1)

            act.wait_ge(cls_T, 1)
            act.wait_ge(presets, 2)
            cp(cxTa[:], small[0][0:DA, 0:B])
            cp(cxTb[0:DB, :], small[0][0:DB, 128:128 + B]).then_inc(cls_xT, 1)
            act.wait_ge(cls_qk, 1)
            cp(qcls[:], small[1][:, 0:HB]).then_inc(cls_q, 1)
            for g in range(2):
                cp(kT2[:, :, g, NP:NKEY], small[1][:, HB:2 * HB].unsqueeze(2))
                for j in range(4):
                    rows = slice(32 * j, 32 * j + DH)
                    cp(k_blk[1][rows, :, g, j, NP:NKEY], small[1][rows, HB:2 * HB].unsqueeze(2))
            act.wait_ge(cls_v, 1)
            for g in range(2):
                last = cp(vv[1][NP:NKEY, g, :, 0:DH], small[2][NP:NKEY, 0:D].rearrange("p (h d) -> p h d", d=DH))
            last.then_inc(acts_preset, 1)

            def first(v):
                yield "h0c"
                features(0, v, 128, S("h0_T"), S("ff0_xT"))
                yield from ff(0, v, 0)
                yield "yc"
                features(0, v, 128, S("y_T"), S("at0_xT"))
                yield from attention(0, v, 0)
                yield "oc0"
                features(0, v, 128, S("at0_oT"), S("at0_oxT"))
                yield "h1c"
                features(0, v, 128, S("h1_T"), S("ff1_xT"))
                yield from ff(0, v, 1)

            def second(v):
                yield "n2c"
                features(1, v, 128, S("n2_T"), S("at1_xT"))
                yield from attention(1, v, 1)
                yield "oc1"
                act.wait_ge(S("cls_oT"), v)
                cp(oclsTa[:, bass.ds(v + v - 2, 2)], small[1][:, 256:258])
                cp(oclsTb[0:DB, bass.ds(v + v - 2, 2)], small[1][0:DB, 258:260])
                features(1, v, 128, S("at1_oT"), S("at1_oxT"))

            run(first(1))
            interleave(second(1), first(2))
            with act.Fori(0, TILES - 3) as k:
                interleave(experts_in(2, k + 1, 128), second(k + 2), first(k + 3))
            interleave(experts_in(2, TILES - 2, 128), second(TILES - 1), first(TILES))
            interleave(experts_in(2, TILES - 1, 128), second(TILES))
            interleave(experts_in(2, TILES, 128))
            run(experts_in(2, NT, B))

            def rows_in(s, v):
                act.wait_ge(S("xe_T"), v)
                cp(xeT[s][:].rearrange("p k c -> p (k c)"), small[s][0:EK, 0:2 * CAP]).then_inc(S("xeT_ready"), 1)

            act.wait_ge(S("list_ready"), 1)
            n2 = act.value_load(lists[0:1, 2 * LIST:2 * LIST + 1], min_val=1, max_val=E // 2)
            rows_in(0, 1)
            with act.Fori(0, n2) as i:
                for s in range(2):
                    v = 2 * i + s + 1
                    for r in range(2):
                        act.wait_ge(S(f"eup{r}"), v + 2 * r)
                        act.wait_ge(S(f"einner{r}"), v)
                        f(eth[r][:], big[r][0:SC, 0, 0:2 * CAP], ACT.Tanh, scale=0.5).then_inc(S(f"eth{r}"), 1)
                    rows_in(1 - s, v + 1)

        @block.vector
        def _(dve):
            V = nc.vector
            ts, tt, stt = V.tensor_scalar, V.tensor_tensor, V.scalar_tensor_tensor

            step = S("step")
            seen = {"base": 0, "n": 0}

            def note(name, s):
                seen["n"] += 1
                seen[name, s] = seen["n"]
                return 1

            def noted(name, s):
                return seen["base"] + seen[name, s]

            def inverse_deviation(s, rows):
                x, r, q = var[s][0:rows, :], rstd[s][0:rows, :], newton[s][0:rows, :]
                dve.wait_ge(step, noted("aggr", s))
                ts(x, mv[s][0:rows, 1:2], 1e-5, None, op0=ALU.add).then_inc(step, note("eps", s))
                yield
                dve.wait_ge(step, noted("eps", s))
                ts(q.bitcast(i32), x.bitcast(i32), 1, None, op0=ALU.logical_shift_right).then_inc(step, note("half_bits", s))
                yield
                dve.wait_ge(step, noted("half_bits", s))
                ts(r.bitcast(i32), q.bitcast(i32), -1.0, float(0x5f3759df), op0=ALU.mult, op1=ALU.add)\
                    .then_inc(step, note("newton2", s))
                yield
                for _ in range(3):
                    dve.wait_ge(step, noted("newton2", s))
                    stt(q, r, r, x, ALU.mult, ALU.mult).then_inc(step, note("newton0", s))
                    yield
                    dve.wait_ge(step, noted("newton0", s))
                    ts(q, q, -0.5, 1.5, op0=ALU.mult, op1=ALU.add).then_inc(step, note("newton1", s))
                    yield
                    dve.wait_ge(step, noted("newton1", s))
                    tt(r, r, q, ALU.mult).then_inc(step, note("newton2", s))
                    yield
                dve.wait_ge(step, noted("newton2", s))

            def layernorm(dst, src, s, v, rows, name, waits=()):
                V.bn_stats(stat[s][0:rows, :], src).then_inc(step, note(name + "_stat", s))
                yield
                hold(dve, step, noted(name + "_stat", s))
                V.bn_aggr(mv[s][0:rows, :], stat[s][0:rows, :]).then_inc(step, note("aggr", s))
                yield
                yield from inverse_deviation(s, rows)
                yield ts(dst, src, mv[s][0:rows, 0:1], rstd[s][0:rows, :], op0=ALU.subtract, op1=ALU.mult)

            def ff(s, v, n):
                u = big[s][:, :, 0:384]
                two_banks = "p (b c) -> p b c"
                yield f"poly{n}"
                dve.wait_ge(S(f"ff{n}_sq"), v)
                stt(sq[:].rearrange(two_banks, b=2), sq[:].rearrange(two_banks, b=2), 1.0, u, ALU.add, ALU.mult)\
                    .then_inc(S(f"ff{n}_poly"), 1)
                yield f"hid{n}"
                dve.wait_ge(S(f"ff{n}_th"), v)
                stt(hid[:].rearrange(two_banks, b=2), hid[:].rearrange(two_banks, b=2), 1.0, u, ALU.add, ALU.mult)\
                    .then_inc(S(f"ff{n}_hid"), 1)

            def keys_of(s, v, n):
                yield f"qc{n}"
                dve.wait_ge(S(f"at{n}_qk"), v)
                if n == 1:
                    V.tensor_copy(kT2[64:128, :, :, 0:NP], k_psum(s)[64:128])
                for j in range(2, 4):
                    rows = slice(32 * j, 32 * j + DH)
                    last = V.tensor_copy(k_blk[s][rows, :, :, j, 0:NP], k_psum(s)[rows])
                last.then_inc(S(f"at{n}_k_sb"), 1)

            def normalise(s, v, n):
                yield f"norm{n}"
                dve.wait_ge(S(f"at{n}_o"), v)
                o = small[s][:, 0:NH * VD].rearrange("p (h d) -> p h d", d=VD)
                V.reciprocal(rr[s][:].unsqueeze(2), o[:, :, DH:VD]).then_inc(step, note(f"at{n}_rr", s))
                if n == 1:
                    V.reciprocal(rc[:], small[s][:, NH * VD + DH:NH * VD + VD]).then_inc(step, note("cls_rr", s))
                yield
                dve.wait_ge(step, noted(f"at{n}_rr", s))
                last = tt(o_sb[s][:].rearrange("p (h d) -> p h d", d=DH), o[:, :, 0:DH],
                          rr[s][:].unsqueeze(2).to_broadcast([128, NH, DH]), ALU.mult)
                if n == 1:
                    dve.wait_ge(step, noted("cls_rr", s))
                    oc = small[s][:, NH * VD:2 * NH * VD].rearrange("p (h d) -> p h d", d=VD)
                    last = stt(oc_sb[:].rearrange("p (h d) -> p h d", d=DH), oc[:, :, 0:DH], rc[:],
                               mask_o[:].rearrange("p (h d) -> p h d", d=DH), ALU.mult, ALU.mult)
                last.then_inc(S(f"at{n}_osb"), 1)

            def experts_in(s, v, rows):
                yield "ln3"
                dve.wait_ge(S("h3_ready"), v)
                V.tensor_copy(h3_kept[0:rows, :], h3[0:rows, :]).then_inc(S("h3_taken"), 1)
                dve.wait_ge(S("x_stored"), 32 * v)
                for last in layernorm(xm[0:rows, :], h3[0:rows, :], s, v, rows, "n3"):
                    if last is not None:
                        last.then_inc(S("xm_ready"), 1)
                    yield
                for r in range(4):
                    view = "p (c t) -> p c t"
                    g, u = (sh_bank[0:SC, at:at + 256].rearrange(view, t=128)[:, :, 0:rows] for at in (0, 256))
                    yield f"sh_in{r}"
                    dve.wait_ge(S("sh_th"), 4 * v - 3 + r)
                    stt(th[:, :, 0:rows], th[:, :, 0:rows], 1.0, g, ALU.add, ALU.mult).then_inc(step, note(f"sh_silu{r}", s))
                    yield
                    dve.wait_ge(step, noted(f"sh_silu{r}", s))
                    tt(inner[:, 2 * r:2 * r + 2, 0:rows], th[:, :, 0:rows], u, ALU.mult).then_inc(S("sh_inner"), 1)
                yield "acc"
                dve.wait_ge(S("sh_down"), v)
                dve.wait_ge(S("acc_stored"), 32 * v)
                stt(acc[0:rows, :], small[s][0:rows, 0:D], 0.5, h3_kept[0:rows, :], ALU.mult, ALU.add).then_inc(S("acc_ready"), 1)

            def route(s, v, rows, t):
                yield "router"
                dve.wait_ge(S("sig_exp"), v)
                ts(sig[0:rows, :], sig[0:rows, :], 1.0, None, op0=ALU.add).then_inc(step, note("sig_add", s))
                yield
                dve.wait_ge(step, noted("sig_add", s))
                V.reciprocal(sig[0:rows, :], sig[0:rows, :]).then_inc(step, note("sig_rec", s))
                yield
                dve.wait_ge(step, noted("sig_rec", s))
                tt(choice[0:rows, 0:E], sig[0:rows, :], e_bias[0:rows, :], ALU.add).then_inc(step, note("choice", s))
                yield
                hold(dve, step, noted("choice", s))
                V.max(best[0:rows, :], choice[0:rows, :]).then_inc(step, note("best", s))
                yield
                hold(dve, step, noted("best", s))
                V.match_replace(picked[0:rows, :], best[0:rows, :], choice[0:rows, :], -3e38).then_inc(step, note("picked", s))
                yield
                dve.wait_ge(step, noted("picked", s))
                ts(chosen[0:rows, t, :], picked[0:rows, 0:E], -2e38, None, op0=ALU.is_lt).then_inc(step, note("chosen", s))
                stt(wtok[0:rows, :], picked[0:rows, 0:E], -2e38, sig[0:rows, :], ALU.is_lt, ALU.mult).then_inc(step, note("w_masked", s))
                yield
                if rows == 128:
                    dve.wait_ge(step, noted("chosen", s))
                    dve.wait_ge(S("sums"), v)
                    tt(before_sum[:, t + 1, :], before_sum[:, t, :], chosen[:, t, :], ALU.add).then_inc(S("sums"), 1)
                    yield
                dve.wait_ge(step, noted("w_masked", s))
                V.reduce_sum(wsum[0:rows, :], wtok[0:rows, :], axis=AX.X).then_inc(step, note("w_sum", s))
                yield
                dve.wait_ge(step, noted("w_sum", s))
                ts(wsum[0:rows, :], wsum[0:rows, :], 1e-20, None, op0=ALU.add).then_inc(step, note("w_eps", s))
                yield
                dve.wait_ge(step, noted("w_eps", s))
                V.reciprocal(wsum[0:rows, :], wsum[0:rows, :]).then_inc(step, note("w_rec", s))
                yield
                dve.wait_ge(step, noted("w_rec", s))
                ts(wtok[0:rows, :], wtok[0:rows, :], wsum[0:rows, :], 2.5, op0=ALU.mult, op1=ALU.mult).then_inc(step, note("w_tok", s))
                yield
                parts = [wsplit[0:rows, t, 0:E, n:n + 1] for n in range(3)]
                wt, wr = wtok[0:rows, :].unsqueeze(2), wres[0:rows, :].unsqueeze(2)
                dve.wait_ge(step, noted("w_tok", s))
                V.tensor_copy(parts[0], wt).then_inc(step, note("w_p0", s))
                yield
                dve.wait_ge(step, noted("w_p0", s))
                tt(wr, wt, parts[0], ALU.subtract).then_inc(step, note("w_r0", s))
                yield
                dve.wait_ge(step, noted("w_r0", s))
                V.tensor_copy(parts[1], wr).then_inc(step, note("w_p1", s))
                yield
                dve.wait_ge(step, noted("w_p1", s))
                tt(parts[2], wr, parts[1], ALU.subtract).then_inc(step, note("w_p2", s))
                yield

            V.memset(zrows[:], 0.0).then_inc(presets, 1)
            V.memset(cxTb[DB:DB + 1, :], 1.0)
            V.memset(oclsTb[DB:DB + 1, :], 1.0)
            for s in range(2):
                V.memset(xTb[s][DB:DB + 1, :], 1.0)
                V.memset(vv[s][:, :, :, DH:VD], 1.0)
                V.memset(k_blk[s], 0.0)
            V.memset(choice[:, E:E + 2], 3e38)
            V.memset(ones[:], 1.0).then_inc(presets, 1)
            V.memset(before_sum[:, 0, :], 0.0).then_inc(S("sums"), 1)
            V.memset(chosen[:, TILES, :], 0.0)
            V.memset(slot[:], -1.0)
            V.memset(wsplit[:], 0.0).then_inc(S("memsets"), 1)
            dve.wait_ge(cls_loads, N_FIRST)
            for last in layernorm(norm2[0:B, :], cls_row[:], 1, 1, B, "cls"):
                if last is not None:
                    last.then_inc(cls_norm, 1)
            dve.wait_ge(cls_q, 1)
            tt(qcls_blk[:], mask_q[:], qcls[:].unsqueeze(2).to_broadcast([128, HB, 64]), ALU.mult)
            dve.wait_ge(consts, N_CONST)
            tt(pe_sb[:], pe_sb[:], ln_b[:], ALU.add)
            V.tensor_copy(before[:], before_f[:])
            V.tensor_copy(cls_before[:], cls_before_f)
            V.tensor_copy(pat_before[:], pat_before_f)
            V.tensor_copy(eval_b[:], eval_f[:])
            for s in range(2):
                V.tensor_copy(rhs[s][:, :, 0:3], tok_f[:].rearrange("p (t c) -> p t c", c=3))
            V.memset(best[0:1, 0:1], 0.0).then_inc(cls_ready, 1)
            dve.wait_ge(cls_ready, 1)
            dve.wait_ge(S("memsets"), 1)
            def patches(v):
                yield "ln0"
                dve.wait_ge(S("patch_mm"), v)
                tt(patch_x[:], sh_bank[:, 0:D], patch_b[:], ALU.add).then_inc(S("patch_taken"), 1)
                yield
                dve.wait_ge(S("patch_taken"), v)
                for last in layernorm(norm0[:], patch_x[:], 3, v, 128, "n0"):
                    if last is not None:
                        last.then_inc(step, note("n0_norm", 3))
                    yield
                dve.wait_ge(step, noted("n0_norm", 3))
                tt(patch_n[:], norm0[:], ln_g[:], ALU.mult).then_inc(S("patches_ready"), 1)

            def first(v):
                yield "pe"
                dve.wait_ge(S("patches_ready"), v)
                tt(h0[:], patch_n[:], pe_sb[:], ALU.add).then_inc(S("h0_ready"), 1)
                yield from ff(0, v, 0)
                yield "y"
                dve.wait_ge(S("ff0_down"), v)
                stt(norm[:], small[0][:, 0:D], 0.5, ff2_b[:], ALU.mult, ALU.add).then_inc(S("y_ready"), 1)
                yield from keys_of(0, v, 0)
                yield "max0"
                dve.wait_ge(S("at0_s"), v)
                V.reduce_max(mx[:].rearrange("p (b h) -> p b h", b=2), s1_scores(), axis=AX.X).then_inc(step, note("at0_max", 0))
                yield "sub0"
                dve.wait_ge(step, noted("at0_max", 0))
                tt(att[0][:, 0:NH * NP].rearrange("p (b h k) -> p b h k", b=2, k=NP), s1_scores(),
                   mx[:].rearrange("p (b h) -> p b h", b=2).unsqueeze(3).to_broadcast([128, 2, 6, NP]),
                   ALU.subtract).then_inc(S("at0_sub"), 1)
                yield from normalise(0, v, 0)
                yield "h1"
                dve.wait_ge(S("at0_proj"), v)
                tt(h1[:], small[0][:, 0:D], h0[:], ALU.add).then_inc(S("h1_ready"), 1)
                yield
                dve.wait_ge(S("h1_ready"), v)
                tt(h1_bias[:], h1[:], ff2_b[:], ALU.add).then_inc(step, note("h1_bias", 0))
                yield from ff(0, v, 1)
                yield "h2"
                dve.wait_ge(S("ff1_down"), v)
                dve.wait_ge(step, noted("h1_bias", 0))
                if not (isinstance(v, int) and v == 1):
                    dve.wait_ge(S("h2_taken"), v - 1)
                stt(h2[:], small[0][:, 0:D], 0.5, h1_bias[:], ALU.mult, ALU.add).then_inc(S("h2_ready"), 1)

            def second(v):
                yield "ln2"
                dve.wait_ge(S("h2_ready"), v)
                V.tensor_copy(h2_kept[:], h2[:]).then_inc(S("h2_taken"), 1)
                for last in layernorm(norm2[:], h2[:], 1, v, 128, "n2"):
                    if last is not None:
                        last.then_inc(S("n2_ready"), 1)
                    yield
                yield from keys_of(1, v, 1)
                yield "top0"
                hold(dve, S("at1_s_sb"), v)
                rounds = (top_a, top_b, top_c, top_d)
                for r, top in enumerate(rounds):
                    if r:
                        yield f"top{r}"
                        hold(dve, step, noted(f"top_cut{r - 1}", 1))
                    src = sc_sb if r == 0 else work
                    for h in range(NH + 1):
                        last = V.max(top[:, 8 * h:8 * h + 8], src[:, h * NKEY:(h + 1) * NKEY])
                        if h == NH // 2:
                            yield
                    if r == 0:
                        last.then_inc(S("top_max"), 1)
                        yield "cut0"
                        hold(dve, S("top_max"), v)
                    else:
                        last.then_inc(step, note(f"top_max{r}", 1))
                        if r == 3:
                            break
                        yield f"cut{r}"
                        hold(dve, step, noted(f"top_max{r}", 1))
                    for h in range(NH + 1):
                        last = V.match_replace(work[:, h * NKEY:(h + 1) * NKEY], top[:, 8 * h:8 * h + 8],
                                               src[:, h * NKEY:(h + 1) * NKEY], -3e38)
                        if h == NH // 2:
                            yield
                    last.then_inc(step, note(f"top_cut{r}", 1))
                yield "mask"
                nth = TOP_KEYS - 24 - 1
                kth = top_d[:].rearrange("p (h e) -> p h e", e=8)[:, :, nth:nth + 1].to_broadcast([128, NH + 1, NKEY])
                by_head = "p (h k) -> p h k"
                dve.wait_ge(step, noted("top_max3", 1))
                tt(work[:].rearrange(by_head, k=NKEY), sc_sb[:].rearrange(by_head, k=NKEY), kth, ALU.is_ge)\
                    .then_inc(step, note("at1_mask", 1))
                yield
                dve.wait_ge(S("at1_exp"), v)
                dve.wait_ge(step, noted("at1_mask", 1))
                tt(att[1][:], att[1][:], work[:], ALU.mult).then_inc(S("at1_p"), 1)
                yield from normalise(1, v, 1)
                yield "h3"
                dve.wait_ge(S("at1_proj"), v)
                if not (isinstance(v, int) and v == 1):
                    dve.wait_ge(S("h3_taken"), v - 1)
                dve.wait_ge(S("h2_taken"), v)
                tt(h3[:], small[1][:, 0:D], h2_kept[:], ALU.add).then_inc(S("h3_ready"), 1)

            def third(v):
                return experts_in(2, v, 128), route(2, v, 128, v - 1)

            run(patches(1))
            interleave(first(1), patches(2))
            interleave(second(1), first(2), patches(3))
            start = seen["n"]
            with dve.Fori(0, TILES - 3) as k:
                seen.clear()
                seen.update(base=STEPS * k + start, n=0)
                interleave(*third(k + 1), second(k + 2), first(k + 3), patches(k + 4))
            assert seen["n"] == STEPS, seen["n"]
            seen.clear()
            seen.update(base=STEPS * (TILES - 3) + start, n=0)
            interleave(*third(TILES - 2), second(TILES - 1), first(TILES))
            interleave(*third(TILES - 1), second(TILES))
            interleave(*third(TILES))
            dve.wait_ge(S("at1_proj"), NT)
            tt(h3[0:B, :], small[1][0:B, 0:D], cls_row[:], ALU.add).then_inc(S("h3_ready"), 1)
            interleave(experts_in(2, NT, B), route(2, NT, B, TILES))
            dve.wait_ge(step, noted("chosen", 2))
            dve.wait_ge(S("sums"), NT)
            V.memset(best[0:1, 0:1], 0.0).then_inc(S("chosen_all"), 1)

            for t in range(NT):
                rows = 128 if t < TILES else B
                dve.wait_ge(S("slots_mm"), t + 1)
                stt(slot[0:rows, t, 0:E], big[t % 2][0:rows, 0, 0:E], 1.0, chosen[0:rows, t, :], ALU.add, ALU.mult)\
                    .then_inc(S("slots_done"), 1)
            dve.wait_ge(S("slots_done"), NT)
            ts(slot[:, 0:TILES, 0:E], slot[:, 0:TILES, 0:E], -1.0, None, op0=ALU.add)
            ts(slot[0:B, TILES, 0:E], slot[0:B, TILES, 0:E], -1.0, None, op0=ALU.add).then_inc(S("slots_ready"), 1)
            dve.wait_ge(S("count_mm"), 1)
            ts(active_f[:], small[1][:, 0:1], 0.0, None, op0=ALU.is_gt).then_inc(S("active_f"), 1)
            dve.wait_ge(S("active_f"), 1)
            V.tensor_copy(active[:], active_f[:]).then_inc(S("active_ready"), 1)
            dve.wait_ge(S("rank_mm"), 1)
            V.tensor_copy(rank[:], small[0][:, 0:1]).then_inc(S("rank_ready"), 1)
            dve.wait_ge(S("rank_ready"), 1)
            ts(pick[:], iota_f[:, 0:LIST], rank[:], active_f[:], op0=ALU.is_equal, op1=ALU.mult).then_inc(S("pick_ready"), 1)
            dve.wait_ge(S("list_mm"), 1)
            ts(lists[:, 0:LIST], aux[1][0:1, 0:LIST], float(E), None, op0=ALU.add)
            V.tensor_copy(lists[:, LIST:2 * LIST], aux[1][0:1, LIST:2 * LIST])
            V.reduce_sum(n_pairs[:], aux[1][0:1, 2 * LIST:2 * LIST + LIST // 2], axis=AX.X).then_inc(S("pairs_counted"), 1)
            dve.wait_ge(S("pairs_counted"), 1)
            V.tensor_copy(lists[:, 2 * LIST:2 * LIST + 1], n_pairs[:]).then_inc(S("list_ready"), 1)

            def slots_of(j, s):
                e = dve.value_load(lists[0:1, bass.ds(j, 1)] if not isinstance(j, int) else lists[0:1, j:j + 1],
                                   min_val=0, max_val=E)
                tt(hot[s][:], iota_f[:, None, 0:CAP].to_broadcast([128, NT, CAP]),
                   slot[:, :, bass.ds(e, 1)].to_broadcast([128, NT, CAP]), ALU.is_equal)
                V.tensor_copy(rhs[s][:, :, 3:6], wsplit[:, :, bass.ds(e, 1), :].squeeze(2)).then_inc(S("hot_ready"), 1)

            def indices_of(s, v):
                dve.wait_ge(S("index_mm"), v)
                p = small[s][0:HS, 400:412].rearrange("p (h c) -> p h c", c=6)
                stt(slot_a[s][:].unsqueeze(2), p[:, :, 2:3], 1.0, dummy_f[:].unsqueeze(2), ALU.subtract, ALU.mult)
                V.reduce_sum(slot_w[s][:].unsqueeze(2), p[:, :, 3:6], axis=AX.X)
                V.tensor_copy(slot_b[s][:].unsqueeze(2), p[:, :, 1:2]).then_inc(S("index_a"), 1)
                dve.wait_ge(S("index_a"), v)
                tt(slot_a[s][:], slot_a[s][:], slot_b[s][:], ALU.add).then_inc(S("index_b"), 1)
                dve.wait_ge(S("index_b"), v)
                stt(index[s][:].unsqueeze(2), p[:, :, 0:1], 64.0, slot_a[s][:].unsqueeze(2), ALU.mult, ALU.add)\
                    .then_inc(S("index_ready"), 1)

            dve.wait_ge(S("list_ready"), 1)
            dve.wait_ge(S("slots_ready"), 1)
            n2 = dve.value_load(lists[0:1, 2 * LIST:2 * LIST + 1], min_val=1, max_val=E // 2)
            for r in range(2):
                dve.sem_inc(S(f"einner{r}"), 1)
            dve.sem_inc(S("y_done"), 2)
            slots_of(0, 0)
            slots_of(1, 1)
            indices_of(0, 1)
            indices_of(1, 2)
            slots_of(2, 0)
            with dve.Fori(0, n2) as i:
                for s in range(2):
                    v = 2 * i + s + 1
                    for r in range(2):
                        g, u = (big[r][0:SC, b, 0:2 * CAP] for b in range(2))
                        dve.wait_ge(S(f"eth{r}"), v)
                        stt(eth[r][:], eth[r][:], 1.0, g, ALU.add, ALU.mult).then_inc(S(f"esilu{r}"), 1)
                        dve.wait_ge(S(f"esilu{r}"), v)
                        if r == 0:
                            dve.wait_ge(S("down_mm"), v)
                        tt(einner[s][:, 2 * r:2 * r + 2, :].rearrange("p c n -> p (c n)"), eth[r][:], u, ALU.mult)\
                            .then_inc(S(f"einner{r}"), 1)
                    dve.wait_ge(S("add_done"), v)
                    V.tensor_copy(add_index[s][:], index[s][:])
                    V.tensor_copy(add_w[s][:], slot_w[s][:]).then_inc(S("kept"), 1)
                    dve.wait_ge(S("kept"), v)
                    indices_of(s, v + 2)
                    slots_of(2 * i + s + 3, 1 - s)
                    dve.wait_ge(S("down_mm"), v + 2)
                    for h in range(2):
                        last = ts(y[s][:, h, :], aux[s][0:HS, h * D:(h + 1) * D], add_w[s][:, h:h + 1], 0.5,
                                  op0=ALU.mult, op1=ALU.mult)
                    last.then_inc(S("y_done"), 1)

        @block.gpsimd
        def _(pool):
            G = nc.gpsimd
            by_head = "p (h k) -> p h k"
            with pool.Fori(0, TILES) as i:
                pool.wait_ge(S("top_max"), i + 1)
                G.tensor_tensor(att[1].rearrange(by_head, k=NKEY), sc_sb.rearrange(by_head, k=NKEY),
                                top_a[:].rearrange("p (h e) -> p h e", e=8)[:, :, 0:1].to_broadcast([128, NH + 1, NKEY]),
                                ALU.subtract).then_inc(S("at1_sub"), 1)

            def gather(s, v):
                hold(pool, S("index_ready"), v)
                for h in range(2):
                    G.indirect_dma_start(xg[s][:, h, :], None, x_rows[:, :],
                                         bass.IndirectOffsetOnAxis(index[s][:, h:h + 1], 0)).then_inc(S(f"gathered{s}"), 16)

            pool.wait_ge(S("rows_ready"), 1)
            pool.wait_ge(S("list_ready"), 1)
            n2 = pool.value_load(lists[0:1, 2 * LIST:2 * LIST + 1], min_val=1, max_val=E // 2)
            gather(0, 1)
            gather(1, 2)
            pool.sem_inc(S("add_done"), 2)
            with pool.Fori(0, n2) as i:
                for s in range(2):
                    v = 2 * i + s + 1
                    gather(s, v + 2)
                    hold(pool, S("y_done"), v + 2)
                    for h in range(2):
                        G.indirect_dma_start(out[:, :], bass.IndirectOffsetOnAxis(add_index[s][:, h:h + 1], 0),
                                             y[s][:, h, :], None, compute_op=ALU.add).then_inc(S("added"), 16)
                    pool.wait_ge(S("added"), 64 * i + 32 * s + 32)
                    pool.sem_inc(S("add_done"), 1)
            for s in range(2):
                pool.wait_ge(S(f"gathered{s}"), 32 * n2 + 32)


def _host_constants():
    import numpy as np
    f = np.float32
    p = np.arange(128)
    pos = np.arange(NP, dtype=f)[:, None]
    ang = pos / np.power(f(10000.0), f(2.0) * np.arange(D // 2, dtype=f)[None, :] / f(D)).astype(f)
    pe = np.zeros((NP, D), f)
    pe[:, 0::2], pe[:, 1::2] = np.sin(ang), np.cos(ang)
    mask_q = np.zeros((128, HB, 64), f)
    for m in range(HB):
        for j in range(4):
            mask_q[32 * j:32 * j + DH, m, 4 * m + j] = 1
    mask_o = np.zeros((128, NH, DH), f)
    for g in range(2):
        for h in range(NH):
            mask_o[64 * g + h, h] = 1
    tile = np.arange(TILES)
    img = 2 * tile[None, :] + (p // 64)[:, None]
    tok = np.zeros((128, NT), np.int64)
    tok[:, :TILES] = img * NKEY + 1 + (p % 64)[:, None]
    tok[:B, TILES] = np.arange(B) * NKEY
    tok = np.stack([tok // 64, tok % 64, np.ones_like(tok)], -1).astype(f).reshape(128, NT * 3)
    return {
        "ident": np.eye(128, dtype=f), "pe": np.concatenate([pe, pe]), "mask_q": mask_q,
        "mask_o": mask_o.reshape(128, D), "img_sel": (p[:, None] // 64 == np.arange(2)).astype(f),
        "before": (p[:, None] < p[None, :]).astype(f),
        "cls_before": (np.arange(B)[:, None, None] <= img.T[None]).astype(f).reshape(B, TILES * 128),
        "pat_before": (img[:, :, None] < np.arange(B)).astype(f).reshape(128, TILES * B),
        "iota": np.tile(np.arange(CAP, dtype=f), (128, 1)), "tok": tok,
        "dummy": -(DUMMY + np.arange(HS)[:, None] + HS * np.arange(2)[None, :]).astype(f),
        "evals": np.stack([p - E, p], -1).astype(f),
    }


def kernel(**inputs):
    import numpy as np
    import concourse.bacc as bacc
    from concourse.bass_utils import run_bass_kernel_spmd

    x = {k: np.ascontiguousarray(v) for k, v in inputs.items()}
    heads = np.arange(HB * 4).reshape(HB, 4, 1) * DH + np.arange(32)
    cols = np.concatenate([heads.reshape(-1), D + heads.reshape(-1)])
    n = IMG // PATCH
    patches = x["x"].reshape(TILES, 2, C, n, PATCH, n, PATCH).transpose(0, 2, 4, 6, 1, 3, 5)
    t, at, m = "L0_tok_", "L0_attn_", "L0_ffn_"
    arrays = {
        "xp": patches.reshape(TILES, KC, 128, 128).transpose(0, 2, 1, 3), "cls": x["cls_tok"].reshape(D),
        "patch_w": x[t + "patch_w"].reshape(D, KC, 128).transpose(2, 1, 0), "patch_b": x[t + "patch_b"],
        "ln_g": x[t + "ln_g"], "ln_b": x[t + "ln_b"],
        "ff1_w": x[t + "ff1_w"], "ff1_b": x[t + "ff1_b"], "ff2_w": x[t + "ff2_w"], "ff2_b": x[t + "ff2_b"],
        "wqk1": x[t + "qkv_w"][:, cols], "bqk1": x[t + "qkv_b"][cols],
        "wv1": x[t + "qkv_w"][:, 2 * D:], "bv1": x[t + "qkv_b"][2 * D:],
        "proj1_w": x[t + "proj_w"], "proj1_b": x[t + "proj_b"],
        "wqk2": x[at + "W_qkv"][:, cols], "bqk2": x[at + "b_qkv"][cols],
        "wv2": x[at + "W_qkv"][:, 2 * D:], "bv2": x[at + "b_qkv"][2 * D:],
        "proj2_w": x[at + "W_proj"], "proj2_b": x[at + "b_proj"],
        "wgT": x[m + "Wg"].T, "e_bias": x[m + "e_bias"],
        "w_gate_up": x[m + "W_gate_up"], "w_down": x[m + "W_down"],
        "wsg": x[m + "Wsg"], "wsu": x[m + "Wsu"], "wsd": x[m + "Wsd"],
        **_host_constants(),
    }
    nc = bacc.Bacc("TRN2", target_bir_lowering=False, num_devices=1)
    f32 = mybir.dt.float32
    arrays = {"in_" + k: np.ascontiguousarray(v) for k, v in arrays.items()}
    aps = {k[3:]: nc.dram_tensor(k, v.shape, f32, kind="ExternalInput").ap() for k, v in arrays.items()}
    out = nc.dram_tensor("out_rows", (ROWS, D), f32, kind="ExternalOutput").ap()
    tower_kernel(nc, aps, out)
    r = run_bass_kernel_spmd(nc, [arrays], core_ids=[0])
    return r.results[0]["out_rows"][0:T].reshape(B, NKEY, D)
```

```python
import concourse.bass as bass
from concourse import mybir
from contextlib import ExitStack

B, C, IMG, PATCH = 32, 3, 128, 16
D = 192
NP = (IMG // PATCH) ** 2
NKEY = NP + 1
T = B * NKEY
NH, DH = 12, 16
F = 768
TOP_KEYS = int(0.4 * NKEY)
E, TOPE, CAP = 128, 6, 192
I = 464
IS = 928
TILES = B * NP // 128
KC = C * PATCH * PATCH // 128
DA, DB = 128, D - 128
FC = F // 128
HB = NH // 4
VD = DH + 1
SC = 116
NSC, NIC = IS // SC, I // SC
EK = D // 2
HS = CAP // 2
NT = TILES + 1
DUMMY = T
ROWS = T + CAP
STEPS = 62
HOT_FIRST = 6
LIST = E + 4


PATCHES = dict(patch=3.92, ln0=226.08)
FIRST = dict(pe=0.74, h0T=0.71, h0c=0.67, up0a=1.41, sq0a=0.89, up0b=0.64, poly0a=1.21, sq0b=0.37, th0a=0.07,
             poly0b=0.15, hid0a=0.10, th0b=0.65, down0a=0.05, hid0b=3.87, down0b=1.32, y=0.80, yT=0.41,
             yc=0.47, qkv0=1.48, qc0=3.36, kc0=2.86, s0=0.96, max0=1.43, sub0=0.63, exp0=0.73, T0a=1.42,
             c0a=0.15, T0b=0.25, c0b=0.71, o0=3.30, norm0=1.66, oT0=0.74, oc0=2.34, proj0=1.54, h1=0.11,
             h1T=1.20, h1c=0.68, up1a=1.23, sq1a=0.84, up1b=0.08, poly1a=1.67, sq1b=0.90, th1a=0.14,
             poly1b=2.39, hid1a=0.12, th1b=2.47, down1a=0.20, hid1b=3.77, down1b=1.36, h2=1.82)
SECOND = dict(ln2=4.34, n2T=1.08, n2c=1.63, qkv1=1.70, qc1=1.33, kc1=1.34, s1=0.73, sc1=1.34, top0=3.07,
              sub1=0.66, cut0=1.13, exp1=2.09, top1=4.89, cut1=4.82, top2=2.16, cut2=3.74, top3=1.88,
              mask=1.94, T1a=1.30, c1a=0.14, T1b=0.93, c1b=2.04, o1=7.27, norm1=1.23, oT1=20.91, oc1=0.79,
              proj1=0.82, h3=0.07)
THIRD = dict(ln3=3.00, xT=0.91, xc=0.72, logits=0.63, router=0.99, sh_up0=1.93, sh_th0=0.33, sh_in0=1.37,
             sh_up1=2.38, sh_th1=0.48, sh_in1=0.43, sh_up2=2.17, sh_th2=0.93, sh_in2=2.03, sh_up3=1.78,
             sh_th3=4.94, sh_in3=0.59, down=2.13, acc=4.24)
CLASS_KEYS = dict(k_ln=6.43, k_T=0.27, k_c=0.13, k_qk=3.23, k_q=0.29, k_copies=3.41, k_tables=2.85)
CLASS_TILE = dict(c_proj=0.65, c_h3=0.41, c_ln3=3.25, c_xT=1.42, c_xc=0.52, c_logits=0.32, c_router=0.08,
                  c_sh_up0=1.46, c_sh_th0=0.32, c_sh_in0=0.97, c_sh_up1=1.46, c_sh_th1=0.32, c_sh_in1=0.97,
                  c_sh_up2=1.46, c_sh_th2=0.32, c_sh_in2=0.26, c_sh_up3=1.46, c_sh_th3=0.32, c_sh_in3=0.89,
                  c_down=2.11, c_acc=0.41)
RANKS = dict(chosen=0.31, slots=2.00, slots_out=1.77, counts=5.77, rank=0.87, list=0.57, hot=8.00)


def _starts(*stages):
    starts = {}
    for stage, at in stages:
        for step, lasts in stage.items():
            starts[step] = at
            at += lasts
    return starts


STARTS = _starts((PATCHES, 34.28), (FIRST, 0.00), (SECOND, 0.00), (THIRD, 6.24),
                 (CLASS_KEYS, 12.94), (CLASS_TILE, 2.22), (RANKS, 19.99))


def interleave(*stages):
    clocks = {stage: STARTS[next(stage)] for stage in stages}
    while clocks:
        stage = min(clocks, key=clocks.get)
        try:
            step = next(stage)
        except StopIteration:
            del clocks[stage]
            continue
        clocks[stage] = STARTS[step] if isinstance(step, str) else clocks[stage] + (step or 0.2)


def run(stage):
    for _ in stage:
        pass

SEMAPHORES = """
    zero_rows x_stored acc_stored patch_mm xm_ready acc_ready c_xm_ready cls_x_stored
    rows_ready c_acc_ready cls_acc_stored list_ready eup1 down_mm w_loaded0 w_loaded1 h0_ready
    h0_T ff0_xT ff0_up ff0_hid ff0_down y_ready y_T at0_xT at0_qk at0_v at0_k_sb at0_qk_sb
    at0_s at0_p at0_T0 at0_T1 at0_aT0 at0_aT1 at0_o at0_osb at0_oT at0_oxT patch_taken at0_proj
    h1_ready h1_T ff1_xT ff1_up ff1_hid ff1_down n2_ready n2_T at1_xT at1_qk at1_v at1_k_sb
    at1_qk_sb at1_s at1_p held at1_T0 at1_aT0 at1_T1 at1_aT1 at1_o at1_osb at1_oT cls_oT
    at1_oxT at1_proj xm_T xm_xT logits sh_up sh_inner sig_exp sh_down h3_ready c_proj c_xm_T
    c_xm_xT c_logits h2_ready c_sh_up c_sh_inner c_sig_exp c_sh_down chosen_all slots_mm
    slots_done count_mm active_ready rank_mm pick_ready list_mm hot_ready index_mm gathered0
    xe_T xeT_ready einner0 eup0 einner1 gathered1 y_done ff0_sq ff0_poly ff0_th at0_v_sb
    at0_sub ff1_sq ff1_poly ff1_th at1_v_sb at1_s_sb at1_sub at1_exp sh_th c_sh_th eth0 eth1
    step pe_ready patches_ready sums h2_taken top_max h3_taken c_h3_ready active_f rank_ready
    pairs_counted index_a index_b index_ready esilu0 esilu1 add_done kept added
"""


def tower_kernel(nc, a, out):
    f32, bf16, i32 = mybir.dt.float32, mybir.dt.bfloat16, mybir.dt.int32
    ALU, ACT, AX = mybir.AluOpType, mybir.ActivationFunctionType, mybir.AxisListType

    ctx = ExitStack()
    with ctx:
        def sb(name, shape, dt=f32):
            return ctx.enter_context(nc.sbuf_tensor("b_" + name, shape, dt))

        def two(name, shape, dt=f32):
            return [sb(f"{name}{s}", shape, dt) for s in range(2)]

        def each(name, shape):
            return [sb(f"{name}{s}", shape) for s in range(4)]

        def of(stages, name, shape, dt=f32):
            return {s: sb(f"{name}{s}", shape, dt) for s in stages}

        arena = [sb(f"arena{s}", [128, 5760]) for s in range(2)]

        def carve(start, rows, *dims, dt=f32):
            n = 1
            for d in dims:
                n *= d
            n = n if dt == f32 else n // 2
            views = [x[0:rows, start:start + n] for x in arena]
            if dt != f32:
                views = [x.bitcast(dt) for x in views]
            if len(dims) == 2:
                views = [x.rearrange("p (a b) -> p a b", b=dims[1]) for x in views]
            return views, start + n

        def pb(name, shape, dt=f32):
            return ctx.enter_context(nc.psum_tensor("p_" + name, shape, dt))

        def sem(name):
            return ctx.enter_context(nc.semaphore("s_" + name))

        ident = sb("ident", [128, 128])
        patch_w = sb("patch_w", [128, KC, D])
        patch_b = sb("patch_b", [128, D])
        ln_g = sb("ln_g", [128, D])
        ln_b = sb("ln_b", [128, D])
        pe_sb = sb("pe", [128, D])
        ff1a, ff1b = sb("ff1a", [DA, F]), sb("ff1b", [DB + 1, F])
        ff2 = sb("ff2", [128, FC, D])
        ff2_b = sb("ff2_b", [128, D])
        wqk = [(sb(f"wqk{n}a", [DA, 2 * HB * 128]), sb(f"wqk{n}b", [DB + 1, 2 * HB * 128])) for n in range(2)]
        wv = [(sb(f"wv{n}a", [DA, D]), sb(f"wv{n}b", [DB + 1, D])) for n in range(2)]
        wo = [(sb(f"wo{n}a", [DA, D]), sb(f"wo{n}b", [DB + 1, D])) for n in range(2)]
        wg_a, wg_b = sb("wg_a", [DA, E]), sb("wg_b", [DB, E])
        e_bias = sb("e_bias", [128, E])
        wsga, wsgb = sb("wsga", [DA, IS]), sb("wsgb", [DB, IS])
        wsua, wsub = sb("wsua", [DA, IS]), sb("wsub", [DB, IS])
        wsd = sb("wsd", [SC, NSC, D])
        cls_row = sb("cls_row", [B, D])
        mask_q = sb("mask_q", [128, HB, 64])
        mask_o = sb("mask_o", [128, D])
        img_sel = sb("img_sel", [128, 2])
        zrows = sb("zrows", [CAP // 2, 2 * D])
        before_f = sb("before_f", [128, 128])
        cls_before_f = arena[1][0:B, 512:512 + TILES * 128]
        pat_before_f = arena[1][:, 0:TILES * B]
        iota_f = sb("iota_f", [128, CAP + 1])
        iota_b = sb("iota_b", [128, CAP], bf16)
        tok_f = sb("tok_f", [128, NT * 3])
        dummy_f = sb("dummy_f", [HS, 2])
        eval_f = sb("eval_f", [128, 2])
        before = sb("before", [128, 128], bf16)
        cls_before = sb("cls_before", [B, TILES * 128], bf16)
        pat_before = sb("pat_before", [128, TILES * B], bf16)
        ones = sb("ones", [128, 128], bf16)
        eval_b = sb("eval_b", [128, 2], bf16)

        xp = sb("xp", [128, KC, 128])
        patch_x, patch_n = sb("patch_x", [128, D]), sb("patch_n", [128, D])
        h0, h1, h1_bias, norm = (sb(n, [128, D]) for n in ("h0", "h1", "h1_bias", "norm"))
        h2, h2_kept, norm2 = (sb(n, [128, D]) for n in ("h2", "h2_kept", "norm2"))
        norm0 = sb("norm0", [128, D])
        h3, h3_kept = sb("h3", [128, D]), {2: sb("h3_kept", [128, D]), 1: sb("h3_cls", [B, D])}
        xm, acc = ({2: sb(n, [128, D]), 1: sb(n + "_cls", [B, D])} for n in ("xm", "acc"))
        stat, mv, rstd = each("stat", [128, 6]), each("mv", [128, 2]), each("rstd", [128, 1])
        var, newton, scaled = each("var", [128, 1]), each("newton", [128, 1]), each("scaled", [128, 3])
        scales = sb("scales", [128, 3])
        xTa, xTb = of(range(3), "xTa", [DA, 128]), of(range(3), "xTb", [DB + 1, 128])
        sq, hid = sb("sq", [128, F]), sb("hid", [128, F])
        q_blk = of(range(2), "q_blk", [128, HB, 2, 128])
        kT2 = sb("kT2", [128, HB, 2, NKEY])
        vv = sb("v1", [NKEY, 2, NH, VD])
        v_pair = sb("v_pair", [128, 2, NH // 2, 2 * VD])
        o_sb = of(range(2), "o_sb", [128, D])
        oc_sb = sb("oc_sb", [128, D])
        rr, rc = of(range(2), "rr", [128, NH]), sb("rc", [128, 1])
        mx = sb("mx", [128, NH])
        att0, at = carve(0, 128, NH * NP)
        aT0, at = carve(at, 128, NH // 2, 128)
        k_blk0, at = carve(at, 128, HB * 2, 2 * NP)
        att1, at = carve(0, 128, (NH + 1) * NKEY)
        sc_sb, at = carve(at, 128, (NH + 1) * NKEY)
        work, at = carve(at, 128, (NH + 1) * NKEY)
        aT1, at = carve(at, NKEY, NH + 1, 128)
        k_blk1, at = carve(at, 128, HB * 2, 2 * NKEY)
        assert at <= 5760
        att, aT, sc_sb, work = {0: att0[0], 1: att1[1]}, {0: aT0[0], 1: aT1[1]}, sc_sb[1], work[1]
        k_blk = {n: x.rearrange("p (m g) (j k) -> p m g j k", g=2, j=2) for n, x in ((0, k_blk0[0]), (1, k_blk1[1]))}
        top_a, top_b, top_c, top_d = (sb(f"top_{n}", [128, (NH + 1) * 8]) for n in "abcd")
        def last(name, n):
            return {2: sb(name, [128, n]), 1: sb(name + "_cls", [B, n])}

        sig, wtok, wres = last("sig", E), last("wtok", E), last("wres", E)
        choice, picked = last("choice", E + 2), last("picked", E + 2)
        best, wsum = last("best", 8), last("wsum", 1)
        inner_buf = sb("inner", [128, NSC * 128])
        th = {2: sb("th", [SC, 2, 128]), 1: sb("th_cls", [SC, 2, B])}
        inner = {2: inner_buf[0:SC, :].rearrange("p (c t) -> p c t", t=128), 1: sb("inner_cls", [SC, NSC, B])}

        oclsTa, oclsTb = sb("oclsTa", [DA, B]), sb("oclsTb", [DB + 1, B])
        cxTa, cxTb = sb("cxTa", [DA, B]), sb("cxTb", [DB + 1, B])
        qcls = sb("qcls", [128, HB])
        qcls_blk = sb("qcls_blk", [128, HB, 64])
        v_cls = sb("v_cls", [NKEY, D])

        chosen = sb("chosen", [128, NT, E], bf16)
        before_sum = sb("before_sum", [128, NT, E], bf16)
        wsplit = sb("wsplit", [128, NT, E + 1, 3], bf16)
        slot = sb("slot", [128, NT, E + 1], bf16)
        counts, active_f = sb("counts", [128, 1]), sb("active_f", [128, 1])
        active = sb("active", [128, 1], bf16)
        rank, pick = sb("rank", [128, 1]), sb("pick", [128, LIST], bf16)
        lists = sb("lists", [1, 2 * LIST + 2], i32)
        n_pairs = sb("n_pairs", [1, 1])

        hot, at = carve(0, 128, NT, CAP, dt=bf16)
        rhs = two("rhs", [128, NT, 6], bf16)
        slot_a, slot_b = two("slot_a", [HS, 2]), two("slot_b", [HS, 2])
        slot_w, add_w = two("slot_w", [HS, 2]), two("add_w", [HS, 2])
        index, add_index = two("index", [HS, 2], i32), two("add_index", [HS, 2], i32)
        xeT = two("xeT", [EK, 2, CAP])
        w_gu, at = carve(at, EK, 2, 2 * I)
        w_dn, at = carve(at, SC, NIC, D)
        xg, at = carve(at, HS, 2, D)
        einner, at = carve(at, SC, NIC, CAP)
        assert at <= 5760
        eth = [hid[0:SC, 0:2 * CAP], inner_buf[0:SC, 0:2 * CAP]]
        y = [x[0:HS, 384:384 + 2 * D].rearrange("p (h d) -> p h d", d=D) for x in (hid, inner_buf)]

        big = [pb(f"big{s}", [128, 2, 512]) for s in range(2)]
        small = [pb(f"small{s}", [128, 512]) for s in range(3)]
        sh_bank = pb("shared", [128, 512])
        up_bank = {2: sh_bank, 1: small[0]}
        aux = [small[2], sh_bank]

        x_rows = nc.dram_tensor("x_rows", [ROWS, D], f32).ap()
        x_img = x_rows[0:T, :].rearrange("(b q) d -> b q d", q=NKEY)
        out_img = out[0:T, :].rearrange("(b q) d -> b q d", q=NKEY)

        loads_patch, loads_tokenizer, loads_cls, loads_rest = (
            sem("loads_" + n) for n in ("patch", "tokenizer", "cls", "rest"))
        xp_loaded = sem("xp_loaded")
        presets, pool_presets = sem("presets"), sem("pool_presets")
        cls_norm = sem("cls_norm")
        cls_T, cls_xT, cls_qk, cls_q, cls_v, cls_ready, cls_copied = (
            sem("cls_" + n) for n in ("T", "xT", "qk", "q", "v", "ready", "copied"))
        named = {name: sem(name) for name in SEMAPHORES.split()}

        def S(name):
            return named[name]

        def hold(eng, semaphore, value):
            eng.wait_ge(semaphore, value)
            eng.sem_inc(S("held"), 1)

        def halves(w, n):
            return [(w[0][:], n[0:DA, :]), (w[1][0:DB, :], n[DA:D, :])]

        def row(w, bias):
            return [(w[1][DB:DB + 1, :], bias.partition_broadcast(1))]

        def everywhere(v, n=128):
            return v.partition_broadcast(n)

        patch_loads = [(patch_w[:], a["patch_w"]), (ident[:], a["ident"]), (patch_b[:], everywhere(a["patch_b"])),
                       (ln_g[:], everywhere(a["ln_g"])), (ln_b[:], everywhere(a["ln_b"])), (pe_sb[:], a["pe"])]
        tokenizer_loads = [*halves((ff1a, ff1b), a["ff1_w"]), *row((ff1a, ff1b), a["ff1_b"]),
                           (ff2[:], a["ff2_w"].rearrange("(c p) d -> p c d", p=128)), (ff2_b[:], everywhere(a["ff2_b"])),
                           *halves(wqk[0], a["wqk1"]), *row(wqk[0], a["bqk1"]),
                           *halves(wv[0], a["wv1"]), *row(wv[0], a["bv1"]),
                           *halves(wo[0], a["proj1_w"]), *row(wo[0], a["proj1_b"])]
        cls_loads = [(cls_row[:], everywhere(a["cls"], B)), (mask_q[:], a["mask_q"]),
                     *halves(wqk[1], a["wqk2"]), *row(wqk[1], a["bqk2"]),
                     *halves(wv[1], a["wv2"]), *row(wv[1], a["bv2"]),
                     (before_f[:], a["before"]), (cls_before_f, a["cls_before"]), (pat_before_f, a["pat_before"]),
                     (iota_f[:], a["iota"]), (tok_f[:], a["tok"]), (dummy_f[:], a["dummy"]), (eval_f[:], a["evals"])]
        rest_loads = [*halves(wo[1], a["proj2_w"]), *row(wo[1], a["proj2_b"]),
                      (wg_a[:], a["wgT"][0:DA, :]), (wg_b[:], a["wgT"][DA:D, :]), (e_bias[:], everywhere(a["e_bias"])),
                      (wsga[:], a["wsg"][0:DA, :]), (wsgb[:], a["wsg"][DA:D, :]),
                      (wsua[:], a["wsu"][0:DA, :]), (wsub[:], a["wsu"][DA:D, :]),
                      (wsd[:], a["wsd"].rearrange("(c p) d -> p c d", p=SC)),
                      (mask_o[:], a["mask_o"]), (img_sel[:], a["img_sel"])]

        block = ctx.enter_context(nc.Block())

        def s1_scores():
            return big[0][:, :, 0:6 * NP].rearrange("p b (h k) -> p b h k", k=NP)

        def k_psum(s):
            return big[s][:, 1, 0:384].rearrange("p (m g t) -> p m g t", g=2, t=NP)

        @block.sync
        def _(sp):
            sp.dma_start(xp[:], a["xp"][0]).then_inc(xp_loaded, 16)
            for group, done in ((patch_loads, loads_patch), (tokenizer_loads, loads_tokenizer),
                                (cls_loads, loads_cls), (rest_loads, loads_rest)):
                for dst, src in group:
                    sp.dma_start(dst, src).then_inc(done, 16)
            sp.wait_ge(presets, 1)
            sp.dma_start(x_rows[T:ROWS, :].rearrange("(p r) d -> p (r d)", r=2), zrows[:]).then_inc(S("zero_rows"), 16)
            sp.dma_start(out[T:ROWS, :].rearrange("(p r) d -> p (r d)", r=2), zrows[:]).then_inc(S("zero_rows"), 16)

            for store in ("x_stored", "acc_stored"):
                sp.sem_inc(S(store), 32)

            def load(v):
                sp.wait_ge(S("patch_mm"), v - 1)
                sp.dma_start(xp[:], a["xp"][v - 1]).then_inc(xp_loaded, 16)

            def store_x(v):
                sp.wait_ge(S("xm_ready"), v)
                for g in range(2):
                    sp.dma_start(x_img[2 * v - 2 + g, 1:NKEY, :], xm[2][64 * g:64 * g + 64, :]).then_inc(S("x_stored"), 16)

            def store_acc(v):
                sp.wait_ge(S("acc_ready"), v)
                for g in range(2):
                    sp.dma_start(out_img[2 * v - 2 + g, 1:NKEY, :], acc[2][64 * g:64 * g + 64, :]).then_inc(S("acc_stored"), 16)

            for v in range(2, 5):
                load(v)
            with sp.Fori(0, TILES - 4) as k:
                store_x(k + 1)
                store_acc(k + 1)
                load(k + 5)
            for v in range(TILES - 3, TILES):
                store_x(v)
                store_acc(v)
            store_x(TILES)
            sp.wait_ge(S("c_xm_ready"), 1)
            sp.dma_start(x_img[:, 0, :], xm[1][:]).then_inc(S("cls_x_stored"), 16)
            sp.wait_ge(S("x_stored"), 32 * TILES + 32)
            sp.wait_ge(S("cls_x_stored"), 16)
            sp.wait_ge(S("zero_rows"), 32)
            sp.sem_inc(S("rows_ready"), 1)
            store_acc(TILES)
            sp.wait_ge(S("c_acc_ready"), 1)
            sp.dma_start(out_img[:, 0, :], acc[1][:]).then_inc(S("cls_acc_stored"), 16)

            sp.wait_ge(S("list_ready"), 1)
            n2 = sp.value_load(lists[0:1, 2 * LIST:2 * LIST + 1], min_val=1, max_val=E // 2)
            sp.sem_inc(S("eup1"), 2)
            sp.sem_inc(S("down_mm"), 2)
            with sp.Fori(0, n2) as i:
                for s in range(2):
                    e = sp.value_load(lists[0:1, bass.ds(LIST + 2 * i + s, 1)], min_val=0, max_val=E - 1)
                    gu = a["w_gate_up"][e].rearrange("(k p) f -> p k f", p=EK)
                    dn = a["w_down"][e].rearrange("(c p) d -> p c d", p=SC)
                    sp.wait_ge(S("eup1"), 2 * i + s + 1)
                    sp.dma_start(w_gu[s][:], gu).then_inc(S(f"w_loaded{s}"), 16)
                    sp.wait_ge(S("down_mm"), 2 * i + s + 1)
                    sp.dma_start(w_dn[s][0:112], dn[0:112]).then_inc(S(f"w_loaded{s}"), 16)
                    sp.dma_start(w_dn[s][112:SC], dn[112:SC]).then_inc(S(f"w_loaded{s}"), 16)

        @block.tensor
        def _(pe):
            mm, tr = nc.tensor.matmul, nc.tensor.transpose

            def to_features(src, s, rows, done):
                tr(small[s][0:DA, 0:rows], src[0:rows, 0:DA], ident[0:rows, 0:rows])
                tr(small[s][0:DB, 128:128 + rows], src[0:rows, DA:D], ident[0:rows, 0:rows]).then_inc(done, 1)

            def ff(s, v, n):
                for half in range(2):
                    yield f"up{n}{'ab'[half]}"
                    if half == 0:
                        pe.wait_ge(S(f"ff{n}_xT"), v)
                    for c in range(3 * half, 3 * half + 3):
                        o = big[s][:, half, (c % 3) * 128:(c % 3 + 1) * 128]
                        mm(o, ff1a[:, c * 128:(c + 1) * 128], xTa[s][:], start=True, stop=False)
                        last = mm(o, ff1b[:, c * 128:(c + 1) * 128], xTb[s][:], start=False, stop=True)
                    last.then_inc(S(f"ff{n}_up"), 1)
                for half in range(2):
                    yield f"down{n}{'ab'[half]}"
                    pe.wait_ge(S(f"ff{n}_hid"), 2 * v - 1 + half)
                    for c in range(3 * half, 3 * half + 3):
                        last = mm(small[s][:, 0:D], hid[:, c * 128:(c + 1) * 128], ff2[:, c, :],
                                  start=(c == 0), stop=(c == FC - 1))
                last.then_inc(S(f"ff{n}_down"), 1)

            def qkv(s, v, n):
                yield f"qkv{n}"
                pe.wait_ge(S(f"at{n}_xT"), v)
                for m in range(2 * HB):
                    o = big[s][:, m // HB, (m % HB) * 128:(m % HB + 1) * 128]
                    mm(o, wqk[n][0][:, m * 128:(m + 1) * 128], xTa[s][:], start=True, stop=False)
                    last = mm(o, wqk[n][1][:, m * 128:(m + 1) * 128], xTb[s][:], start=False, stop=True)
                    if m % HB == HB - 1:
                        last.then_inc(S(f"at{n}_qk"), 1)
                for g in range(2):
                    if n == 0:
                        for odd in range(2):
                            o, cols = small[s][64 * odd:64 * odd + 64, g * D // 2:(g + 1) * D // 2], slice(odd * D // 2, (odd + 1) * D // 2)
                            mm(o, xTa[s][:, 64 * g:64 * g + 64], wv[n][0][:, cols], start=True, stop=False)
                            last = mm(o, xTb[s][:, 64 * g:64 * g + 64], wv[n][1][:, cols], start=False, stop=True)
                        continue
                    o = small[s][0:NP, g * D:(g + 1) * D]
                    mm(o, xTa[s][:, 64 * g:64 * g + 64], wv[n][0][:], start=True, stop=False)
                    last = mm(o, xTb[s][:, 64 * g:64 * g + 64], wv[n][1][:], start=False, stop=True)
                last.then_inc(S(f"at{n}_v"), 1)

            def scores(s, v, n):
                yield f"s{n}"
                keys = (NP, NKEY)[n]
                pe.wait_ge(S(f"at{n}_k_sb"), v)
                pe.wait_ge(S(f"at{n}_qk_sb"), v)
                for g in range(2):
                    for m in range(HB):
                        last = mm(big[s][:, g, 2 * m * keys:(2 * m + 2) * keys], q_blk[s][:, m, g, :],
                                  k_blk[s][:, m, g, :, :].rearrange("p j k -> p (j k)"), start=True, stop=True)
                if n == 1:
                    for g in range(2):
                        for m in range(HB):
                            last = mm(big[s][64 * g:64 * g + 64, 0, 6 * keys:7 * keys],
                                      qcls_blk[:, m, :], kT2[:, m, g, :], start=(m == 0), stop=(m == HB - 1))
                last.then_inc(S(f"at{n}_s"), 1)

            def weigh0(v):
                yield "T0a"
                pe.wait_ge(S("at0_p"), v)
                for part in range(2):
                    for p in range(4 * part, min(4 * part + 4, NH // 2)):
                        last = tr(big[0][:, part, (p % 4) * 128:(p % 4 + 1) * 128], att[0][:, p * 128:(p + 1) * 128], ident[:])
                    last.then_inc(S(f"at0_T{part}"), 1)
                yield "o0"
                for part in range(2):
                    pe.wait_ge(S(f"at0_aT{part}"), v)
                    for p in range(4 * part, min(4 * part + 4, NH // 2)):
                        g, m = p // HB, p % HB
                        for hg in range(2):
                            at = (2 * m + hg) * 2 * VD
                            last = mm(small[0][64 * g:64 * g + 64, at:at + 2 * VD], aT[0][:, p, 64 * hg:64 * hg + 64], v_pair[:, g, 2 * m + hg, :],
                                          start=True, stop=True)
                last.then_inc(S("at0_o"), 1)
                yield "oT0"
                pe.wait_ge(S("at0_osb"), v)
                to_features(o_sb[0], 0, 128, S("at0_oT"))

            def weigh1(v, s=1, n=1):
                keys, heads = ((NP, NH), (NKEY, NH + 1))[n]
                for part, (lo, hi) in enumerate(((0, 8), (8, heads))):
                    yield f"T{n}{'ab'[part]}"
                    hold(pe, S(f"at{n}_p") if part == 0 else S(f"at{n}_aT0"), v)
                    for h in range(lo, hi):
                        r = h - lo
                        last = tr(big[s][0:keys, r // 4, (r % 4) * 128:(r % 4 + 1) * 128],
                                  att[s][:, h * keys:(h + 1) * keys], ident[:])
                    last.then_inc(S(f"at{n}_T{part}"), 1)
                yield f"o{n}"
                v_sb = vv
                hold(pe, S(f"at{n}_aT1"), v)
                for g in range(2):
                    rows = slice(64 * g, 64 * g + 64)
                    for h in range(NH):
                        block, hg = 7 * g + 2 * (h // 4) + h % 2, h % 4 // 2
                        last = mm(small[s][rows, h * VD:(h + 1) * VD], aT[s][0:keys, block, 64 * hg:64 * hg + 64],
                                  v_sb[:, g, h, :], start=True, stop=True)
                    if n == 1:
                        last = mm(small[s][rows, NH * VD:2 * NH * VD], aT[s][0:keys, 6, rows],
                                  v_sb[:, g, :, :].rearrange("p h d -> p (h d)"), start=True, stop=True)
                last.then_inc(S(f"at{n}_o"), 1)
                yield f"oT{n}"
                pe.wait_ge(S(f"at{n}_osb"), v)
                to_features(o_sb[s], s, 128, S(f"at{n}_oT"))
                if n == 1:
                    mm(small[s][:, 256:258], oc_sb[:, 0:DA], img_sel[:], start=True, stop=True)
                    mm(small[s][0:DB, 258:260], oc_sb[:, DA:D], img_sel[:], start=True, stop=True).then_inc(S("cls_oT"), 1)

            def project(s, v, n, la, lb, rows, ready):
                yield f"proj{n}"
                pe.wait_ge(ready, v)
                mm(small[s][0:rows, 0:D], la, wo[n][0][:], start=True, stop=False)
                mm(small[s][0:rows, 0:D], lb, wo[n][1][:], start=False, stop=True).then_inc(S(f"at{n}_proj"), 1)

            def experts_in(s, v, rows):
                c_ = "" if s == 2 else "c_"
                yield c_ + "xT"
                pe.wait_ge(S(c_ + "xm_ready"), v)
                to_features(xm[s], s, rows, S(c_ + "xm_T"))
                yield c_ + "logits"
                pe.wait_ge(S(c_ + "xm_xT"), v)
                mm(small[s][0:rows, 256:256 + E], xTa[s][:, 0:rows], wg_a[:], start=True, stop=False)
                mm(small[s][0:rows, 256:256 + E], xTb[s][0:DB, 0:rows], wg_b[:], start=False, stop=True).then_inc(S(c_ + "logits"), 1)
                for r in range(4):
                    yield c_ + f"sh_up{r}"
                    if not r and s == 1:
                        pe.wait_ge(S("h2_ready"), TILES)
                    if not r and s == 2:
                        pe.wait_ge(S("patch_taken"), min(v + 2, TILES) if isinstance(v, int) else v + 2)
                    if r:
                        pe.wait_ge(S(c_ + "sh_inner"), 4 * v - 4 + r)
                    for n, (wa, wb) in enumerate(((wsga, wsgb), (wsua, wsub))):
                        for c in (2 * r, 2 * r + 1):
                            at = n * 256 + (c % 2) * 128
                            o = up_bank[s][0:SC, at:at + rows]
                            mm(o, wa[:, c * SC:(c + 1) * SC], xTa[s][:, 0:rows], start=True, stop=False)
                            last = mm(o, wb[:, c * SC:(c + 1) * SC], xTb[s][0:DB, 0:rows], start=False, stop=True)
                    last.then_inc(S(c_ + "sh_up"), 1)
                yield c_ + "down"
                pe.wait_ge(S(c_ + "sh_inner"), 4 * v)
                pe.wait_ge(S(c_ + "sig_exp"), v)
                for c in range(NSC):
                    last = mm(small[s][0:rows, 0:D], inner[s][:, c, 0:rows], wsd[:, c, :],
                              start=(c == 0), stop=(c == NSC - 1))
                last.then_inc(S(c_ + "sh_down"), 1)

            def class_keys():
                yield "k_T"
                pe.wait_ge(loads_cls, 16 * len(cls_loads))
                pe.wait_ge(cls_norm, 1)
                tr(small[1][0:DA, 0:B], norm2[0:B, 0:DA], ident[0:B, 0:B])
                tr(small[1][0:DB, 128:128 + B], norm2[0:B, DA:D], ident[0:B, 0:B]).then_inc(cls_T, 1)
                yield "k_qk"
                pe.wait_ge(cls_xT, 1)
                for m in range(2 * HB):
                    mm(small[1][:, m:m + 1], wqk[1][0][:, m * 128:(m + 1) * 128], cxTa[:, 0:1], start=True, stop=False)
                    last = mm(small[1][:, m:m + 1], wqk[1][1][:, m * 128:(m + 1) * 128], cxTb[:, 0:1], start=False, stop=True)
                last.then_inc(cls_qk, 1)
                mm(small[2][NP:NKEY, 0:D], cxTa[:, 0:1], wv[1][0][:], start=True, stop=False)
                mm(small[2][NP:NKEY, 0:D], cxTb[:, 0:1], wv[1][1][:], start=False, stop=True).then_inc(cls_v, 1)

            def patches(v):
                yield "patch"
                pe.wait_ge(xp_loaded, 16 * v)
                if isinstance(v, int):
                    if v > 1:
                        pe.wait_ge(S("patch_taken"), v - 1)
                else:
                    pe.wait_ge(S("sh_inner"), 4 * v - 12)
                for c in range(KC):
                    last = mm(sh_bank[:, 0:D], xp[:, c, :], patch_w[:, c, :], start=(c == 0), stop=(c == KC - 1))
                last.then_inc(S("patch_mm"), 1)

            def first(v):
                yield "h0T"
                pe.wait_ge(S("h0_ready"), v)
                to_features(h0, 0, 128, S("h0_T"))
                yield from ff(0, v, 0)
                yield "yT"
                pe.wait_ge(S("y_ready"), v)
                to_features(norm, 0, 128, S("y_T"))
                yield from qkv(0, v, 0)
                yield from scores(0, v, 0)
                yield from weigh0(v)
                yield from project(0, v, 0, xTa[0][:], xTb[0][:], 128, S("at0_oxT"))
                yield "h1T"
                pe.wait_ge(S("h1_ready"), v)
                to_features(h1, 0, 128, S("h1_T"))
                yield from ff(0, v, 1)

            def second(v):
                yield "n2T"
                pe.wait_ge(S("n2_ready"), v)
                to_features(norm2, 1, 128, S("n2_T"))
                yield from qkv(1, v, 1)
                yield from scores(1, v, 1)
                yield from weigh1(v)
                yield from project(1, v, 1, xTa[1][:], xTb[1][:], 128, S("at1_oxT"))

            pe.wait_ge(loads_patch, 16 * len(patch_loads))
            run(patches(1))
            pe.wait_ge(loads_tokenizer, 16 * len(tokenizer_loads))
            pe.wait_ge(presets, 2)
            pe.wait_ge(pool_presets, 1)
            interleave(first(1), class_keys(), patches(2))
            pe.wait_ge(cls_ready, 1)
            pe.wait_ge(cls_copied, 1)
            pe.wait_ge(loads_rest, 16 * len(rest_loads))
            interleave(second(1), first(2), patches(3))
            with pe.Fori(0, TILES - 3) as k:
                interleave(experts_in(2, k + 1, 128), second(k + 2), first(k + 3), patches(k + 4))
            interleave(experts_in(2, TILES - 2, 128), second(TILES - 1), first(TILES))
            interleave(experts_in(2, TILES - 1, 128), second(TILES))

            def class_tile():
                yield "c_proj"
                pe.wait_ge(S("h3_ready"), TILES)
                mm(small[1][0:B, 0:D], oclsTa[:], wo[1][0][:], start=True, stop=False)
                mm(small[1][0:B, 0:D], oclsTb[:], wo[1][1][:], start=False, stop=True).then_inc(S("c_proj"), 1)
                yield from experts_in(1, 1, B)

            def ranks():
                yield "slots"
                pe.wait_ge(S("chosen_all"), 1)
                for t in range(TILES):
                    b = t // 4
                    p = big[b // 2][:, b % 2, (t % 4) * E:(t % 4 + 1) * E]
                    mm(p, before[:], chosen[:, t, :], start=True, stop=False)
                    mm(p, ones[:], before_sum[:, t, :], start=False, stop=False)
                    last = mm(p, cls_before[:, t * 128:(t + 1) * 128], chosen[0:B, TILES, :], start=False, stop=True)
                    if t % 4 == 3:
                        last.then_inc(S("slots_mm"), 1)
                yield "counts"
                pe.wait_ge(S("slots_done"), 1)
                for t in range(TILES):
                    mm(big[0][0:B, 0, 0:E], pat_before[:, t * B:(t + 1) * B], chosen[:, t, :], start=(t == 0), stop=False)
                mm(big[0][0:B, 0, 0:E], before[0:B, 0:B], chosen[0:B, TILES, :], start=False, stop=True)\
                    .then_inc(S("slots_mm"), 1)
                pe.wait_ge(S("slots_done"), 2)
                mm(big[0][:, 1, 0:1], before_sum[:, TILES, :], ones[:, 0:1], start=True, stop=False)
                mm(big[0][:, 1, 0:1], chosen[0:B, TILES, :], ones[0:B, 0:1], start=False, stop=True).then_inc(S("count_mm"), 1)
                yield "rank"
                pe.wait_ge(S("active_ready"), 1)
                mm(big[0][:, 1, 2:3], before[:], active[:], start=True, stop=True).then_inc(S("rank_mm"), 1)
                yield "list"
                pe.wait_ge(S("pick_ready"), 1)
                pe.wait_ge(S("slots_done"), 3)
                o = big[1][0:1, 0, :]
                mm(o[:, 0:LIST], eval_b[:, 0:1], pick[:], start=True, stop=True)
                mm(o[:, LIST:2 * LIST], eval_b[:, 1:2], pick[:], start=True, stop=True)
                mm(o[:, 2 * LIST:2 * LIST + LIST // 2], ones[:, 0:1], pick[:, 0:LIST:2], start=True, stop=True)\
                    .then_inc(S("list_mm"), 1)

            interleave(experts_in(2, TILES, 128), class_tile(), ranks())

            def slots_of(s, v):
                pe.wait_ge(S("hot_ready"), v)
                for h in range(2):
                    for t in range(NT):
                        last = mm(small[s][0:HS, 400 + 6 * h:406 + 6 * h], hot[s][:, t, h * HS:(h + 1) * HS], rhs[s][:, t, :],
                                  start=(t == 0), stop=(t == NT - 1))
                last.then_inc(S("index_mm"), 1)

            def gathered(s, gather_value, v):
                pe.wait_ge(S(f"gathered{s}"), gather_value)
                for h in range(2):
                    for k in range(2):
                        last = tr(small[s][0:EK, k * CAP + h * HS:k * CAP + (h + 1) * HS],
                                  xg[s][:, h, k * EK:(k + 1) * EK], ident[0:HS, 0:HS])
                last.then_inc(S("xe_T"), 1)

            pe.wait_ge(S("list_ready"), 1)
            n2 = pe.value_load(lists[0:1, 2 * LIST:2 * LIST + 1], min_val=1, max_val=E // 2)
            pe.wait_ge(S("c_acc_ready"), 1)
            pe.wait_ge(S("acc_ready"), TILES)
            slots_of(0, 1)
            slots_of(1, 2)
            gathered(0, 32, 1)
            with pe.Fori(0, n2) as i:
                for s in range(2):
                    v = 2 * i + s + 1
                    pe.wait_ge(S(f"w_loaded{s}"), 48 * i + 48)
                    pe.wait_ge(S("xeT_ready"), v)
                    for r in range(2):
                        pe.wait_ge(S(f"einner{r}"), v)
                        for bank in range(2):
                            for j in range(2):
                                c = bank * I + (2 * r + j) * SC
                                for k in range(2):
                                    last = mm(big[r][0:SC, bank, j * CAP:(j + 1) * CAP], w_gu[s][:, k, c:c + SC],
                                              xeT[s][:, k, :], start=(k == 0), stop=(k == 1))
                        last.then_inc(S(f"eup{r}"), 1)
                    gathered(1 - s, 32 * i + 32 + 32 * s, v + 1)
                    slots_of(s, v + 2)
                    pe.wait_ge(S("y_done"), v)
                    pe.wait_ge(S("einner0"), v + 1)
                    pe.wait_ge(S("einner1"), v + 1)
                    for h in range(2):
                        for c in range(NIC):
                            last = mm(aux[s][0:HS, h * D:(h + 1) * D],
                                      einner[s][:, c, h * HS:(h + 1) * HS], w_dn[s][:, c, :],
                                      start=(c == 0), stop=(c == NIC - 1))
                    last.then_inc(S("down_mm"), 1)

        @block.scalar
        def _(act):
            f, cp = nc.scalar.activation, nc.scalar.copy

            def features(s, v, rows, wait, done):
                act.wait_ge(wait, v)
                cp(xTa[s][:, 0:rows], small[s][0:DA, 0:rows])
                cp(xTb[s][0:DB, 0:rows], small[s][0:DB, 128:128 + rows]).then_inc(done, 1)

            def ff(s, v, n):
                for step, half in (("sq", 0), ("sq", 1), ("th", 0), ("th", 1)):
                    cols, u = slice(384 * half, 384 * half + 384), big[s][:, half, 0:384]
                    yield f"{step}{n}{'ab'[half]}"
                    if step == "sq":
                        act.wait_ge(S(f"ff{n}_up"), 2 * v - 1 + half)
                        f(sq[:, cols], u, ACT.Square, scale=0.044715 ** 0.5).then_inc(S(f"ff{n}_sq"), 1)
                    else:
                        act.wait_ge(S(f"ff{n}_poly"), 2 * v - 1 + half)
                        f(hid[:, cols], sq[:, cols], ACT.Tanh, scale=0.7978845608028654).then_inc(S(f"ff{n}_th"), 1)

            def attention(s, v, n):
                yield f"qc{n}"
                act.wait_ge(S(f"at{n}_qk"), 2 * v - 1)
                for hg in range(2):
                    rows = slice(64 * hg, 64 * hg + 64)
                    cp(q_blk[s][rows, :, :, rows], big[s][rows, 0, 0:384].rearrange("p (m g t) -> p m g t", g=2, t=NP))
                yield f"kc{n}"
                act.wait_ge(S(f"at{n}_qk"), 2 * v)
                k_in = k_psum(s)
                if n == 1:
                    cp(kT2[0:64, :, :, 0:NP], k_in[0:64])
                for j in range(2):
                    rows = slice(32 * j, 32 * j + DH)
                    last = cp(k_blk[s][rows, :, :, j % 2, 0:NP], k_in[rows])
                last.then_inc(S(f"at{n}_qk_sb"), 1)
                act.wait_ge(S(f"at{n}_v"), v)
                for g in range(2):
                    if n == 0:
                        rows = slice(64 * g, 64 * g + 64)
                        last = cp(v_pair[rows, :, :, g * VD:g * VD + DH],
                                  small[s][rows, 0:D].rearrange("p (g h d) -> p g h d", g=2, d=DH))
                        continue
                    last = cp(vv[0:NP, g, :, 0:DH],
                              small[s][0:NP, g * D:(g + 1) * D].rearrange("p (h d) -> p h d", d=DH))
                last.then_inc(S(f"at{n}_v_sb"), 1)
                if n == 1:
                    yield "sc1"
                    act.wait_ge(S("at1_s"), v)
                    cp(sc_sb[:, 0:7 * NKEY], big[s][:, 0, 0:7 * NKEY])
                    cp(sc_sb[:, 7 * NKEY:13 * NKEY], big[s][:, 1, 0:6 * NKEY]).then_inc(S("at1_s_sb"), 1)
                yield f"exp{n}"
                keys, heads = ((NP, NH), (NKEY, NH + 1))[n]
                act.wait_ge(S(f"at{n}_sub"), v)
                f(att[s][:, 0:heads * keys], att[s][:, 0:heads * keys], ACT.Exp, scale=float(DH) ** -0.5)\
                    .then_inc(S(f"at{n}_exp" if n else "at0_p"), 1)
                if n == 0:
                    for part, pairs in enumerate((4, NH // 2 - 4)):
                        yield f"c0{'ab'[part]}"
                        act.wait_ge(S(f"at0_T{part}"), v)
                        cp(aT[0][:, 4 * part:4 * part + pairs, :],
                           big[0][:, part, 0:pairs * 128].rearrange("p (h t) -> p h t", t=128)).then_inc(S(f"at0_aT{part}"), 1)
                    return
                for part, (lo, hi) in enumerate(((0, 8), (8, heads))):
                    yield f"c{n}{'ab'[part]}"
                    act.wait_ge(S(f"at{n}_T{part}"), v)
                    for bank in range((hi - lo + 3) // 4):
                        m = min(hi - lo - 4 * bank, 4)
                        last = cp(aT[s][0:keys, lo + 4 * bank:lo + 4 * bank + m, :],
                                  big[s][0:keys, bank, 0:m * 128].rearrange("p (h t) -> p h t", t=128))
                    last.then_inc(S(f"at{n}_aT{part}"), 1)

            def experts_in(s, v, rows):
                c_ = "" if s == 2 else "c_"
                yield c_ + "xc"
                features(s, v, rows, S(c_ + "xm_T"), S(c_ + "xm_xT"))
                yield c_ + "router"
                act.wait_ge(S(c_ + "logits"), v)
                f(sig[s][0:rows, :], small[s][0:rows, 256:256 + E], ACT.Exp, scale=-1.0).then_inc(S(c_ + "sig_exp"), 1)
                for r in range(4):
                    yield c_ + f"sh_th{r}"
                    act.wait_ge(S(c_ + "sh_up"), 4 * v - 3 + r)
                    g = up_bank[s][0:SC, 0:256].rearrange("p (c t) -> p c t", t=128)[:, :, 0:rows]
                    f(th[s][:, :, 0:rows], g, ACT.Tanh, scale=0.5).then_inc(S(c_ + "sh_th"), 1)

            def class_keys():
                yield "k_c"
                act.wait_ge(cls_T, 1)
                act.wait_ge(presets, 2)
                cp(cxTa[:], small[1][0:DA, 0:B])
                cp(cxTb[0:DB, :], small[1][0:DB, 128:128 + B]).then_inc(cls_xT, 1)
                yield "k_q"
                act.wait_ge(cls_qk, 1)
                cp(qcls[:], small[1][:, 0:HB]).then_inc(cls_q, 1)
                yield "k_copies"
                act.wait_ge(pool_presets, 2)
                for g in range(2):
                    cp(kT2[:, :, g, NP:NKEY], small[1][:, HB:2 * HB].unsqueeze(2))
                    for j in range(4):
                        rows = slice(32 * j, 32 * j + DH)
                        cp(k_blk[1][rows, :, g, j % 2, NP:NKEY], small[1][rows, HB:2 * HB].unsqueeze(2))
                yield
                act.wait_ge(cls_v, 1)
                for g in range(2):
                    last = cp(vv[NP:NKEY, g, :, 0:DH], small[2][NP:NKEY, 0:D].rearrange("p (h d) -> p h d", d=DH))
                last.then_inc(cls_copied, 1)

            def first(v):
                yield "h0c"
                features(0, v, 128, S("h0_T"), S("ff0_xT"))
                yield from ff(0, v, 0)
                yield "yc"
                features(0, v, 128, S("y_T"), S("at0_xT"))
                yield from attention(0, v, 0)
                yield "oc0"
                features(0, v, 128, S("at0_oT"), S("at0_oxT"))
                yield "h1c"
                features(0, v, 128, S("h1_T"), S("ff1_xT"))
                yield from ff(0, v, 1)

            def second(v):
                yield "n2c"
                features(1, v, 128, S("n2_T"), S("at1_xT"))
                yield from attention(1, v, 1)
                yield "oc1"
                act.wait_ge(S("cls_oT"), v)
                cp(oclsTa[:, bass.ds(v + v - 2, 2)], small[1][:, 256:258])
                cp(oclsTb[0:DB, bass.ds(v + v - 2, 2)], small[1][0:DB, 258:260])
                features(1, v, 128, S("at1_oT"), S("at1_oxT"))

            act.wait_ge(presets, 2)
            act.wait_ge(pool_presets, 1)
            interleave(first(1), class_keys())
            interleave(second(1), first(2))
            with act.Fori(0, TILES - 3) as k:
                interleave(experts_in(2, k + 1, 128), second(k + 2), first(k + 3))
            interleave(experts_in(2, TILES - 2, 128), second(TILES - 1), first(TILES))
            interleave(experts_in(2, TILES - 1, 128), second(TILES))
            interleave(experts_in(2, TILES, 128), experts_in(1, 1, B))

            def rows_in(s, v):
                act.wait_ge(S("xe_T"), v)
                cp(xeT[s][:].rearrange("p k c -> p (k c)"), small[s][0:EK, 0:2 * CAP]).then_inc(S("xeT_ready"), 1)

            act.wait_ge(S("list_ready"), 1)
            n2 = act.value_load(lists[0:1, 2 * LIST:2 * LIST + 1], min_val=1, max_val=E // 2)
            rows_in(0, 1)
            with act.Fori(0, n2) as i:
                for s in range(2):
                    v = 2 * i + s + 1
                    for r in range(2):
                        act.wait_ge(S(f"eup{r}"), v + 2 * r)
                        act.wait_ge(S(f"einner{r}"), v)
                        f(eth[r][:], big[r][0:SC, 0, 0:2 * CAP], ACT.Tanh, scale=0.5).then_inc(S(f"eth{r}"), 1)
                    rows_in(1 - s, v + 1)

        @block.vector
        def _(dve):
            V = nc.vector
            ts, tt, stt = V.tensor_scalar, V.tensor_tensor, V.scalar_tensor_tensor

            step = S("step")
            seen = {"base": 0, "n": 0}

            def note(name, s):
                seen["n"] += 1
                seen[name, s] = seen["n"]
                return 1

            def noted(name, s):
                return seen["base"] + seen[name, s]

            def inverse_deviation(s, rows):
                x, r, q, nx = var[s][0:rows, :], rstd[s][0:rows, :], newton[s][0:rows, :], scaled[s][0:rows, :]
                dve.wait_ge(step, noted("aggr", s))
                ts(x, mv[s][0:rows, 1:2], 1e-5, None, op0=ALU.add).then_inc(step, note("eps", s))
                yield
                dve.wait_ge(step, noted("eps", s))
                ts(r.bitcast(i32), x.bitcast(i32), -0.5, float(0x5f3759df - (3 << 23)), op0=ALU.mult, op1=ALU.add)
                tt(nx, x.to_broadcast([rows, 3]), scales[0:rows, :], ALU.mult).then_inc(step, note("newton1", s))
                yield
                for k in range(3):
                    dve.wait_ge(step, noted("newton1", s))
                    stt(q, r, nx[:, k:k + 1], r, ALU.mult, ALU.mult).then_inc(step, note("newton0", s))
                    yield
                    dve.wait_ge(step, noted("newton0", s))
                    stt(r, q, 3.0, r, ALU.add, ALU.mult).then_inc(step, note("newton1", s))
                    yield
                dve.wait_ge(step, noted("newton1", s))

            def layernorm(dst, src, s, v, rows, name, waits=()):
                V.bn_stats(stat[s][0:rows, :], src).then_inc(step, note(name + "_stat", s))
                yield
                hold(dve, step, noted(name + "_stat", s))
                V.bn_aggr(mv[s][0:rows, :], stat[s][0:rows, :]).then_inc(step, note("aggr", s))
                yield
                yield from inverse_deviation(s, rows)
                yield ts(dst, src, mv[s][0:rows, 0:1], rstd[s][0:rows, :], op0=ALU.subtract, op1=ALU.mult)

            def ff(s, v, n):
                for step, half in (("poly", 0), ("poly", 1), ("hid", 0), ("hid", 1)):
                    cols, u = slice(384 * half, 384 * half + 384), big[s][:, half, 0:384]
                    yield f"{step}{n}{'ab'[half]}"
                    if step == "poly":
                        dve.wait_ge(S(f"ff{n}_sq"), 2 * v - 1 + half)
                        stt(sq[:, cols], sq[:, cols], 1.0, u, ALU.add, ALU.mult).then_inc(S(f"ff{n}_poly"), 1)
                    else:
                        dve.wait_ge(S(f"ff{n}_th"), 2 * v - 1 + half)
                        stt(hid[:, cols], hid[:, cols], 1.0, u, ALU.add, ALU.mult).then_inc(S(f"ff{n}_hid"), 1)

            def keys_of(s, v, n):
                yield f"kc{n}"
                dve.wait_ge(S(f"at{n}_qk"), 2 * v)
                if n == 1:
                    V.tensor_copy(kT2[64:128, :, :, 0:NP], k_psum(s)[64:128])
                for j in range(2, 4):
                    rows = slice(32 * j, 32 * j + DH)
                    last = V.tensor_copy(k_blk[s][rows, :, :, j % 2, 0:NP], k_psum(s)[rows])
                last.then_inc(S(f"at{n}_k_sb"), 1)

            def normalise(s, v, n):
                yield f"norm{n}"
                dve.wait_ge(S(f"at{n}_o"), v)
                o = small[s][:, 0:NH * VD].rearrange("p (h d) -> p h d", d=VD)
                V.reciprocal(rr[s][:].unsqueeze(2), o[:, :, DH:VD]).then_inc(step, note(f"at{n}_rr", s))
                if n == 1:
                    V.reciprocal(rc[:], small[s][:, NH * VD + DH:NH * VD + VD]).then_inc(step, note("cls_rr", s))
                yield
                dve.wait_ge(step, noted(f"at{n}_rr", s))
                last = tt(o_sb[s][:].rearrange("p (h d) -> p h d", d=DH), o[:, :, 0:DH],
                          rr[s][:].unsqueeze(2).to_broadcast([128, NH, DH]), ALU.mult)
                if n == 1:
                    dve.wait_ge(step, noted("cls_rr", s))
                    oc = small[s][:, NH * VD:2 * NH * VD].rearrange("p (h d) -> p h d", d=VD)
                    last = stt(oc_sb[:].rearrange("p (h d) -> p h d", d=DH), oc[:, :, 0:DH], rc[:],
                               mask_o[:].rearrange("p (h d) -> p h d", d=DH), ALU.mult, ALU.mult)
                last.then_inc(S(f"at{n}_osb"), 1)

            def experts_in(s, v, rows):
                c_ = "" if s == 2 else "c_"
                yield c_ + "ln3"
                dve.wait_ge(S(c_ + "h3_ready"), v)
                if s == 2:
                    dve.wait_ge(S("acc_stored"), 32 * v)
                    V.tensor_copy(h3_kept[s][:], h3[:]).then_inc(S("h3_taken"), 1)
                    dve.wait_ge(S("h3_taken"), v)
                    dve.wait_ge(S("x_stored"), 32 * v)
                for last in layernorm(xm[s][0:rows, :], h3_kept[s][0:rows, :], s, v, rows, "n3"):
                    if last is not None:
                        last.then_inc(S(c_ + "xm_ready"), 1)
                    yield
                for r in range(4):
                    view = "p (c t) -> p c t"
                    g, u = (up_bank[s][0:SC, at:at + 256].rearrange(view, t=128)[:, :, 0:rows] for at in (0, 256))
                    yield c_ + f"sh_in{r}"
                    dve.wait_ge(S(c_ + "sh_th"), 4 * v - 3 + r)
                    stt(th[s][:, :, 0:rows], th[s][:, :, 0:rows], 1.0, g, ALU.add, ALU.mult).then_inc(step, note(f"sh_silu{r}", s))
                    yield
                    dve.wait_ge(step, noted(f"sh_silu{r}", s))
                    tt(inner[s][:, 2 * r:2 * r + 2, 0:rows], th[s][:, :, 0:rows], u, ALU.mult).then_inc(S(c_ + "sh_inner"), 1)
                yield c_ + "acc"
                dve.wait_ge(S(c_ + "sh_down"), v)
                stt(acc[s][0:rows, :], small[s][0:rows, 0:D], 0.5, h3_kept[s][0:rows, :], ALU.mult, ALU.add).then_inc(S(c_ + "acc_ready"), 1)

            def route(s, v, rows, t):
                c_ = "" if s == 2 else "c_"
                yield c_ + "router"
                dve.wait_ge(S(c_ + "sig_exp"), v)
                ts(sig[s][0:rows, :], sig[s][0:rows, :], 1.0, None, op0=ALU.add).then_inc(step, note("sig_add", s))
                yield
                dve.wait_ge(step, noted("sig_add", s))
                V.reciprocal(sig[s][0:rows, :], sig[s][0:rows, :]).then_inc(step, note("sig_rec", s))
                yield
                dve.wait_ge(step, noted("sig_rec", s))
                tt(choice[s][0:rows, 0:E], sig[s][0:rows, :], e_bias[0:rows, :], ALU.add).then_inc(step, note("choice", s))
                yield
                hold(dve, step, noted("choice", s))
                V.max(best[s][0:rows, :], choice[s][0:rows, :]).then_inc(step, note("best", s))
                yield
                hold(dve, step, noted("best", s))
                V.match_replace(picked[s][0:rows, :], best[s][0:rows, :], choice[s][0:rows, :], -3e38).then_inc(step, note("picked", s))
                yield
                dve.wait_ge(step, noted("picked", s))
                ts(chosen[0:rows, t, :], picked[s][0:rows, 0:E], -2e38, None, op0=ALU.is_lt).then_inc(step, note("chosen", s))
                stt(wtok[s][0:rows, :], picked[s][0:rows, 0:E], -2e38, sig[s][0:rows, :], ALU.is_lt, ALU.mult).then_inc(step, note("w_masked", s))
                yield
                if rows == 128:
                    dve.wait_ge(step, noted("chosen", s))
                    dve.wait_ge(S("sums"), v)
                    tt(before_sum[:, t + 1, :], before_sum[:, t, :], chosen[:, t, :], ALU.add).then_inc(S("sums"), 1)
                    yield
                dve.wait_ge(step, noted("w_masked", s))
                V.reduce_sum(wsum[s][0:rows, :], wtok[s][0:rows, :], axis=AX.X).then_inc(step, note("w_sum", s))
                yield
                dve.wait_ge(step, noted("w_sum", s))
                ts(wsum[s][0:rows, :], wsum[s][0:rows, :], 1e-20, None, op0=ALU.add).then_inc(step, note("w_eps", s))
                yield
                dve.wait_ge(step, noted("w_eps", s))
                V.reciprocal(wsum[s][0:rows, :], wsum[s][0:rows, :]).then_inc(step, note("w_rec", s))
                yield
                dve.wait_ge(step, noted("w_rec", s))
                ts(wtok[s][0:rows, :], wtok[s][0:rows, :], wsum[s][0:rows, :], 2.5, op0=ALU.mult, op1=ALU.mult).then_inc(step, note("w_tok", s))
                yield
                parts = [wsplit[0:rows, t, 0:E, n:n + 1] for n in range(3)]
                wt, wr = wtok[s][0:rows, :].unsqueeze(2), wres[s][0:rows, :].unsqueeze(2)
                dve.wait_ge(step, noted("w_tok", s))
                V.tensor_copy(parts[0], wt).then_inc(step, note("w_p0", s))
                yield
                dve.wait_ge(step, noted("w_p0", s))
                tt(wr, wt, parts[0], ALU.subtract).then_inc(step, note("w_r0", s))
                yield
                dve.wait_ge(step, noted("w_r0", s))
                V.tensor_copy(parts[1], wr).then_inc(step, note("w_p1", s))
                yield
                dve.wait_ge(step, noted("w_p1", s))
                tt(parts[2], wr, parts[1], ALU.subtract).then_inc(step, note("w_p2", s))
                yield

            V.memset(zrows[:], 0.0).then_inc(presets, 1)
            for k, scale in enumerate((-64.0, -16.0, -4.0)):
                V.memset(scales[:, k:k + 1], scale)
            V.memset(cxTb[DB:DB + 1, :], 1.0)
            V.memset(oclsTb[DB:DB + 1, :], 1.0)
            for s in range(3):
                V.memset(xTb[s][DB:DB + 1, :], 1.0)
            V.memset(v_pair[0:64, :, :, VD:2 * VD], 0.0)
            V.memset(v_pair[64:128, :, :, 0:VD], 0.0)
            for s in range(2):
                V.memset(v_pair[64 * s:64 * s + 64, :, :, s * VD + DH:(s + 1) * VD], 1.0)
                V.memset(choice[s + 1][:, E:E + 2], 3e38)
            V.memset(vv[:, :, :, DH:VD], 1.0)
            V.memset(ones[:], 1.0).then_inc(presets, 1)

            def class_keys():
                yield "k_ln"
                dve.wait_ge(loads_cls, 16 * len(cls_loads))
                for last in layernorm(norm2[0:B, :], cls_row[:], 1, 1, B, "cls"):
                    if last is not None:
                        last.then_inc(cls_norm, 1)
                    yield
                yield "k_copies"
                dve.wait_ge(cls_q, 1)
                tt(qcls_blk[:], mask_q[:], qcls[:].unsqueeze(2).to_broadcast([128, HB, 64]), ALU.mult)
                yield "k_tables"
                V.tensor_copy(before[:], before_f[:])
                yield
                V.tensor_copy(cls_before[:], cls_before_f)
                yield
                V.tensor_copy(pat_before[:], pat_before_f)
                V.tensor_copy(eval_b[:], eval_f[:])
                V.tensor_copy(iota_b[:], iota_f[:, 1:CAP + 1])
                yield
                for s in range(2):
                    V.tensor_copy(rhs[s][:, :, 0:3], tok_f[:].rearrange("p (t c) -> p t c", c=3))
                V.memset(before_sum[:, 0, :], 0.0).then_inc(cls_ready, 1)

            def patches(v):
                yield "ln0"
                dve.wait_ge(S("patch_mm"), v)
                tt(patch_x[:], sh_bank[:, 0:D], patch_b[:], ALU.add).then_inc(S("patch_taken"), 1)
                yield
                dve.wait_ge(S("patch_taken"), v)
                for last in layernorm(norm0[:], patch_x[:], 3, v, 128, "n0"):
                    if last is not None:
                        last.then_inc(step, note("n0_norm", 3))
                    yield
                dve.wait_ge(step, noted("n0_norm", 3))
                tt(patch_n[:], norm0[:], ln_g[:], ALU.mult).then_inc(S("patches_ready"), 1)

            def first(v):
                yield "pe"
                dve.wait_ge(S("patches_ready"), v)
                tt(h0[:], patch_n[:], pe_sb[:], ALU.add).then_inc(S("h0_ready"), 1)
                yield from ff(0, v, 0)
                yield "y"
                dve.wait_ge(S("ff0_down"), v)
                stt(norm[:], small[0][:, 0:D], 0.5, ff2_b[:], ALU.mult, ALU.add).then_inc(S("y_ready"), 1)
                yield from keys_of(0, v, 0)
                yield "max0"
                dve.wait_ge(S("at0_s"), v)
                V.reduce_max(mx[:].rearrange("p (b h) -> p b h", b=2), s1_scores(), axis=AX.X).then_inc(step, note("at0_max", 0))
                yield "sub0"
                dve.wait_ge(step, noted("at0_max", 0))
                tt(att[0][:, 0:NH * NP].rearrange("p (b h k) -> p b h k", b=2, k=NP), s1_scores(),
                   mx[:].rearrange("p (b h) -> p b h", b=2).unsqueeze(3).to_broadcast([128, 2, 6, NP]),
                   ALU.subtract).then_inc(S("at0_sub"), 1)
                yield from normalise(0, v, 0)
                yield "h1"
                dve.wait_ge(S("at0_proj"), v)
                tt(h1[:], small[0][:, 0:D], h0[:], ALU.add).then_inc(S("h1_ready"), 1)
                yield
                dve.wait_ge(S("h1_ready"), v)
                tt(h1_bias[:], h1[:], ff2_b[:], ALU.add).then_inc(step, note("h1_bias", 0))
                yield from ff(0, v, 1)
                yield "h2"
                dve.wait_ge(S("ff1_down"), v)
                dve.wait_ge(step, noted("h1_bias", 0))
                if not (isinstance(v, int) and v == 1):
                    dve.wait_ge(S("h2_taken"), v - 1)
                stt(h2[:], small[0][:, 0:D], 0.5, h1_bias[:], ALU.mult, ALU.add).then_inc(S("h2_ready"), 1)

            def second(v):
                yield "ln2"
                dve.wait_ge(S("h2_ready"), v)
                if not (isinstance(v, int) and v == 1):
                    dve.wait_ge(S("h3_ready"), v - 1)
                V.tensor_copy(h2_kept[:], h2[:]).then_inc(S("h2_taken"), 1)
                for last in layernorm(norm2[:], h2[:], 1, v, 128, "n2"):
                    if last is not None:
                        last.then_inc(S("n2_ready"), 1)
                    yield
                yield from keys_of(1, v, 1)
                yield "top0"
                hold(dve, S("at1_s_sb"), v)
                rounds = (top_a, top_b, top_c, top_d)
                for r, top in enumerate(rounds):
                    if r:
                        yield f"top{r}"
                        hold(dve, step, noted(f"top_cut{r - 1}", 1))
                    src = sc_sb if r == 0 else work
                    for h in range(NH + 1):
                        last = V.max(top[:, 8 * h:8 * h + 8], src[:, h * NKEY:(h + 1) * NKEY])
                        if h % 3 == 2:
                            yield 0.4
                    if r == 0:
                        last.then_inc(S("top_max"), 1)
                        yield "cut0"
                        hold(dve, S("top_max"), v)
                    else:
                        last.then_inc(step, note(f"top_max{r}", 1))
                        if r == 3:
                            break
                        yield f"cut{r}"
                        hold(dve, step, noted(f"top_max{r}", 1))
                    for h in range(NH + 1):
                        last = V.match_replace(work[:, h * NKEY:(h + 1) * NKEY], top[:, 8 * h:8 * h + 8],
                                               src[:, h * NKEY:(h + 1) * NKEY], -3e38)
                        if h % 3 == 2:
                            yield 0.4
                    last.then_inc(step, note(f"top_cut{r}", 1))
                yield "mask"
                nth = TOP_KEYS - 24 - 1
                kth = top_d[:].rearrange("p (h e) -> p h e", e=8)[:, :, nth:nth + 1].to_broadcast([128, NH + 1, NKEY])
                by_head = "p (h k) -> p h k"
                dve.wait_ge(step, noted("top_max3", 1))
                tt(work[:].rearrange(by_head, k=NKEY), sc_sb[:].rearrange(by_head, k=NKEY), kth, ALU.is_ge)\
                    .then_inc(step, note("at1_mask", 1))
                yield
                dve.wait_ge(S("at1_exp"), v)
                dve.wait_ge(step, noted("at1_mask", 1))
                tt(att[1][:], att[1][:], work[:], ALU.mult).then_inc(S("at1_p"), 1)
                yield from normalise(1, v, 1)
                yield "h3"
                dve.wait_ge(S("at1_proj"), v)
                if not (isinstance(v, int) and v == 1):
                    dve.wait_ge(S("h3_taken"), v - 1)
                dve.wait_ge(S("h2_taken"), v)
                tt(h3[:], small[1][:, 0:D], h2_kept[:], ALU.add).then_inc(S("h3_ready"), 1)

            def third(v):
                return experts_in(2, v, 128), route(2, v, 128, v - 1)

            dve.wait_ge(presets, 2)
            dve.wait_ge(loads_patch, 16 * len(patch_loads))
            tt(pe_sb[:], pe_sb[:], ln_b[:], ALU.add).then_inc(S("pe_ready"), 1)
            run(patches(1))
            dve.wait_ge(S("pe_ready"), 1)
            dve.wait_ge(loads_tokenizer, 16 * len(tokenizer_loads))
            dve.wait_ge(pool_presets, 1)
            interleave(first(1), class_keys(), patches(2))
            dve.wait_ge(pool_presets, 2)
            dve.wait_ge(loads_rest, 16 * len(rest_loads))
            dve.wait_ge(cls_ready, 1)
            dve.sem_inc(S("sums"), 1)
            interleave(second(1), first(2), patches(3))
            start = seen["n"]
            with dve.Fori(0, TILES - 3) as k:
                seen.clear()
                seen.update(base=STEPS * k + start, n=0)
                interleave(*third(k + 1), second(k + 2), first(k + 3), patches(k + 4))
            assert seen["n"] == STEPS, seen["n"]
            seen.clear()
            seen.update(base=STEPS * (TILES - 3) + start, n=0)
            interleave(*third(TILES - 2), second(TILES - 1), first(TILES))
            interleave(*third(TILES - 1), second(TILES))

            def class_tile():
                yield "c_h3"
                dve.wait_ge(S("c_proj"), 1)
                tt(h3_kept[1][:], small[1][0:B, 0:D], cls_row[:], ALU.add).then_inc(S("c_h3_ready"), 1)
                yield from experts_in(1, 1, B)

            def slots_of(j, s):
                e = dve.value_load(lists[0:1, bass.ds(j, 1)] if not isinstance(j, int) else lists[0:1, j:j + 1],
                                   min_val=0, max_val=E)
                for tiles in (slice(0, HOT_FIRST), slice(HOT_FIRST, NT)):
                    n = tiles.stop - tiles.start
                    last = tt(hot[s][:, tiles, :], iota_b[:, None, :].to_broadcast([128, n, CAP]),
                              slot[:, tiles, bass.ds(e, 1)].to_broadcast([128, n, CAP]), ALU.is_equal)
                    if tiles.stop == NT:
                        V.tensor_copy(rhs[s][:, :, 3:6], wsplit[:, :, bass.ds(e, 1), :].squeeze(2)).then_inc(S("hot_ready"), 1)
                    yield

            def ranks():
                yield "chosen"
                dve.wait_ge(step, noted("chosen", 2))
                dve.wait_ge(step, noted("chosen", 1))
                dve.wait_ge(S("sums"), NT)
                dve.sem_inc(S("chosen_all"), 1)
                yield "slots_out"
                for b in range(TILES // 4):
                    dve.wait_ge(S("slots_mm"), b + 1)
                    stt(slot[:, 4 * b:4 * b + 4, 0:E], big[b // 2][:, b % 2, :].rearrange("p (t e) -> p t e", e=E), 1.0,
                        chosen[:, 4 * b:4 * b + 4, :], ALU.add, ALU.mult).then_inc(S("slots_done"), 1)
                    yield
                yield "rank"
                dve.wait_ge(S("count_mm"), 1)
                ts(active_f[:], big[0][:, 1, 0:1], 0.0, None, op0=ALU.is_gt).then_inc(S("active_f"), 1)
                yield
                dve.wait_ge(S("active_f"), 1)
                V.tensor_copy(active[:], active_f[:]).then_inc(S("active_ready"), 1)
                stt(slot[0:B, TILES, 0:E], big[0][0:B, 0, 0:E], 1.0, chosen[0:B, TILES, :], ALU.add, ALU.mult)\
                    .then_inc(S("slots_done"), 1)
                yield "list"
                dve.wait_ge(S("rank_mm"), 1)
                V.tensor_copy(rank[:], big[0][:, 1, 2:3]).then_inc(S("rank_ready"), 1)
                yield
                dve.wait_ge(S("rank_ready"), 1)
                ts(pick[:], iota_f[:, 0:LIST], rank[:], active_f[:], op0=ALU.is_equal, op1=ALU.mult).then_inc(S("pick_ready"), 1)
                yield "hot"
                dve.wait_ge(S("list_mm"), 1)
                o = big[1][0:1, 0, :]
                ts(lists[:, 0:LIST], o[:, 0:LIST], float(E), None, op0=ALU.add)
                V.tensor_copy(lists[:, LIST:2 * LIST], o[:, LIST:2 * LIST])
                V.reduce_sum(n_pairs[:], o[:, 2 * LIST:2 * LIST + LIST // 2], axis=AX.X).then_inc(S("pairs_counted"), 1)
                yield
                dve.wait_ge(S("pairs_counted"), 1)
                V.tensor_copy(lists[:, 2 * LIST:2 * LIST + 1], n_pairs[:]).then_inc(S("list_ready"), 1)
                dve.wait_ge(S("list_ready"), 1)
                dve.wait_ge(S("slots_done"), TILES // 4 + 1)
                yield
                yield from slots_of(0, 0)
                yield from slots_of(1, 1)

            interleave(*third(TILES), class_tile(), route(1, 1, B, TILES), ranks())

            def indices_of(s, v):
                dve.wait_ge(S("index_mm"), v)
                p = small[s][0:HS, 400:412].rearrange("p (h c) -> p h c", c=6)
                stt(slot_a[s][:].unsqueeze(2), p[:, :, 2:3], 1.0, dummy_f[:].unsqueeze(2), ALU.subtract, ALU.mult)
                V.reduce_sum(slot_w[s][:].unsqueeze(2), p[:, :, 3:6], axis=AX.X)
                V.tensor_copy(slot_b[s][:].unsqueeze(2), p[:, :, 1:2]).then_inc(S("index_a"), 1)
                dve.wait_ge(S("index_a"), v)
                tt(slot_a[s][:], slot_a[s][:], slot_b[s][:], ALU.add).then_inc(S("index_b"), 1)
                dve.wait_ge(S("index_b"), v)
                stt(index[s][:].unsqueeze(2), p[:, :, 0:1], 64.0, slot_a[s][:].unsqueeze(2), ALU.mult, ALU.add)\
                    .then_inc(S("index_ready"), 1)

            n2 = dve.value_load(lists[0:1, 2 * LIST:2 * LIST + 1], min_val=1, max_val=E // 2)
            for r in range(2):
                dve.sem_inc(S(f"einner{r}"), 1)
            dve.sem_inc(S("y_done"), 2)
            indices_of(0, 1)
            indices_of(1, 2)
            run(slots_of(2, 0))
            with dve.Fori(0, n2) as i:
                for s in range(2):
                    v = 2 * i + s + 1
                    slots = slots_of(2 * i + s + 3, 1 - s)
                    for r in range(2):
                        if r:
                            next(slots)
                        g, u = (big[r][0:SC, b, 0:2 * CAP] for b in range(2))
                        dve.wait_ge(S(f"eth{r}"), v)
                        stt(eth[r][:], eth[r][:], 1.0, g, ALU.add, ALU.mult).then_inc(S(f"esilu{r}"), 1)
                        dve.wait_ge(S(f"esilu{r}"), v)
                        if r == 0:
                            dve.wait_ge(S("down_mm"), v)
                        tt(einner[s][:, 2 * r:2 * r + 2, :].rearrange("p c n -> p (c n)"), eth[r][:], u, ALU.mult)\
                            .then_inc(S(f"einner{r}"), 1)
                    dve.wait_ge(S("add_done"), v)
                    V.tensor_copy(add_index[s][:], index[s][:])
                    V.tensor_copy(add_w[s][:], slot_w[s][:]).then_inc(S("kept"), 1)
                    dve.wait_ge(S("kept"), v)
                    indices_of(s, v + 2)
                    run(slots)
                    dve.wait_ge(S("down_mm"), v + 2)
                    for h in range(2):
                        last = ts(y[s][:, h, :], aux[s][0:HS, h * D:(h + 1) * D], add_w[s][:, h:h + 1], 0.5,
                                  op0=ALU.mult, op1=ALU.mult)
                    last.then_inc(S("y_done"), 1)

        @block.gpsimd
        def _(pool):
            G = nc.gpsimd
            G.memset(q_blk[0][:], 0.0)
            G.memset(k_blk[0], 0.0).then_inc(pool_presets, 1)
            G.memset(q_blk[1][:], 0.0)
            G.memset(k_blk[1], 0.0)
            G.memset(chosen[:, TILES, :], 0.0)
            G.memset(slot[:], 0.0)
            G.memset(wsplit[:], 0.0).then_inc(pool_presets, 1)
            by_head = "p (h k) -> p h k"
            with pool.Fori(0, TILES) as i:
                pool.wait_ge(S("top_max"), i + 1)
                G.tensor_tensor(att[1].rearrange(by_head, k=NKEY), sc_sb.rearrange(by_head, k=NKEY),
                                top_a[:].rearrange("p (h e) -> p h e", e=8)[:, :, 0:1].to_broadcast([128, NH + 1, NKEY]),
                                ALU.subtract).then_inc(S("at1_sub"), 1)

            def gather(s, v):
                hold(pool, S("index_ready"), v)
                for h in range(2):
                    G.indirect_dma_start(xg[s][:, h, :], None, x_rows[:, :],
                                         bass.IndirectOffsetOnAxis(index[s][:, h:h + 1], 0)).then_inc(S(f"gathered{s}"), 16)

            pool.wait_ge(S("rows_ready"), 1)
            pool.wait_ge(S("list_ready"), 1)
            n2 = pool.value_load(lists[0:1, 2 * LIST:2 * LIST + 1], min_val=1, max_val=E // 2)
            gather(0, 1)
            gather(1, 2)
            pool.sem_inc(S("add_done"), 2)
            pool.wait_ge(S("acc_stored"), 32 * TILES + 32)
            pool.wait_ge(S("cls_acc_stored"), 16)
            with pool.Fori(0, n2) as i:
                for s in range(2):
                    v = 2 * i + s + 1
                    gather(s, v + 2)
                    hold(pool, S("y_done"), v + 2)
                    for h in range(2):
                        G.indirect_dma_start(out[:, :], bass.IndirectOffsetOnAxis(add_index[s][:, h:h + 1], 0),
                                             y[s][:, h, :], None, compute_op=ALU.add).then_inc(S("added"), 16)
                    pool.wait_ge(S("added"), 64 * i + 32 * s + 32)
                    pool.sem_inc(S("add_done"), 1)
            for s in range(2):
                pool.wait_ge(S(f"gathered{s}"), 32 * n2 + 32)


def _host_constants():
    import numpy as np
    f = np.float32
    p = np.arange(128)
    pos = np.arange(NP, dtype=f)[:, None]
    ang = pos / np.power(f(10000.0), f(2.0) * np.arange(D // 2, dtype=f)[None, :] / f(D)).astype(f)
    pe = np.zeros((NP, D), f)
    pe[:, 0::2], pe[:, 1::2] = np.sin(ang), np.cos(ang)
    mask_q = np.zeros((128, HB, 64), f)
    for m in range(HB):
        for j in range(4):
            mask_q[32 * j:32 * j + DH, m, 4 * m + j] = 1
    mask_o = np.zeros((128, NH, DH), f)
    for g in range(2):
        for h in range(NH):
            mask_o[64 * g + h, h] = 1
    tile = np.arange(TILES)
    img = 2 * tile[None, :] + (p // 64)[:, None]
    tok = np.zeros((128, NT), np.int64)
    tok[:, :TILES] = img * NKEY + 1 + (p % 64)[:, None]
    tok[:B, TILES] = np.arange(B) * NKEY
    tok = np.stack([tok // 64, tok % 64, np.ones_like(tok)], -1).astype(f).reshape(128, NT * 3)
    return {
        "ident": np.eye(128, dtype=f), "pe": np.concatenate([pe, pe]), "mask_q": mask_q,
        "mask_o": mask_o.reshape(128, D), "img_sel": (p[:, None] // 64 == np.arange(2)).astype(f),
        "before": (p[:, None] < p[None, :]).astype(f),
        "cls_before": (np.arange(B)[:, None, None] <= img.T[None]).astype(f).reshape(B, TILES * 128),
        "pat_before": (img[:, :, None] < np.arange(B)).astype(f).reshape(128, TILES * B),
        "iota": np.tile(np.arange(CAP + 1, dtype=f), (128, 1)), "tok": tok,
        "dummy": -(DUMMY + np.arange(HS)[:, None] + HS * np.arange(2)[None, :]).astype(f),
        "evals": np.stack([p - E, p], -1).astype(f),
    }


def kernel(**inputs):
    import numpy as np
    import concourse.bacc as bacc
    from concourse.bass_utils import run_bass_kernel_spmd

    x = {k: np.ascontiguousarray(v) for k, v in inputs.items()}
    heads = np.arange(HB * 4).reshape(HB, 4, 1) * DH + np.arange(32)
    cols = np.concatenate([heads.reshape(-1), D + heads.reshape(-1)])
    by_parity = 2 * D + np.arange(D).reshape(NH // 2, 2, DH).transpose(1, 0, 2).reshape(D)
    n = IMG // PATCH
    patches = x["x"].reshape(TILES, 2, C, n, PATCH, n, PATCH).transpose(0, 2, 4, 6, 1, 3, 5)
    t, at, m = "L0_tok_", "L0_attn_", "L0_ffn_"
    arrays = {
        "xp": patches.reshape(TILES, KC, 128, 128).transpose(0, 2, 1, 3), "cls": x["cls_tok"].reshape(D),
        "patch_w": x[t + "patch_w"].reshape(D, KC, 128).transpose(2, 1, 0), "patch_b": x[t + "patch_b"],
        "ln_g": x[t + "ln_g"], "ln_b": x[t + "ln_b"],
        "ff1_w": x[t + "ff1_w"], "ff1_b": x[t + "ff1_b"], "ff2_w": x[t + "ff2_w"], "ff2_b": x[t + "ff2_b"],
        "wqk1": x[t + "qkv_w"][:, cols], "bqk1": x[t + "qkv_b"][cols],
        "wv1": x[t + "qkv_w"][:, by_parity], "bv1": x[t + "qkv_b"][by_parity],
        "proj1_w": x[t + "proj_w"], "proj1_b": x[t + "proj_b"],
        "wqk2": x[at + "W_qkv"][:, cols], "bqk2": x[at + "b_qkv"][cols],
        "wv2": x[at + "W_qkv"][:, 2 * D:], "bv2": x[at + "b_qkv"][2 * D:],
        "proj2_w": x[at + "W_proj"], "proj2_b": x[at + "b_proj"],
        "wgT": x[m + "Wg"].T, "e_bias": x[m + "e_bias"],
        "w_gate_up": x[m + "W_gate_up"], "w_down": x[m + "W_down"],
        "wsg": x[m + "Wsg"], "wsu": x[m + "Wsu"], "wsd": x[m + "Wsd"],
        **_host_constants(),
    }
    nc = bacc.Bacc("TRN2", target_bir_lowering=False, num_devices=1)
    f32 = mybir.dt.float32
    arrays = {"in_" + k: np.ascontiguousarray(v) for k, v in arrays.items()}
    aps = {k[3:]: nc.dram_tensor(k, v.shape, f32, kind="ExternalInput").ap() for k, v in arrays.items()}
    out = nc.dram_tensor("out_rows", (ROWS, D), f32, kind="ExternalOutput").ap()
    tower_kernel(nc, aps, out)
    r = run_bass_kernel_spmd(nc, [arrays], core_ids=[0])
    return r.results[0]["out_rows"][0:T].reshape(B, NKEY, D)
```
